# Optimizing a Trainium2 kernel written in Bass

```python
import numpy as np
import jax
import jax.numpy as jnp

def _softmax(x, axis=-1):
    return jax.nn.softmax(x, axis=axis)

def _gelu(x):
    return jax.nn.gelu(x, approximate=True)

def _silu(x):
    return jax.nn.silu(x)

def _sigmoid(x):
    return jax.nn.sigmoid(x)

def _layernorm(x, axis=-1, eps=1e-05):
    m = jnp.mean(x, axis=axis, keepdims=True)
    v = jnp.var(x, axis=axis, keepdims=True)
    return (x - m) / jnp.sqrt(v + eps)

def _scatter_add(tgt, idx, src, axis=0):
    return tgt.at[idx].add(src)

def _segment_sum(src, seg, n):
    return jax.ops.segment_sum(src, seg, n)
kernel_name = 'mk_lm_tower_d1_tok_ids1024_r4_6ead93'

def setup_inputs(seed: int=0):
    np.random.seed(seed)
    _w = jnp.asarray

    def _rec_inputs():
        import jax
        import jax.numpy as jnp
        _rk = jax.random.key(seed)
        x = jax.random.randint(jax.random.fold_in(_rk, 1), (4, 1024), 0, 2000, jnp.int32)
        return x
    x = _rec_inputs()

    def _L0_tok_setup():
        import jax, jax.numpy as jnp
        import numpy as np
        EMB_DIM = 256
        HIDDEN_DIM = 256
        VOCAB = 2000
        N_HEADS = 4
        HEAD_DIM = HIDDEN_DIM // N_HEADS
        BATCH = 8
        SEQ = 512

        def _pos_encoding(seq_len, d_model):
            pos = jnp.arange(seq_len, dtype=jnp.float32)[:, None]
            div = jnp.exp(jnp.arange(0, d_model, 2, dtype=jnp.float32) * (-np.log(10000.0) / d_model))
            ang = pos * div
            pe = jnp.zeros((seq_len, d_model), jnp.float32)
            pe = pe.at[:, 0::2].set(jnp.sin(ang)).at[:, 1::2].set(jnp.cos(ang))
            return pe

        def _layernorm(x, eps=1e-05):
            mu = jnp.mean(x, axis=-1, keepdims=True)
            var = jnp.var(x, axis=-1, keepdims=True)
            return (x - mu) / jnp.sqrt(var + eps)
        key = jax.random.key(seed)
        ks = jax.random.split(key, 10)
        input_ids = jax.random.randint(ks[0], (BATCH, SEQ), 0, VOCAB)
        emb_table = jax.random.normal(ks[1], (VOCAB, EMB_DIM), jnp.float32) * 0.02
        s = 1.0 / np.sqrt(EMB_DIM)
        Wq = jax.random.uniform(ks[2], (N_HEADS, EMB_DIM, HEAD_DIM), jnp.float32, -s, s)
        Wk = jax.random.uniform(ks[3], (N_HEADS, EMB_DIM, HEAD_DIM), jnp.float32, -s, s)
        Wv = jax.random.uniform(ks[4], (N_HEADS, EMB_DIM, HEAD_DIM), jnp.float32, -s, s)
        bq = jax.random.uniform(ks[5], (N_HEADS, HEAD_DIM), jnp.float32, -s, s)
        bk = jax.random.uniform(ks[6], (N_HEADS, HEAD_DIM), jnp.float32, -s, s)
        bv = jax.random.uniform(ks[7], (N_HEADS, HEAD_DIM), jnp.float32, -s, s)
        sh = 1.0 / np.sqrt(HIDDEN_DIM)
        Wf = jax.random.uniform(ks[8], (HIDDEN_DIM, HIDDEN_DIM), jnp.float32, -sh, sh)
        bf = jax.random.uniform(ks[9], (HIDDEN_DIM,), jnp.float32, -sh, sh)
        return {'input_ids': input_ids, 'is_first': 1, 'emb_table': emb_table, 'Wq': Wq, 'bq': bq, 'Wk': Wk, 'bk': bk, 'Wv': Wv, 'bv': bv, 'Wf': Wf, 'bf': bf}
    _L0_tok_all = _L0_tok_setup()
    _L0_tok_in = {k: v for k, v in _L0_tok_all.items() if k in ('emb_table', 'Wq', 'bq', 'Wk', 'bk', 'Wv', 'bv', 'Wf', 'bf')}
    del _L0_tok_all

    def _L0_attn_setup():
        import jax, jax.numpy as jnp
        import numpy as np
        HEADS = 16
        DIM_HEAD = 64
        T_MAX = DIM_HEAD

        def _cope(q, sim, pos_emb):
            G = jax.nn.sigmoid(sim)
            P = jnp.flip(jnp.cumsum(jnp.flip(G, axis=-1), axis=-1), axis=-1)
            P = jnp.minimum(P, T_MAX - 1)
            P_floor = jnp.floor(P)
            P_ceil_i = jnp.ceil(P).astype(jnp.int32)
            P_floor_i = P_floor.astype(jnp.int32)
            E = jnp.einsum('bnc,ct->bnt', q, pos_emb)
            E_ceil = jnp.take_along_axis(E, P_ceil_i, axis=-1)
            E_floor = jnp.take_along_axis(E, P_floor_i, axis=-1)
            w = P - P_floor
            return w * E_ceil + (1.0 - w) * E_floor
        key = jax.random.key(seed)
        ks = jax.random.split(key, 6)
        B, N, D = (1, 512, 256)
        inner = HEADS * DIM_HEAD
        return {'x': jax.random.normal(ks[0], (B, N, D), dtype=jnp.float32), 'Wq': jax.random.normal(ks[1], (D, inner), dtype=jnp.float32) * 0.02, 'Wkv': jax.random.normal(ks[2], (D, 2 * inner), dtype=jnp.float32) * 0.02, 'Wout': jax.random.normal(ks[3], (inner, D), dtype=jnp.float32) * 0.02, 'b_out': jnp.zeros((D,), dtype=jnp.float32), 'pos_emb': jax.random.normal(ks[4], (DIM_HEAD, T_MAX), dtype=jnp.float32) * 0.02}
    _L0_attn_all = _L0_attn_setup()
    _L0_attn_in = {k: v for k, v in _L0_attn_all.items() if k in ('Wq', 'Wkv', 'Wout', 'b_out', 'pos_emb')}
    del _L0_attn_all

    def _L0_ffn_setup():
        import jax, jax.numpy as jnp
        import numpy as np
        B, T, D, FF, E, TOP_K = (4, 512, 256, 1024, 8, 2)
        key = jax.random.key(seed)
        k0, k1, k2, k3 = jax.random.split(key, 4)
        x = jax.random.normal(k0, (B, T, D), dtype=jnp.float32)
        router_w = jax.random.normal(k1, (E, D), dtype=jnp.float32) * D ** (-0.5)
        w1 = jax.random.normal(k2, (E, D, FF), dtype=jnp.float32) * D ** (-0.5)
        w2 = jax.random.normal(k3, (E, FF, D), dtype=jnp.float32) * FF ** (-0.5)
        return {'x': x, 'router_w': router_w, 'w1': w1, 'w2': w2}
    _L0_ffn_all = _L0_ffn_setup()
    _L0_ffn_in = {k: v for k, v in _L0_ffn_all.items() if k in ('router_w', 'w1', 'w2')}
    del _L0_ffn_all
    return {'x': x, 'L0_tok_emb_table': _L0_tok_in['emb_table'], 'L0_tok_Wq': _L0_tok_in['Wq'], 'L0_tok_bq': _L0_tok_in['bq'], 'L0_tok_Wk': _L0_tok_in['Wk'], 'L0_tok_bk': _L0_tok_in['bk'], 'L0_tok_Wv': _L0_tok_in['Wv'], 'L0_tok_bv': _L0_tok_in['bv'], 'L0_tok_Wf': _L0_tok_in['Wf'], 'L0_tok_bf': _L0_tok_in['bf'], 'L0_attn_Wq': _L0_attn_in['Wq'], 'L0_attn_Wkv': _L0_attn_in['Wkv'], 'L0_attn_Wout': _L0_attn_in['Wout'], 'L0_attn_b_out': _L0_attn_in['b_out'], 'L0_attn_pos_emb': _L0_attn_in['pos_emb'], 'L0_ffn_router_w': _L0_ffn_in['router_w'], 'L0_ffn_w1': _L0_ffn_in['w1'], 'L0_ffn_w2': _L0_ffn_in['w2']}

def reference(x, L0_tok_emb_table, L0_tok_Wq, L0_tok_bq, L0_tok_Wk, L0_tok_bk, L0_tok_Wv, L0_tok_bv, L0_tok_Wf, L0_tok_bf, L0_attn_Wq, L0_attn_Wkv, L0_attn_Wout, L0_attn_b_out, L0_attn_pos_emb, L0_ffn_router_w, L0_ffn_w1, L0_ffn_w2):
    import jax
    import jax.numpy as jnp

    def _L0_tok_ref(input_ids, is_first, emb_table, Wq, bq, Wk, bk, Wv, bv, Wf, bf):
        import jax, jax.numpy as jnp
        import numpy as np
        EMB_DIM = 256
        HIDDEN_DIM = 256
        VOCAB = 2000
        N_HEADS = 4
        HEAD_DIM = HIDDEN_DIM // N_HEADS
        BATCH = 8
        SEQ = 512

        def _pos_encoding(seq_len, d_model):
            pos = jnp.arange(seq_len, dtype=jnp.float32)[:, None]
            div = jnp.exp(jnp.arange(0, d_model, 2, dtype=jnp.float32) * (-np.log(10000.0) / d_model))
            ang = pos * div
            pe = jnp.zeros((seq_len, d_model), jnp.float32)
            pe = pe.at[:, 0::2].set(jnp.sin(ang)).at[:, 1::2].set(jnp.cos(ang))
            return pe

        def _layernorm(x, eps=1e-05):
            mu = jnp.mean(x, axis=-1, keepdims=True)
            var = jnp.var(x, axis=-1, keepdims=True)
            return (x - mu) / jnp.sqrt(var + eps)
        B, S = input_ids.shape
        if is_first == 1:
            x = emb_table[input_ids] + _pos_encoding(S, EMB_DIM)[None]
        else:
            x = input_ids
        q = jnp.einsum('bse,hed->bhsd', x, Wq) + bq[:, None, :]
        k = jnp.einsum('bse,hed->bhsd', x, Wk) + bk[:, None, :]
        v = jnp.einsum('bse,hed->bhsd', x, Wv) + bv[:, None, :]
        scores = jnp.einsum('bhsd,bhtd->bhst', q, k) / 4.0
        attn = jax.nn.softmax(scores, axis=2)
        z = jnp.einsum('bhst,bhtd->bhsd', attn, v)
        z = z.transpose(0, 2, 1, 3).reshape(B, S, HIDDEN_DIM)
        z = _layernorm(z + x)
        zz = jax.nn.relu(z) @ Wf + bf
        return _layernorm(z + zz)

    def _L0_attn_ref(x, Wq, Wkv, Wout, b_out, pos_emb):
        import jax, jax.numpy as jnp
        import numpy as np
        HEADS = 16
        DIM_HEAD = 64
        T_MAX = DIM_HEAD

        def _cope(q, sim, pos_emb):
            G = jax.nn.sigmoid(sim)
            P = jnp.flip(jnp.cumsum(jnp.flip(G, axis=-1), axis=-1), axis=-1)
            P = jnp.minimum(P, T_MAX - 1)
            P_floor = jnp.floor(P)
            P_ceil_i = jnp.ceil(P).astype(jnp.int32)
            P_floor_i = P_floor.astype(jnp.int32)
            E = jnp.einsum('bnc,ct->bnt', q, pos_emb)
            E_ceil = jnp.take_along_axis(E, P_ceil_i, axis=-1)
            E_floor = jnp.take_along_axis(E, P_floor_i, axis=-1)
            w = P - P_floor
            return w * E_ceil + (1.0 - w) * E_floor
        B, N, D = x.shape
        h, d = (HEADS, DIM_HEAD)
        scale = d ** (-0.5)
        q = x @ Wq
        kv = x @ Wkv
        k, v = jnp.split(kv, 2, axis=-1)

        def to_heads(t):
            return t.reshape(B, N, h, d).transpose(0, 2, 1, 3).reshape(B * h, N, d)
        q, k, v = (to_heads(q), to_heads(k), to_heads(v))
        sim = jnp.einsum('bid,bjd->bij', q, k) * scale
        sim = sim + _cope(q, sim, pos_emb)
        attn = jax.nn.softmax(sim, axis=-1)
        out = jnp.einsum('bij,bjd->bid', attn, v)
        out = out.reshape(B, h, N, d).transpose(0, 2, 1, 3).reshape(B, N, h * d)
        return out @ Wout + b_out

    def _L0_ffn_ref(x, router_w, w1, w2):
        import jax, jax.numpy as jnp
        import numpy as np
        B, T, D, FF, E, TOP_K = (4, 512, 256, 1024, 8, 2)
        b, t, d = x.shape
        e, k = (router_w.shape[0], TOP_K)
        xf = x.reshape(-1, d)
        n = xf.shape[0]
        logits = xf @ router_w.T
        topv, topi = jax.lax.top_k(logits, k)
        topw = jax.nn.softmax(topv.astype(jnp.float32), axis=-1).astype(x.dtype)
        idx_flat = topi.reshape(-1)
        w_flat = topw.reshape(-1)
        sort_idx = jnp.argsort(idx_flat)
        src = jnp.repeat(jnp.arange(n), k)
        rev = src[sort_idx]
        sw = w_flat[sort_idx]
        perm = xf[rev]
        chunks = perm.reshape(e, n * k // e, d)
        h = jax.nn.gelu(jnp.einsum('ecd,edf->ecf', chunks, w1), approximate=False)
        y = jnp.einsum('ecf,efd->ecd', h, w2).reshape(n * k, d)
        y = y * sw[:, None]
        out = jnp.zeros((n, d), dtype=x.dtype).at[rev].add(y)
        return out.reshape(b, t, d)
    h = _L0_tok_ref(x, 1, L0_tok_emb_table, L0_tok_Wq, L0_tok_bq, L0_tok_Wk, L0_tok_bk, L0_tok_Wv, L0_tok_bv, L0_tok_Wf, L0_tok_bf)
    h = h + _L0_attn_ref(_layernorm(h, axis=-1), L0_attn_Wq, L0_attn_Wkv, L0_attn_Wout, L0_attn_b_out, L0_attn_pos_emb)
    h = h + _L0_ffn_ref(_layernorm(h, axis=-1), L0_ffn_router_w, L0_ffn_w1, L0_ffn_w2)
    return h

_drawn_inputs = setup_inputs


def setup_inputs(seed=0):
    import zlib

    import numpy as np

    out = dict(_drawn_inputs(seed))
    spreads = {'L0_attn_b_out': (0.0, 0.1)}
    factors = {'L0_tok_bq': 8.0, 'L0_attn_pos_emb': 6.402}
    for name, (base, spread) in spreads.items():
        noise = np.random.default_rng([zlib.crc32(name.encode()), seed]).standard_normal(out[name].shape)
        drawn = base * np.exp(spread * noise) if base else spread * noise
        out[name] = jnp.asarray(drawn.astype(out[name].dtype))
    for name, factor in factors.items():
        out[name] = (out[name] * factor).astype(out[name].dtype)
    return out
```

```python
from contextlib import ExitStack

import concourse.bass as bass
from concourse import mybir

F32 = mybir.dt.float32
I32 = mybir.dt.int32
U32 = mybir.dt.uint32
ALU = mybir.AluOpType
ACT = mybir.ActivationFunctionType
AX = mybir.AxisListType.X
ds = bass.ds

P = 128
B, S, D = 4, 1024, 256
R = B * S
T = S // P
NT = R // P
KC = D // P
HB = 512
H1, DH = 4, 64
H2 = 16
NPAIR = B * H2 // 2
EPS = 1e-5
TMAX = DH
E, FF, TOPK = 8, 1024, 2
NR = R * TOPK
FC = FF // P


class Count:

    def __init__(self, eng, sem, base=0):
        self.eng, self.sem, self.base, self.n = eng, sem, base, 0

    def inc(self, instruction):
        self.n += 1
        instruction.then_inc(self.sem, 1)

    def link(self, instruction):
        self.inc(instruction)
        self.eng.wait_ge(self.sem, self.base + self.n)


def bcast(ap, shape):
    return ap.to_broadcast(shape)


def layernorm_rows(nc, link, inc_last, x, out, n, stats, mv, rstd, act_sqrt, settled):
    for i in range(n):
        last = nc.vector.bn_stats(stats[:, i, :], x[:, i, :])
    link(last)
    settled()
    for i in range(n):
        last = nc.vector.bn_aggr(mv[:, i, :], stats[:, i, :])
    act_sqrt(last)
    link(nc.vector.reciprocal(rstd[:, 0:n], rstd[:, 0:n]))
    for i in range(n):
        last = nc.vector.tensor_scalar(out[:, i, :], x[:, i, :], mv[:, i, 0:1], rstd[:, i:i + 1],
                                       ALU.subtract, ALU.mult)
    inc_last(last)


def token_stage(nc, keep, ids, emb, pos, wq, bq, wk, bk, wv, bv, wf, bf, b_out):
    with ExitStack() as ctx:
        def sb(name, shape, dt=F32):
            return ctx.enter_context(nc.sbuf_tensor(name, shape, dt))

        def sem(name):
            return ctx.enter_context(nc.semaphore(name))

        rows, hT = keep.rows, keep.hT
        ids_sb = sb("ids_sb", [P, NT], I32)
        pos_sb = sb("pos_sb", [P, T, D])
        wq_sb, wk_sb, wv_sb, wf_sb = (sb(n, [P, KC, D]) for n in ("wq1", "wk1", "wv1", "wf1"))
        bq_sb, bk_sb = sb("bq1", [P, 2]), sb("bk1", [P, 2])
        bv_sb, bf_sb = sb("bv1", [P, D]), sb("bf1", [P, D])
        x = sb("x1", [P, T, D])
        xT = sb("xT1", [P, KC, S])
        qT, kT = sb("qT1", [P, 2, S]), sb("kT1", [P, 2, S])
        v = sb("v1", [P, T, D])
        vs = sb("vs1", [P, 2, T, DH])
        probs = sb("probs1", [P, 2, T, S])
        z = sb("z1", [P, T, D])
        mx, nmx = sb("mx1", [P, T]), sb("nmx1", [P, 2, T])
        ssum, rsum = sb("ssum1", [P, 2, T]), sb("rsum1", [P, T])
        stats, mv, rstd = sb("stats1", [P, T, 6]), sb("mv1", [P, T, 2]), sb("rstd1", [P, T])

        work = [ctx.enter_context(nc.psum_tensor(f"work1_{i}", [P, HB], F32)) for i in range(3)]
        score = [ctx.enter_context(nc.psum_tensor(f"score1_{i}", [P, S], F32)) for i in range(2)]
        zp = ctx.enter_context(nc.psum_tensor("zp1", [P, HB], F32))

        s_w, s_ids, s_gather = sem("weights_in"), sem("ids_in"), sem("rows_gathered")
        s_x, s_tr, s_xT = sem("x_ready"), sem("work_full_for_act"), sem("work_copied_by_act")
        s_vp, s_v = sem("work_full_for_dve"), sem("work_read_by_dve")
        s_score, s_mx, s_max, s_exp = sem("score_ready"), sem("max_found"), sem("minus_max_ready"), sem("exp_ready")
        s_vs, s_z, s_zread = sem("scaled_v_ready"), sem("z_ready"), sem("z_read")
        s_zz, s_var, s_root, s_c = sem("zn_ready"), sem("var_ready"), sem("root_ready"), sem("dve_chain1")
        s_h = sem("h_ready")

        jobs = ([("xT", c, h, "act") for c in range(KC) for h in range(2)]
                + [(n, g, h, "act") for n in ("q", "k") for g in range(2) for h in range(2)]
                + [("v", t, 0, "dve") for t in range(T // 2)]
                + [("zT", c, h, "act") for c in range(KC) for h in range(2)]
                + [("ff", t, 0, "dve") for t in range(T // 2)]
                + [("hT", c, h, "act") for c in range(KC) for h in range(2)])
        n_act = sum(j[3] == "act" for j in jobs)
        n_dve = len(jobs) - n_act
        nb = len(work)

        def done_before(j, who):
            return sum(k[3] == who for k in jobs[:j])

        def first(name):
            return next(j for j, k in enumerate(jobs) if k[0] == name)

        block = ctx.enter_context(nc.Block())

        @block.sync
        def _(sp):
            sp.dma_start(ids_sb[:, :], ids).then_inc(s_ids, 16)
            sp.dma_start(pos_sb[:, :, :], pos.rearrange("(t p) d -> p t d", p=P)).then_inc(s_w, 16)
            for dst, src in ((wq_sb, wq), (wk_sb, wk), (wv_sb, wv)):
                for h in range(H1):
                    sp.dma_start(dst[:, :, h * DH:(h + 1) * DH],
                                 src[h].rearrange("(c p) d -> p c d", p=P)).then_inc(s_w, 16)
            sp.dma_start(wf_sb[:, :, :], wf.rearrange("(c p) n -> p c n", p=P)).then_inc(s_w, 16)
            for dst, src in ((bq_sb, bq), (bk_sb, bk)):
                for g in range(2):
                    sp.dma_start(dst[:, g:g + 1], src[2 * g:2 * g + 2, :].rearrange("h (d o) -> (h d) o", o=1)).then_inc(s_w, 16)
            sp.dma_start(bv_sb[:, :], bv.rearrange("h d -> (h d)").partition_broadcast(P)).then_inc(s_w, 16)
            sp.dma_start(bf_sb[:, :], bf.partition_broadcast(P)).then_inc(s_w, 16)
            sp.dma_start(keep.bout[:, :], b_out.partition_broadcast(P)).then_inc(s_w, 16)
        n_w = 16 * (1 + 3 * H1 + 1 + 4 + 3)

        @block.gpsimd
        def _(pool):
            pool.wait_ge(s_ids, 16)
            for t in range(NT):
                pool.indirect_dma_start(rows[:, t, :], None, emb,
                                        bass.IndirectOffsetOnAxis(ap=ids_sb[:, t:t + 1], axis=0)).then_inc(s_gather, 16)
            pool.wait_ge(s_gather, 16 * NT)

        @block.vector
        def _(dve):
            dve.wait_ge(s_w, n_w)
            dve.wait_ge(s_gather, 16 * NT)
            with dve.Fori(0, B) as b:
                dve_links = Count(dve, s_c, b * N_LINKS1)
                nc.vector.tensor_tensor(x[:, :, :], rows[:, ds(b * T, T), :], pos_sb[:, :, :], ALU.add).then_inc(s_x, 1)
                for t in range(T // 2):
                    dve.wait_ge(s_vp, b * n_dve + t + 1)
                    nc.vector.tensor_tensor(
                        v[:, 2 * t:2 * t + 2, :],
                        work[(first("v") + t) % nb][:, :].rearrange("p (a d) -> p a d", a=2),
                        bv_sb[:, :].rearrange("p (o d) -> p o d", o=1).to_broadcast([P, 2, D]),
                        ALU.add).then_inc(s_v, 1)
                dve.wait_ge(s_v, b * n_dve + T // 2)

                def head_max(h):
                    for t in range(T):
                        k = h * T + t
                        dve.wait_ge(s_score, b * H1 * T + k + 1)
                        nc.vector.reduce_max(mx[:, t:t + 1], score[k % 2][:, :], AX).then_inc(s_mx, 1)
                        dve.wait_ge(s_mx, b * H1 * T + k + 1)
                        nc.vector.tensor_scalar(nmx[:, h % 2, t:t + 1], mx[:, t:t + 1], -0.25, None, ALU.mult).then_inc(s_max, 1)

                def head_values(h):
                    dve.wait_ge(s_exp, b * H1 * T + (h + 1) * T)
                    dve_links.link(nc.vector.reciprocal(rsum[:, :], ssum[:, h % 2, :]))
                    nc.vector.tensor_tensor(
                        vs[:, h % 2, :, :], v[:, :, h * DH:(h + 1) * DH],
                        rsum[:, :].rearrange("p (t o) -> p t o", o=1).to_broadcast([P, T, DH]), ALU.mult).then_inc(s_vs, 1)

                def head_z(h):
                    dve.wait_ge(s_z, b * H1 + h + 1)
                    nc.vector.tensor_tensor(z[:, :, h * DH:(h + 1) * DH], zp[:, :].rearrange("p (t d) -> p t d", t=T),
                                            x[:, :, h * DH:(h + 1) * DH], ALU.add).then_inc(s_zread, 1)

                for h in range(H1):
                    head_max(h)
                    if h >= 1:
                        head_z(h - 1)
                    head_values(h)
                head_z(H1 - 1)
                dve.wait_ge(s_zread, (b + 1) * H1)

                def norm(i, src, dst, done):
                    def root(last):
                        last.then_inc(s_var, 1)
                        dve.wait_ge(s_root, b * 3 + i + 1)
                    layernorm_rows(nc, dve_links.link, done, src, dst, T, stats, mv, rstd, root, lambda: nc.vector.tensor_copy(rstd[:, 0:1], stats[:, T - 1, 0:1]))

                norm(0, z, z, lambda last: last.then_inc(s_zz, 1))
                dve.wait_ge(s_zz, b * 3 + 1)
                dve_links.link(nc.vector.tensor_tensor(
                    v[:, :, :], z[:, :, :], bf_sb[:, :].rearrange("p (o d) -> p o d", o=1).to_broadcast([P, T, D]), ALU.add))
                for t in range(T // 2):
                    dve.wait_ge(s_vp, b * n_dve + T // 2 + t + 1)
                    nc.vector.tensor_tensor(v[:, 2 * t:2 * t + 2, :], v[:, 2 * t:2 * t + 2, :],
                                            work[(first("ff") + t) % nb][:, :].rearrange("p (a d) -> p a d", a=2),
                                            ALU.add).then_inc(s_v, 1)
                dve.wait_ge(s_v, b * n_dve + T)
                norm(1, v, z, lambda last: last.then_inc(s_zz, 1))
                dve.wait_ge(s_zz, b * 3 + 2)
                nc.vector.tensor_tensor(rows[:, ds(b * T, T), :], z[:, :, :],
                                        keep.bout[:, :].rearrange("p (o d) -> p o d", o=1).to_broadcast([P, T, D]), ALU.add)
                norm(2, z, z, lambda last: last.then_inc(s_zz, 1))
                dve.wait_ge(s_xT, (b + 1) * n_act)
                assert dve_links.n == N_LINKS1, dve_links.n

        @block.scalar
        def _(act):
            act.wait_ge(s_w, n_w)
            with act.Fori(0, B) as b:
                def empty(j, dst, func=ACT.Copy, **kw):
                    act.wait_ge(s_tr, b * n_act + done_before(j, "act") + 1)
                    nc.scalar.activation(dst, work[j % nb][:, :], func, **kw).then_inc(s_xT, 1)

                for j, (name, g, h, who) in enumerate(jobs[:first("zT")]):
                    half = slice(h * HB, (h + 1) * HB)
                    if name == "xT":
                        empty(j, xT[:, g, half])
                    elif name == "q":
                        empty(j, qT[:, g, half], ACT.Identity, bias=bq_sb[:, g:g + 1])
                    elif name == "k":
                        empty(j, kT[:, g, half], ACT.Identity, bias=bk_sb[:, g:g + 1])
                for h in range(H1):
                    if h >= 2:
                        act.wait_ge(s_z, b * H1 + h - 1)
                    for t in range(T):
                        k = h * T + t
                        act.wait_ge(s_max, b * H1 * T + k + 1)
                        nc.scalar.activation(probs[:, h % 2, t, :], score[k % 2][:, :], ACT.Exp,
                                             bias=nmx[:, h % 2, t:t + 1], scale=0.25,
                                             accum_out=ssum[:, h % 2, t:t + 1]).then_inc(s_exp, 1)

                def root(i):
                    act.wait_ge(s_var, b * 3 + i + 1)
                    nc.scalar.activation(rstd[:, :], mv[:, :, 1], ACT.Sqrt, bias=keep.eps[:, :]).then_inc(s_root, 1)

                root(0)
                for j, (name, g, h, who) in enumerate(jobs):
                    half = slice(h * HB, (h + 1) * HB)
                    if name == "zT":
                        empty(j, xT[:, g, half], ACT.Relu)
                root(1)
                root(2)
                for j, (name, g, h, who) in enumerate(jobs):
                    if name == "hT":
                        empty(j, hT[:, g, ds(b * S + h * HB, HB)])

        @block.tensor
        def _(pe):
            pe.wait_ge(s_w, n_w)
            with pe.Fori(0, B) as b:
                def bank(j):
                    k = j - nb
                    if k >= 0:
                        who = jobs[k][3]
                        pe.wait_ge(s_xT if who == "act" else s_v,
                                   b * (n_act if who == "act" else n_dve) + done_before(k, who) + 1)
                    return work[j % nb]

                def full(j, last):
                    last.then_inc(s_tr if jobs[j][3] == "act" else s_vp, 1)

                def transposes(j, src, c, h):
                    w = bank(j)
                    for i in range(4):
                        last = nc.tensor.transpose(w[:, i * P:(i + 1) * P],
                                                   src[:, 4 * h + i, c * P:(c + 1) * P], keep.ident[:, :])
                    full(j, last)

                pe.wait_ge(s_x, b + 1)
                pe.wait_ge(s_xT, b * n_act)
                for j, (name, g, h, who) in enumerate(jobs[:first("zT")]):
                    if name == "xT":
                        transposes(j, x, g, h)
                    elif name in "qk":
                        pe.wait_ge(s_xT, b * n_act + 2 * KC)
                        w = bank(j)
                        for c in range(KC):
                            last = nc.tensor.matmul(w[:, :], (wq_sb if name == "q" else wk_sb)[:, c, g * P:(g + 1) * P],
                                                    xT[:, c, h * HB:(h + 1) * HB], start=(c == 0), stop=(c == KC - 1))
                        full(j, last)
                    else:
                        w = bank(j)
                        for a in range(2):
                            for c in range(KC):
                                t = 2 * g + a
                                last = nc.tensor.matmul(w[:, a * D:(a + 1) * D], xT[:, c, t * P:(t + 1) * P],
                                                        wv_sb[:, c, :], start=(c == 0), stop=(c == KC - 1))
                        full(j, last)
                pe.wait_ge(s_xT, b * n_act + 2 * KC + 8)

                def scores(h):
                    g, o = h // 2, DH * (h % 2)
                    for t in range(T):
                        k = h * T + t
                        if k >= 2:
                            pe.wait_ge(s_exp, b * H1 * T + k - 1)
                        for n in range(2):
                            last = nc.tensor.matmul(score[k % 2][:, n * HB:(n + 1) * HB], kT[o:o + DH, g, t * P:(t + 1) * P],
                                                    qT[o:o + DH, g, n * HB:(n + 1) * HB], start=True, stop=True)
                        last.then_inc(s_score, 1)

                def products(h):
                    pe.wait_ge(s_vs, b * H1 + h + 1)
                    pe.wait_ge(s_zread, b * H1 + h)
                    for s in range(T):
                        for t in range(T):
                            last = nc.tensor.matmul(zp[:, s * DH:(s + 1) * DH], probs[:, h % 2, t, s * P:(s + 1) * P],
                                                    vs[:, h % 2, t, :], start=(t == 0), stop=(t == T - 1))
                    last.then_inc(s_z, 1)

                for h in range(H1):
                    scores(h)
                    if h >= 1:
                        products(h - 1)
                products(H1 - 1)
                pe.wait_ge(s_zz, b * 3 + 1)
                for j, (name, g, h, who) in enumerate(jobs):
                    if name == "zT":
                        transposes(j, z, g, h)
                    elif name == "ff":
                        if g == 0:
                            pe.wait_ge(s_xT, b * n_act + 2 * KC + 8 + 2 * KC)
                        w = bank(j)
                        for a in range(2):
                            for c in range(KC):
                                t = 2 * g + a
                                last = nc.tensor.matmul(w[:, a * D:(a + 1) * D], xT[:, c, t * P:(t + 1) * P],
                                                        wf_sb[:, c, :], start=(c == 0), stop=(c == KC - 1))
                        full(j, last)
                pe.wait_ge(s_zz, b * 3 + 3)
                for j, (name, g, h, who) in enumerate(jobs):
                    if name == "hT":
                        transposes(j, z, g, h)


N_LINKS1 = H1 + 3 * 2 + 1


PER, RISE = 5, 2
BLOCKS = (TMAX // RISE)
TAIL = BLOCKS * PER
BODY = S - TAIL


def hinge_blocks():
    out = []
    l = 1
    while True:
        a0 = next((a for a in range(BLOCKS) if 0.61 * PER * (a + 1) + 0.3 > RISE * a + l), BLOCKS)
        a1 = (TMAX - 1 - l) // RISE
        if a0 > a1:
            return out
        out.append((l, a0, a1 + 1))
        l += 1


HINGES = hinge_blocks()
GROUPS = T
RING = 4
NBANK = 6
SLOTS = 4


def cope_tables():
    import numpy as np
    low = np.repeat(RISE * np.arange(BLOCKS), PER).astype(np.float32)
    least = np.zeros(TAIL, np.float32)
    least[-1] = TMAX - 1 - low[-1]
    most = np.full(TAIL, 1e30, np.float32)
    for a in range(BLOCKS):
        covered = max((l for l, a0, a1 in HINGES if a0 <= a < a1), default=0)
        if RISE * a + covered < TMAX - 1:
            most[a * PER:(a + 1) * PER] = covered + 1
    return np.stack([low, least, most])


def cope_stage(nc, keep, a, saved):
    with ExitStack() as ctx:
        def sb(name, shape, dt=F32):
            return ctx.enter_context(nc.sbuf_tensor(name, shape, dt))

        def sem(name):
            return ctx.enter_context(nc.semaphore(name))

        rows, hT, ident = keep.rows, keep.hT, keep.ident
        w_in = sb("w_in", [P, 3, KC, P])
        wout = sb("wout", [P, H2 // 2, D])
        pos = sb("pos2", [P, TMAX])
        one, zero, idle = sb("one", [P, 1]), sb("zero", [P, 1]), sb("idle", [P, 1])
        q = [sb(f"q{s}", [P, S]) for s in range(SLOTS)]
        k = [sb(f"k{s}", [P, S]) for s in range(SLOTS)]
        vT = sb("vT", [P, S])
        v1 = [sb(f"v1_{s}", [P, T, P]) for s in range(SLOTS)]
        ex = [sb(f"ex{i}", [P, S]) for i in range(RING)]
        nsum = sb("nsum", [P, S])
        aT = sb("aT", [P, S])
        gate = sb("gate", [P, T, TAIL])
        psum_p = sb("p_low", [P, T, TAIL])
        f = [sb(f"f{i}", [P, T, TAIL]) for i in range(2)]
        relu = [sb(f"relu{i}", [P, T * TAIL]) for i in range(2)]
        table = sb("table", [P, 3, TAIL])
        carry = sb("carry", [P, T, TAIL], mybir.dt.bfloat16)
        over, breach = sb("over", [P, T, TAIL]), sb("breach", [P, T, TAIL])
        ent = [sb(f"ent{i}", [P, T, TMAX]) for i in range(2)]
        slope, bend = sb("slope", [P, T, TMAX]), sb("bend", [P, T, TMAX])
        bmax, tmax = sb("bmax", [P, T, 2]), sb("tmax", [P, T])
        shift = [sb(f"shift{i}", [P, T]) for i in range(2)]
        bm = sb("bm", [P, T])
        nmax = [sb(f"nmax{i}", [P, T]) for i in range(2)]
        rcol = sb("rcol", [P, T])

        bank = [ctx.enter_context(nc.psum_tensor(f"bank{i}", [P, HB], F32)) for i in range(NBANK)]
        pv = [ctx.enter_context(nc.psum_tensor(f"pv{i}", [P, HB], F32)) for i in range(2)]

        s_const, s_w = sem("consts_in"), sem("pair_weights_in")
        s_set, s_ones = sem("memsets_done"), sem("ones_set")
        s_fa, s_fd = sem("bank_full_for_act"), sem("bank_full_for_dve")
        s_ra, s_rd = sem("bank_read_by_act"), sem("bank_read_by_dve")
        s_zero = sem("shift_row_zeroed")
        s_p, s_seen, s_relu, s_used = sem("p_ready"), sem("p_checked"), sem("relu_ready"), sem("relu_used")
        s_gate = sem("gate_used")
        s_m, s_xt, s_pvm, s_ns = sem("max_known"), sem("tail_exp_ready"), sem("product_done"), sem("products_copied")
        s_saved = sem("rows_saved")
        s_c, s_pc, s_rev = sem("dve_chain2"), sem("pool_chain"), sem("breach_known")

        def tail_jobs(s):
            return [("tail", s, i, "act") for i in range(3)] + [("ent", s, 0, "act")]

        def pair_jobs(s):
            return [[("pq", s, h, "act") for h in range(2)], [("pk", s, h, "act") for h in range(2)],
                    [("pv", s, h, "act") for h in range(2)], [("vtr", s, h, "act") for h in range(2)]]

        def slot_plan(s):
            nxt, nnxt = (s + 1) % SLOTS, (s + 2) % SLOTS
            plan = [[("row", s, h, "act") for h in range(2)] + [("tt", s, i, "act") for i in range(2)]]
            for m in range(GROUPS):
                g = []
                if m:
                    g += [("sT", s, 2 * m + h, "act") for h in range(2)]
                if m == 1:
                    g += [("tt", s, i, "act") for i in (2, 3)]
                if m:
                    g += [("PV", s, m - 1)]
                g += [("body", nxt, 2 * m + h, "dve") for h in range(2)]
                if s % 2 == 0 and 1 <= m <= 4:
                    g += pair_jobs(nnxt)[m - 1]
                if m == GROUPS - 1:
                    g += [("PV", s, m)] + tail_jobs(nnxt)
                plan.append(g)
            end = [("sum", s, 0, "dve"), ("rep", s, 0, "dve"), ("rep", s, 1, "dve")]
            if s % 2:
                end += [("out", s, i, "dve") for i in range(4)]
            plan.append(end)
            return plan

        pro_plan = [[j for js in pair_jobs(0) for j in js] + tail_jobs(0) + tail_jobs(1)]
        pro_plan += [[("body", 0, 2 * m + h, "dve") for h in range(2)] for m in range(GROUPS)]
        body_plan = [slot_plan(s) for s in range(SLOTS)]

        def is_job(x):
            return x[0] != "PV"

        pro = [j for g in pro_plan for j in g]
        turn = [j for p in body_plan for g in p for j in g if is_job(j)]
        pad = -len(turn) % NBANK
        index = {}
        counts = {"act": 0, "dve": 0}
        last_of_bank = {}
        info = {}

        def place(part, jobs, first):
            n = {"act": 0, "dve": 0}
            pos = first
            for i, j in enumerate(jobs):
                n[j[3]] += 1
                info[(part, j)] = (pos % NBANK, n[j[3]], last_of_bank.get(pos % NBANK))
                last_of_bank[pos % NBANK] = (part, j)
                pos += 1
                if part == "turn" and i == len(jobs) // 2:
                    pos += pad
            return n

        n_pro = place("pro", pro, -len(pro))
        n_turn = place("turn", turn, 0)
        assert all(j[3] == "dve" for j in pro[-NBANK:] + turn[-NBANK:])

        class Place:

            def __init__(self, eng, part, it):
                self.eng, self.part, self.it = eng, part, it

            def at(self, who, n, part=None):
                part = part or self.part
                if part == "pro":
                    return n
                return n_pro[who] + self.it * n_turn[who] + n

            def job(self, j):
                return info[(self.part, j)]

            def head(self, sem, s, per, n):
                if self.part == "pro":
                    self.eng.wait_ge(sem, s * per + n)
                else:
                    self.eng.wait_ge(sem, self.it * (SLOTS * per) + (s * per + n))

        def pe_take(w, j):
            b, _, before = w.job(j)
            if before is None and w.part == "pro":
                return bank[b]
            part, prev = before
            who, n = prev[3], info[before][1]
            if part == w.part:
                w.eng.wait_ge(s_ra if who == "act" else s_rd, w.at(who, n))
            else:
                total = (n_pro if part == "pro" else n_turn)[who]
                w.eng.wait_ge(s_ra if who == "act" else s_rd, w.at(who, n - total))
            return bank[b]

        def pe_need(w, part, j):
            who, n = j[3], info[(part, j)][1]
            w.eng.wait_ge(s_ra if who == "act" else s_rd, w.at(who, n, part))

        def pe_job(w, j, b_of, hp_of):
            kind, s, i, who = j
            ps = pe_take(w, j)
            if kind in ("pq", "pk", "pv"):
                x = ("pq", "pk", "pv").index(kind)
                for c in range(KC):
                    last = nc.tensor.matmul(ps[:, :], w_in[:, x, c, :], hT[:, c, ds(b_of * S + i * HB, HB)],
                                            start=(c == 0), stop=(c == KC - 1))
            elif kind == "vtr":
                pe_need(w, w.part, ("pv", s, 1, "act"))
                for n in range(4):
                    last = nc.tensor.transpose(ps[:, n * P:(n + 1) * P], vT[:, (4 * i + n) * P:(4 * i + n + 1) * P], ident[:, :])
            elif kind == "tail":
                for n, t in enumerate(range(3 * i, min(3 * i + 3, T))):
                    last = nc.tensor.matmul(ps[:, n * TAIL:(n + 1) * TAIL], q[s][:, t * P:(t + 1) * P], k[s][:, 0:TAIL],
                                            start=True, stop=True)
            elif kind == "ent":
                for t in range(T):
                    last = nc.tensor.matmul(ps[:, t * TMAX:(t + 1) * TMAX], q[s][:, t * P:(t + 1) * P], pos[:, :],
                                            start=True, stop=True)
            elif kind == "body":
                t, h = divmod(i, 2)
                last = nc.tensor.matmul(ps[:, 0:BODY // 2], q[s][:, t * P:(t + 1) * P],
                                        k[s][:, TAIL + h * (BODY // 2):TAIL + (h + 1) * (BODY // 2)], start=True, stop=True)
            elif kind == "row":
                for n in range(4):
                    last = nc.tensor.matmul(ps[DH:DH + 1, n * P:(n + 1) * P], shift[s % 2][:, 4 * i + n:4 * i + n + 1],
                                            ident[:, :], start=True, stop=True)
            elif kind == "tt":
                part, half = divmod(i, 2)
                c0, c1 = (0, P) if part == 0 else (P, TAIL)
                for n in range(4):
                    last = nc.tensor.transpose(ps[0:c1 - c0, n * P:(n + 1) * P], f[s % 2][:, 4 * half + n, c0:c1], ident[:, :])
            elif kind == "sT":
                m, h = divmod(i, 2)
                last = nc.tensor.matmul(ps[:, :], k[s][:, m * P:(m + 1) * P], q[s][:, h * HB:(h + 1) * HB], start=True, stop=True)
            elif kind == "sum":
                o = DH * (1 - s % 2)
                for t in range(T):
                    last = nc.tensor.matmul(ps[:, t:t + 1], nsum[o:o + 1, t * P:(t + 1) * P], one[o:o + 1, :], start=True, stop=True)
            elif kind == "rep":
                for n in range(4):
                    t = 4 * i + n
                    last = nc.tensor.matmul(ps[:, n * P:(n + 1) * P], rcol[:, t:t + 1].to_broadcast([P, P]), ident[:, :],
                                            start=True, stop=True)
            elif kind == "out":
                for n in range(2):
                    t = 2 * i + n
                    last = nc.tensor.matmul(ps[:, n * D:(n + 1) * D], aT[:, t * P:(t + 1) * P], wout[:, hp_of, :]
                                            if isinstance(hp_of, int) else wout[:, ds(hp_of, 1), :].rearrange("p o d -> p (o d)"),
                                            start=True, stop=True)
            last.then_inc(s_fa if who == "act" else s_fd, 1)
            return last

        block = ctx.enter_context(nc.Block())

        def pair_place(eng, it, s):
            if s == 0:
                n = it * 2 + 1
            else:
                n = ((it + 1) % (NPAIR // 2)) * 2
            return n // (H2 // 2), n % (H2 // 2)

        @block.tensor
        def _(pe):
            pe.wait_ge(s_const, 16 * 4)
            pe.wait_ge(s_set, N_SET2)
            w = Place(pe, "pro", 0)
            for g in pro_plan:
                for j in g:
                    if j[0] == "pq" and j[2] == 0:
                        pe.wait_ge(s_w, 16 * 3)
                    if j[0] == "tail" and j[2] == 0:
                        pe_need(w, "pro", ("pk", 0, 1, "act"))
                    pe_job(w, j, 0, 0)
            with pe.Fori(0, NPAIR // 2) as it:
                w = Place(pe, "turn", it)
                for s in range(SLOTS):
                    for gi, g in enumerate(body_plan[s]):
                        for j in g:
                            if j[0] == "PV":
                                m = j[2]
                                if m == 0:
                                    pe_need(w, "turn", ("tt", s, 1, "act"))
                                    w.head(s_ns, s, 1, 0)
                                else:
                                    pe_need(w, "turn", ("sT", s, 2 * m + 1, "act") if m > 1 else ("tt", s, 3, "act"))
                                for h in range(2):
                                    last = nc.tensor.matmul(pv[h][:, :], v1[s][:, m, :], ex[m % RING][:, h * HB:(h + 1) * HB],
                                                            start=(m == 0), stop=(m == T - 1))
                                last.then_inc(s_pvm, 1)
                                continue
                            if j[0] == "row" and j[2] == 0:
                                w.head(s_m, s, 1, 1)
                            if j[0] == "tt" and j[2] == 0:
                                w.head(s_xt, s, 1, 1)
                            if j[0] == "sT" and j[2] == 2:
                                pe_need(w, "turn", ("row", s, 1, "act"))
                            if j[0] == "pq" and j[2] == 0:
                                pe.wait_ge(s_w, it * (2 * 48) + 48 * (2 + s // 2))
                            if j[0] == "tail" and j[2] == 0:
                                if s % 2 == 0:
                                    pe_need(w, "turn", ("pk", (s + 2) % SLOTS, 1, "act"))
                                w.head(s_zero, s, 1, 0)
                            if j[0] == "sum":
                                w.head(s_ns, s, 1, 1)
                            if j[0] == "rep" and j[2] == 0:
                                pe_need(w, "turn", ("sum", s, 0, "dve"))
                            if j[0] == "out" and j[2] == 0:
                                pe_need(w, "turn", ("rep", s, 1, "dve"))
                            b_of, hp = pair_place(pe, it, s) if j[0] in ("pq", "pk", "pv") else (0, 0)
                            if j[0] == "out":
                                hp = pe.snap((it * 2 + s // 2) % (H2 // 2))
                            elif j[0] in ("pq", "pk", "pv"):
                                b_of = pe.snap(b_of)
                            pe_job(w, j, b_of, hp)

        def act_read(w, j):
            b, n, _ = w.job(j)
            w.eng.wait_ge(s_fa, w.at("act", n))
            return bank[b]

        def act_job(w, j):
            kind, s, i, _ = j
            ps = act_read(w, j)
            half = slice(i % 2 * HB, (i % 2 + 1) * HB)
            if kind in ("pq", "pk"):
                dst, scale = (q, 1.0) if kind == "pq" else (k, DH ** -0.5)
                for e in range(2):
                    last = nc.scalar.activation(dst[s + e][0:DH, half], ps[e * DH:(e + 1) * DH, :], ACT.Copy, scale=scale)
            elif kind == "pv":
                last = nc.scalar.activation(vT[:, half], ps[:, :], ACT.Copy)
            elif kind == "vtr":
                for e in range(2):
                    last = nc.scalar.activation(v1[s + e][:, 4 * i:4 * i + 4, e * DH:(e + 1) * DH],
                                                ps[:, :].rearrange("p (n d) -> p n d", n=4)[:, :, e * DH:(e + 1) * DH], ACT.Copy)
            elif kind == "tail":
                t0, t1 = 3 * i, min(3 * i + 3, T)
                src = ps[:, 0:(t1 - t0) * TAIL].rearrange("p (t c) -> p t c", t=t1 - t0)
                nc.scalar.activation(gate[:, t0:t1, :], src, ACT.Tanh, scale=0.5)
                last = nc.scalar.activation(f[s % 2][:, t0:t1, :], src, ACT.Copy)
            elif kind == "ent":
                last = nc.scalar.activation(ent[s % 2][:, :, :], ps[:, :].rearrange("p (t c) -> p t c", t=T), ACT.Copy)
            elif kind == "row":
                last = nc.scalar.activation(q[s][DH:DH + 1, half], ps[DH:DH + 1, :], ACT.Copy)
            elif kind == "tt":
                if i < 2:
                    last = nc.scalar.activation(ex[0][:, half], ps[:, :], ACT.Copy)
                else:
                    last = nc.scalar.activation(ex[1][0:TAIL - P, half], ps[0:TAIL - P, :], ACT.Copy)
            elif kind == "sT":
                m = i // 2
                last = nc.scalar.activation(ex[m % RING][:, half], ps[:, :], ACT.Exp)
            last.then_inc(s_ra, 1)

        def groups_of_hinges(m):
            n = len(HINGES)
            return range(n * m // GROUPS, n * (m + 1) // GROUPS)

        def act_hinges(w, s, m):
            for n in groups_of_hinges(m):
                l, a0, a1 = HINGES[n]
                if n == 0:
                    w.head(s_p, s, 1, 1)
                w.head(s_used, s, len(HINGES), max(n + 1 - len(relu), 0))
                cols = (a1 - a0) * PER
                nc.scalar.activation(relu[n % 2][:, 0:T * cols].rearrange("p (t c) -> p t c", t=T),
                                     psum_p[:, :, a0 * PER:a1 * PER], ACT.Relu, bias=keep.minus[:, l:l + 1]).then_inc(s_relu, 1)

        @block.scalar
        def _(act):
            act.wait_ge(s_set, N_SET2)
            w = Place(act, "pro", 0)
            for gi, g in enumerate(pro_plan):
                for j in g:
                    if j[3] == "act":
                        if j[0] == "tail" and j[1] == 1 and j[2] == 0:
                            act.wait_ge(s_gate, 1)
                        act_job(w, j)
                if gi:
                    act_hinges(w, 0, gi - 1)
            with act.Fori(0, NPAIR // 2) as it:
                w = Place(act, "turn", it)
                for s in range(SLOTS):
                    nxt = (s + 1) % SLOTS
                    w.head(s_m, s, 1, 1)
                    for t in range(T):
                        last = nc.scalar.activation(f[s % 2][:, t, :], f[s % 2][:, t, :], ACT.Exp, bias=nmax[s % 2][:, t:t + 1])
                    last.then_inc(s_xt, 1)
                    for gi, g in enumerate(body_plan[s]):
                        for j in g:
                            if j[0] == "PV" or j[3] != "act":
                                continue
                            if j[0] == "tt" and j[2] == 0:
                                w.head(s_pvm, s, T, 0)
                            if j[0] == "sT" and j[2] % 2 == 0:
                                m = j[2] // 2
                                w.head(s_pvm, s, T, max(m + 1 - RING, 0))
                            if j[0] == "tail" and j[2] == 0:
                                w.head(s_gate, s, 1, 2)
                            if j[0] == "tt" and j[2] == 2:
                                w.eng.wait_ge(s_ra, w.at("act", w.job(("sT", s, 3, "act"))[1]))
                            act_job(w, j)
                        if 1 <= gi <= GROUPS:
                            act_hinges(w, s + 1, gi - 1)
                        if gi == GROUPS:
                            w.head(s_pvm, s, T, T)
                            n = info[("turn", ("rep", (s - 1) % SLOTS, 1, "dve"))][1]
                            act.wait_ge(s_rd, w.at("dve", n if s else n - n_turn["dve"]))
                            for h in range(2):
                                last = nc.scalar.activation(nsum[:, h * HB:(h + 1) * HB], pv[h][:, :], ACT.Copy)
                            last.then_inc(s_ns, 1)

        def low_of(tab, a0, a1, l):
            first = RISE * a0 + l
            return tab[:, :, first:RISE * (a1 - 1) + l + 1:RISE].rearrange("p t (a o) -> p t a o", o=1)\
                .to_broadcast([P, T, a1 - a0, PER])

        def blocks(ap, a0, a1):
            return ap[:, :, a0 * PER:a1 * PER].rearrange("p t (a r) -> p t a r", r=PER)

        def dve_first(w, s, link):
            e = s % 2
            w.eng.wait_ge(s_ra, after_ent(w, s))
            link(nc.vector.tensor_scalar(gate[:, :, :], gate[:, :, :], 0.5, 0.5, ALU.mult, ALU.add))
            link(nc.vector.tensor_tensor(slope[:, :, 0:TMAX - 1], ent[e][:, :, 1:TMAX], ent[e][:, :, 0:TMAX - 1], ALU.subtract))
            w.head(s_used, s, len(HINGES), 0)
            w.head(s_seen, s, 1, 0)
            last = nc.vector.tensor_tensor_scan(psum_p[:, :, :].rearrange("p t c -> p (t c)"),
                                                carry[:, :, :].rearrange("p t c -> p (t c)"),
                                                gate[:, :, :].rearrange("p t c -> p (t c)"), 0.0, ALU.mult, ALU.add)
            link(last)
            link(nc.vector.tensor_tensor(bend[:, :, 1:TMAX], slope[:, :, 1:TMAX], slope[:, :, 0:TMAX - 1], ALU.subtract))
            nc.vector.tensor_tensor(psum_p[:, :, :], psum_p[:, :, :],
                                    table[:, 0:1, :].to_broadcast([P, T, TAIL]), ALU.subtract).then_inc(s_p, 1)
            w.head(s_p, s, 1, 1)
            link(nc.vector.tensor_tensor(blocks(gate, 0, BLOCKS), blocks(psum_p, 0, BLOCKS), low_of(slope, 0, BLOCKS, 0), ALU.mult))
            nc.vector.tensor_tensor(f[e][:, :, :], f[e][:, :, :], gate[:, :, :], ALU.add).then_inc(s_gate, 1)
            w.head(s_gate, s, 1, 1)
            link(nc.vector.tensor_tensor(blocks(f[e], 0, BLOCKS), blocks(f[e], 0, BLOCKS), low_of(ent[e], 0, BLOCKS, 0), ALU.add))

        N_FIRST = 6

        def after_ent(w, s):
            if w.part == "pro":
                return w.at("act", info[("pro", ("ent", 0, 0, "act"))][1])
            if s == 1:
                n = info[("turn", ("ent", 1, 0, "act"))][1]
                return w.at("act", n - n_turn["act"])
            return w.at("act", info[("turn", ("ent", s % SLOTS, 0, "act"))][1])

        def dve_hinges(w, s, m, link):
            for n in groups_of_hinges(m):
                l, a0, a1 = HINGES[n]
                cols = (a1 - a0) * PER
                w.head(s_relu, s, len(HINGES), n + 1)
                r4 = relu[n % 2][:, 0:T * cols].rearrange("p (t a r) -> p t a r", t=T, r=PER)
                link(nc.vector.tensor_tensor(r4, r4, low_of(bend, a0, a1, l), ALU.mult))
                nc.vector.tensor_tensor(f[s % 2][:, :, a0 * PER:a1 * PER], f[s % 2][:, :, a0 * PER:a1 * PER],
                                        relu[n % 2][:, 0:T * cols].rearrange("p (t c) -> p t c", t=T),
                                        ALU.add).then_inc(s_used, 1)
                w.head(s_used, s, len(HINGES), n + 1)

        def dve_full(w, j):
            b, n, _ = w.job(j)
            w.eng.wait_ge(s_fd, w.at("dve", n))
            return bank[b]

        def dve_job(w, j, rows_at=None):
            kind, s, i, _ = j
            ps = dve_full(w, j)
            if kind == "body":
                t, h = divmod(i, 2)
                last = nc.vector.reduce_max(bmax[:, t, h:h + 1], ps[:, 0:BODY // 2], AX)
            elif kind == "sum":
                last = nc.vector.reciprocal(rcol[:, :], ps[:, 0:T])
            elif kind == "rep":
                o = DH * (s % 2)
                last = nc.vector.tensor_tensor(aT[o:o + DH, i * HB:(i + 1) * HB], nsum[o:o + DH, i * HB:(i + 1) * HB],
                                               ps[o:o + DH, :], ALU.mult)
            elif kind == "out":
                dst = rows[:, ds(rows_at, 2), :]
                last = nc.vector.tensor_tensor(dst, dst, ps[:, :].rearrange("p (n d) -> p n d", n=2), ALU.add)
            last.then_inc(s_rd, 1)

        def dve_last(w, s, link):
            e = s % 2
            link(nc.vector.tensor_reduce(tmax[:, :], f[e][:, :, :], AX, ALU.max))
            w.eng.wait_ge(s_rd, w.at("dve", w.job(("body", s % SLOTS, 2 * T - 1, "dve"))[1]))
            link(nc.vector.tensor_tensor(bm[:, :], bmax[:, :, 0], bmax[:, :, 1], ALU.max))
            link(nc.vector.tensor_tensor(bm[:, :], bm[:, :], ent[e][:, :, TMAX - 1], ALU.add))
            link(nc.vector.tensor_tensor(bm[:, :], bm[:, :], tmax[:, :], ALU.max))
            link(nc.vector.tensor_scalar(nmax[e][:, :], bm[:, :], -1.0, None, ALU.mult))
            nc.vector.tensor_tensor(shift[e][:, :], ent[e][:, :, TMAX - 1], bm[:, :], ALU.subtract).then_inc(s_m, 1)

        N_LAST = 5
        per_head = N_FIRST + len(HINGES) + N_LAST

        @block.vector
        def _(dve):
            for s in range(SLOTS):
                nc.vector.memset(q[s][DH:P, :], 0.0).then_inc(s_set, 1)
                nc.vector.memset(k[s][DH:P, :], 0.0).then_inc(s_ones, 1)
                nc.vector.memset(v1[s][:, :, DH * (1 - s % 2):DH * (2 - s % 2)], 1.0).then_inc(s_set, 1)
            for ap, val in ((one[:, :], 1.0), (zero[:, :], 0.0), (slope[:, :, TMAX - 1:TMAX], 0.0),
                            (breach[:, :, :], 0.0), (pos[DH:P, :], 0.0)):
                nc.vector.memset(ap, val).then_inc(s_set, 1)
            nc.vector.memset(carry[:, :, :], 1.0).then_inc(s_ones, 1)
            dve.wait_ge(s_ones, SLOTS + 1)
            for s in range(SLOTS):
                nc.vector.memset(k[s][DH:DH + 1, :], 1.0).then_inc(s_set, 1)
            nc.vector.memset(carry[:, :, 0:1], 0.0).then_inc(s_set, 1)
            dve.wait_ge(s_const, 16 * 4)
            dve.wait_ge(s_set, N_SET2)
            w = Place(dve, "pro", 0)
            chain = Count(dve, s_c)
            dve_first(w, 0, chain.link)
            for gi, g in enumerate(pro_plan):
                if gi:
                    for j in g:
                        dve_job(w, j)
                    dve_hinges(w, 0, gi - 1, chain.link)
            dve_last(w, 0, chain.link)
            assert chain.n == per_head, (chain.n, per_head)
            with dve.Fori(0, NPAIR // 2) as it:
                w = Place(dve, "turn", it)
                for s in range(SLOTS):
                    chain = Count(dve, s_c, it * (SLOTS * per_head) + (s + 1) * per_head)
                    for gi, g in enumerate(body_plan[s]):
                        if gi == 1:
                            dve_first(w, s + 1, chain.link)
                        for j in g:
                            if j[0] == "PV" or j[3] != "dve":
                                continue
                            at = None
                            if j[0] == "out":
                                at = dve.snap(((it * 2 + s // 2) // (H2 // 2)) * T + 2 * j[2])
                            if j[0] == "out" and j[2] == 0 and s == 1:
                                dve.wait_ge(s_saved, 16)
                            if j[0] == "sum":
                                dve_last(w, s + 1, chain.link)
                            dve_job(w, j, at)
                        if 1 <= gi <= GROUPS:
                            dve_hinges(w, s + 1, gi - 1, chain.link)
            dve.wait_ge(s_pc, (NPAIR * 2 + 1) * 5)
            nc.vector.tensor_reduce(keep.excess[:, :], breach[:, :, :].rearrange("p t c -> p (t c)"), AX,
                                    ALU.min).then_inc(s_rev, 1)

        @block.gpsimd
        def _(pool):
            def look(w, s):
                w.head(s_p, s, 1, 1)
                base = (w.it * SLOTS + s) * 5 if w.part == "turn" else 0
                chain = Count(pool, s_pc, base)
                for x, y in ((0, 1), (2, 0)):
                    v = (psum_p[:, :, :], table[:, 1:2, :].to_broadcast([P, T, TAIL]),
                         table[:, 2:3, :].to_broadcast([P, T, TAIL]))
                    ins = nc.gpsimd.tensor_tensor(over[:, :, :], v[x], v[y], ALU.subtract)
                    if y == 0:
                        ins.then_inc(s_seen, 1)
                        w.head(s_seen, s, 1, 1)
                    else:
                        chain.link(ins)
                    nc.gpsimd.tensor_tensor(idle[:, :], zero[:, :], zero[:, :], ALU.add)
                    chain.link(nc.gpsimd.tensor_scalar(over[:, :, :], over[:, :, :], 0.0, None, ALU.min))
                    chain.link(nc.gpsimd.tensor_tensor(breach[:, :, :], breach[:, :, :], over[:, :, :], ALU.add))

            pool.wait_ge(s_set, N_SET2)
            pool.wait_ge(s_const, 16 * 4)
            pool.sem_inc(s_zero, 1)
            look(Place(pool, "pro", 0), 0)
            with pool.Fori(0, NPAIR // 2) as it:
                w = Place(pool, "turn", it)
                for s in range(SLOTS):
                    look(w, s + 1)
                    w.head(s_pvm, s, T, T)
                    z = zero[DH:DH + 1, 0:1].to_broadcast([1, S])
                    nc.gpsimd.tensor_tensor(q[s][DH:DH + 1, :], z, z, ALU.add).then_inc(s_zero, 1)
                    w.head(s_zero, s, 1, 2)

        def weights_used(s):
            if s == 2:
                return info[("turn", ("pv", 2, 1, "act"))][1]
            return info[("pro", ("pv", 0, 1, "act"))][1] - n_pro["act"]

        @block.sync
        def _(sp):
            sp.dma_start(saved.rearrange("(t p) d -> p t d", p=P), rows[:, :, :]).then_inc(s_saved, 16)
            sp.dma_start(pos[0:DH, :], a["L0_attn_pos_emb"]).then_inc(s_const, 16)
            sp.dma_start(wout[:, :, :], a["L0_attn_Wout"].rearrange("(g p) n -> p g n", p=P)).then_inc(s_const, 16)
            sp.dma_start(table[:, :, :].rearrange("p a c -> p (a c)"), a["tables"].rearrange("a c -> (a c)").partition_broadcast(P)).then_inc(s_const, 16)
            sp.dma_start(keep.minus[:, :], a["minus"].partition_broadcast(P)).then_inc(s_const, 16)
            wq_r = a["L0_attn_Wq"].rearrange("(c p) n -> p c n", p=P)
            wkv_r = a["L0_attn_Wkv"].rearrange("(c p) n -> p c n", p=P)

            def pair(col):
                for x, src, o in ((0, wq_r, 0), (1, wkv_r, 0), (2, wkv_r, H2 * DH)):
                    c = col + o
                    sp.dma_start(w_in[:, x, :, :], src[:, :, ds(c, P)] if not isinstance(c, int) else src[:, :, c:c + P]).then_inc(s_w, 16)

            pair(0)
            with sp.Fori(0, NPAIR // 2) as it:
                w = Place(sp, "turn", it)
                for s in (0, 2):
                    _, hp = pair_place(sp, it, s)
                    col = sp.snap(hp * P)
                    sp.wait_ge(s_ra, w.at("act", weights_used(s)))
                    pair(col)
            sp.wait_ge(s_saved, 16)



N_SET2 = 3 * SLOTS + 5 + 1


def verdict_stage(nc, keep):
    with ExitStack() as ctx:
        line = ctx.enter_context(nc.psum_tensor("line", [1, P], F32))
        low = ctx.enter_context(nc.sbuf_tensor("lowest", [1, 2], F32))
        s_line, s_low, s_is, s_flag = (ctx.enter_context(nc.semaphore(x)) for x in
                                       ("breach_in_line", "lowest_found", "breach_judged", "flag_set"))
        block = ctx.enter_context(nc.Block())

        @block.tensor
        def _(pe):
            nc.tensor.matmul(line[:, :], keep.excess[:, :], keep.ident[:, :], start=True, stop=True).then_inc(s_line, 1)

        @block.vector
        def _(dve):
            dve.wait_ge(s_line, 1)
            nc.vector.tensor_reduce(low[:, 0:1], line[:, :], AX, ALU.min).then_inc(s_low, 1)
            dve.wait_ge(s_low, 1)
            nc.vector.tensor_scalar(low[:, 1:2], low[:, 0:1], 0.0, None, ALU.is_lt).then_inc(s_is, 1)
            dve.wait_ge(s_is, 1)
            nc.vector.tensor_copy(keep.flag[:, :], low[:, 1:2]).then_inc(s_flag, 1)
            dve.wait_ge(s_flag, 1)


def general_cope_stage(nc, keep, a, saved):
    with ExitStack() as ctx:
        def sb(name, shape, dt=F32):
            return ctx.enter_context(nc.sbuf_tensor(name, shape, dt))

        def sem(name):
            return ctx.enter_context(nc.semaphore(name))

        rows, hT, ident = keep.rows, keep.hT, keep.ident
        w_in, wout = sb("gw_in", [P, 3, KC, P]), sb("gwout", [P, D])
        pos, number = sb("gpos", [DH, TMAX]), sb("gnumber", [P, TMAX])
        q, k = [sb(f"gq{e}", [DH, S]) for e in range(2)], [sb(f"gk{e}", [DH, S]) for e in range(2)]
        vT, v = sb("gvT", [P, S]), sb("gv", [P, T, P])
        qt, ent, slope = sb("gqt", [DH, P]), sb("gent", [P, TMAX]), sb("gslope", [P, TMAX])
        gate, p, f, part, ones = (sb(n, [P, S]) for n in ("ggate", "gp", "gf", "gpart", "gones"))
        prob, probT = sb("gprob", [P, S]), sb("gprobT", [P, T, P])
        top, ntop, total, recip = (sb(n, [P, 1]) for n in ("gtop", "gntop", "gtotal", "grecip"))
        o, oT = sb("go", [P, P]), sb("goT", [P, P])

        bank = [ctx.enter_context(nc.psum_tensor(f"gbank{i}", [P, HB], F32)) for i in range(8)]
        s_const, s_w, s_set = sem("g_consts_in"), sem("g_weights_in"), sem("g_set")
        s_pj, s_pjc, s_vt, s_vc = sem("g_projected"), sem("g_qkv_copied"), sem("g_v_turned"), sem("g_v_copied")
        s_qt, s_sc, s_cp, s_f, s_c = sem("g_q_tile"), sem("g_scores"), sem("g_scores_copied"), sem("g_max"), sem("g_dve_chain")
        s_ex, s_nr, s_tp, s_tc = sem("g_exp"), sem("g_normalised"), sem("g_probs_turned"), sem("g_probsT_copied")
        s_o, s_oc, s_at, s_ac = sem("g_product"), sem("g_product_copied"), sem("g_product_turned"), sem("g_productT_copied")
        s_y, s_add = sem("g_out"), sem("g_added")

        block = ctx.enter_context(nc.Block())
        PB = H2 // 2
        CHAIN = 5 + 3 * (TMAX - 1) + 3

        @block.sync
        def _(sp):
            flag = sp.value_load(keep.flag[0:1, 0:1], min_val=0, max_val=1)
            with sp.If(flag == 1):
                sp.dma_start(pos[:, :], a["L0_attn_pos_emb"]).then_inc(s_const, 16)
                sp.dma_start(number[:, :], a["number"].partition_broadcast(P)).then_inc(s_const, 16)
                sp.dma_start(rows[:, :, :], saved.rearrange("(t p) d -> p t d", p=P)).then_inc(s_const, 16)
                wq_r = a["L0_attn_Wq"].rearrange("(c p) n -> p c n", p=P)
                wkv_r = a["L0_attn_Wkv"].rearrange("(c p) n -> p c n", p=P)
                with sp.Fori(0, B) as b:
                    with sp.Fori(0, PB) as hp:
                        col = sp.snap(hp * P)
                        colv = sp.snap(hp * P + H2 * DH)
                        sp.wait_ge(s_add, (b * PB + hp) * T)
                        sp.dma_start(w_in[:, 0, :, :], wq_r[:, :, ds(col, P)]).then_inc(s_w, 16)
                        sp.dma_start(w_in[:, 1, :, :], wkv_r[:, :, ds(col, P)]).then_inc(s_w, 16)
                        sp.dma_start(w_in[:, 2, :, :], wkv_r[:, :, ds(colv, P)]).then_inc(s_w, 16)
                        sp.dma_start(wout[:, :], a["L0_attn_Wout"][ds(col, P), :]).then_inc(s_w, 16)
            with sp.Else():
                sp.nop()

        @block.tensor
        def _(pe):
            flag = pe.value_load(keep.flag[0:1, 0:1], min_val=0, max_val=1)
            with pe.If(flag == 1):
                pe.wait_ge(s_const, 48)
                with pe.Fori(0, B) as b:
                    with pe.Fori(0, PB) as hp:
                        pe.wait_ge(s_w, (b * PB + hp) * 64 + 64)
                        for x in range(3):
                            for h in range(2):
                                for c in range(KC):
                                    last = nc.tensor.matmul(bank[2 * x + h][:, :], w_in[:, x, c, :], hT[:, c, ds(b * S + h * HB, HB)],
                                                            start=(c == 0), stop=(c == KC - 1))
                        last.then_inc(s_pj, 1)
                        pe.wait_ge(s_pjc, (b * PB + hp) + 1)
                        for t in range(T):
                            last = nc.tensor.transpose(bank[t // 4][:, t % 4 * P:(t % 4 + 1) * P], vT[:, t * P:(t + 1) * P], ident[:, :])
                        last.then_inc(s_vt, 1)
                        with pe.Fori(0, T) as i:
                            pe.wait_ge(s_vc, (b * PB + hp) + 1)
                            for e in range(2):
                                n = ((b * PB + hp) * T + i) * 2 + e
                                pe.wait_ge(s_qt, n + 1)
                                for h in range(2):
                                    nc.tensor.matmul(bank[h][:, :], qt[:, :], k[e][:, h * HB:(h + 1) * HB], start=True, stop=True)
                                nc.tensor.matmul(bank[2][:, 0:TMAX], qt[:, :], pos[:, :], start=True, stop=True).then_inc(s_sc, 1)
                                pe.wait_ge(s_nr, n + 1)
                                for t in range(T):
                                    last = nc.tensor.transpose(bank[3 + t // 4][:, t % 4 * P:(t % 4 + 1) * P],
                                                               prob[:, t * P:(t + 1) * P], ident[:, :])
                                last.then_inc(s_tp, 1)
                                pe.wait_ge(s_tc, n + 1)
                                for t in range(T):
                                    last = nc.tensor.matmul(bank[5][:, 0:DH], probT[:, t, :], v[:, t, e * DH:(e + 1) * DH],
                                                            start=(t == 0), stop=(t == T - 1))
                                last.then_inc(s_o, 1)
                            m = (b * PB + hp) * T + i
                            pe.wait_ge(s_oc, m * 2 + 2)
                            nc.tensor.transpose(bank[6][:, 0:P], o[:, :], ident[:, :]).then_inc(s_at, 1)
                            pe.wait_ge(s_ac, m + 1)
                            nc.tensor.matmul(bank[7][:, 0:D], oT[:, :], wout[:, :], start=True, stop=True).then_inc(s_y, 1)
                            pe.wait_ge(s_add, m + 1)
            with pe.Else():
                pe.nop()

        @block.scalar
        def _(act):
            flag = act.value_load(keep.flag[0:1, 0:1], min_val=0, max_val=1)
            with act.If(flag == 1):
                with act.Fori(0, B) as b:
                    with act.Fori(0, PB) as hp:
                        act.wait_ge(s_pj, (b * PB + hp) + 1)
                        for h in range(2):
                            half = slice(h * HB, (h + 1) * HB)
                            for e in range(2):
                                nc.scalar.activation(q[e][:, half], bank[h][e * DH:(e + 1) * DH, :], ACT.Copy)
                                nc.scalar.activation(k[e][:, half], bank[2 + h][e * DH:(e + 1) * DH, :], ACT.Copy, scale=DH ** -0.5)
                            last = nc.scalar.activation(vT[:, half], bank[4 + h][:, :], ACT.Copy)
                        last.then_inc(s_pjc, 1)
                        act.wait_ge(s_pjc, (b * PB + hp) + 1)
                        act.wait_ge(s_vt, (b * PB + hp) + 1)
                        for h in range(2):
                            last = nc.scalar.activation(v[:, 4 * h:4 * h + 4, :], bank[h][:, :].rearrange("p (t d) -> p t d", t=4), ACT.Copy)
                        last.then_inc(s_vc, 1)
                        with act.Fori(0, T) as i:
                            for e in range(2):
                                n = ((b * PB + hp) * T + i) * 2 + e
                                act.wait_ge(s_oc, n)
                                nc.scalar.activation(qt[:, :], q[e][:, ds(i * P, P)], ACT.Copy).then_inc(s_qt, 1)
                                act.wait_ge(s_sc, n + 1)
                                for h in range(2):
                                    half = slice(h * HB, (h + 1) * HB)
                                    nc.scalar.activation(gate[:, half], bank[h][:, :], ACT.Tanh, scale=0.5)
                                    nc.scalar.activation(f[:, half], bank[h][:, :], ACT.Copy)
                                nc.scalar.activation(ent[:, :], bank[2][:, 0:TMAX], ACT.Copy).then_inc(s_cp, 1)
                                act.wait_ge(s_f, n + 1)
                                nc.scalar.activation(prob[:, :], f[:, :], ACT.Exp, bias=ntop[:, :], accum_out=total[:, :]).then_inc(s_ex, 1)
                                act.wait_ge(s_tp, n + 1)
                                for h in range(2):
                                    last = nc.scalar.activation(probT[:, 4 * h:4 * h + 4, :], bank[3 + h][:, :].rearrange("p (t d) -> p t d", t=4), ACT.Copy)
                                last.then_inc(s_tc, 1)
                                act.wait_ge(s_o, n + 1)
                                nc.scalar.activation(o[:, e * DH:(e + 1) * DH], bank[5][:, 0:DH], ACT.Copy).then_inc(s_oc, 1)
                            m = (b * PB + hp) * T + i
                            act.wait_ge(s_at, m + 1)
                            nc.scalar.activation(oT[:, :], bank[6][:, 0:P], ACT.Copy).then_inc(s_ac, 1)
            with act.Else():
                act.nop()

        @block.vector
        def _(dve):
            flag = dve.value_load(keep.flag[0:1, 0:1], min_val=0, max_val=1)
            with dve.If(flag == 1):
                nc.vector.memset(ones[:, :], 1.0).then_inc(s_set, 1)
                dve.wait_ge(s_set, 1)
                dve.wait_ge(s_const, 48)
                with dve.Fori(0, B) as b:
                    with dve.Fori(0, PB) as hp:
                        with dve.Fori(0, T) as i:
                            for e in range(2):
                                n = ((b * PB + hp) * T + i) * 2 + e
                                dve.wait_ge(s_cp, n + 1)
                                chain = Count(dve, s_c, n * CHAIN)
                                chain.link(nc.vector.tensor_scalar(gate[:, :], gate[:, :], 0.5, 0.5, ALU.mult, ALU.add))
                                chain.link(nc.vector.tensor_tensor_scan(p[:, :], ones[:, :], gate[:, :], 0.0, ALU.mult, ALU.add))
                                chain.link(nc.vector.tensor_scalar(p[:, :], p[:, :], float(TMAX - 1), None, ALU.min))
                                chain.link(nc.vector.tensor_tensor(slope[:, 0:TMAX - 1], ent[:, 1:TMAX], ent[:, 0:TMAX - 1], ALU.subtract))
                                chain.inc(nc.vector.tensor_scalar(f[:, :], f[:, :], ent[:, 0:1], None, ALU.add))
                                with dve.Fori(0, TMAX - 1) as j:
                                    hinge = Count(dve, s_c, n * CHAIN + 5 + j * 3)
                                    dve.wait_ge(s_c, n * CHAIN + 5 + j * 3)
                                    hinge.link(nc.vector.tensor_scalar(part[:, :], p[:, :], number[:, ds(j, 1)], 0.0, ALU.subtract, ALU.max))
                                    hinge.link(nc.vector.tensor_scalar(part[:, :], part[:, :], 1.0, slope[:, ds(j, 1)], ALU.min, ALU.mult))
                                    hinge.inc(nc.vector.tensor_tensor(f[:, :], f[:, :], part[:, :], ALU.add))
                                chain.n += 3 * (TMAX - 1)
                                dve.wait_ge(s_c, n * CHAIN + 5 + 3 * (TMAX - 1))
                                chain.link(nc.vector.reduce_max(top[:, :], f[:, :], AX))
                                nc.vector.tensor_scalar(ntop[:, :], top[:, :], -1.0, None, ALU.mult).then_inc(s_f, 1)
                                dve.wait_ge(s_ex, n + 1)
                                chain.link(nc.vector.reciprocal(recip[:, :], total[:, :]))
                                chain.link(nc.vector.tensor_copy(part[:, 0:1], recip[:, :]))
                                nc.vector.tensor_scalar(prob[:, :], prob[:, :], recip[:, :], None, ALU.mult).then_inc(s_nr, 1)
                                assert chain.n == CHAIN
                            m = (b * PB + hp) * T + i
                            at = dve.snap(b * T + i)
                            dve.wait_ge(s_y, m + 1)
                            nc.vector.tensor_tensor(rows[:, ds(at, 1), :].rearrange("p o d -> p (o d)"),
                                                    rows[:, ds(at, 1), :].rearrange("p o d -> p (o d)"), bank[7][:, 0:D], ALU.add).then_inc(s_add, 1)
            with dve.Else():
                dve.nop()


def route_stage(nc, keep, a, xp):
    with ExitStack() as ctx:
        def sb(name, shape, dt=F32):
            return ctx.enter_context(nc.sbuf_tensor(name, shape, dt))

        def sem(name):
            return ctx.enter_context(nc.semaphore(name))

        rows = keep.rows
        normed = sb("normed", [P, NT, D])
        n = sb("n3", [P, T, D])
        nT = sb("nT3", [P, KC, S])
        rw = sb("rw", [P, KC, E])
        experts = sb("experts", [P, E])
        upto = sb("upto", [P, P])
        ones = sb("ones3", [P, P])
        logit, best = sb("logit", [P, T, E]), sb("best", [P, T, 8])
        best_i, best_f = sb("best_i", [P, T, 8], U32), sb("best_f", [P, T, TOPK])
        diff, ratio, den = sb("diff", [P, T]), sb("ratio", [P, T]), sb("den", [P, T])
        hot = [sb(f"hot{i}", [P, NT, E]) for i in range(TOPK)]
        both = sb("both", [P, NT, E])
        before, total = sb("before", [P, NT, E]), sb("total", [P, NT, E])
        run = sb("run", [P, E, NT])
        ends = sb("ends", [P, E])
        one_nt = sb("one_nt", [P, NT])
        picked = sb("picked", [P, NT, E])
        place_f = sb("place_f", [P, TOPK, NT])
        stats, mv, rstd = sb("stats3", [P, T, 6]), sb("mv3", [P, T, 2]), sb("rstd3", [P, T])
        work = [ctx.enter_context(nc.psum_tensor(f"work3_{i}", [P, HB], F32)) for i in range(4)]
        plog = ctx.enter_context(nc.psum_tensor("plog", [P, HB], F32))
        pcount = [ctx.enter_context(nc.psum_tensor(f"pcount{i}", [P, HB], F32)) for i in range(2)]

        s_in, s_set, s_var, s_root, s_c = sem("router_in"), sem("set3"), sem("var3"), sem("root3"), sem("dve_chain3")
        s_n, s_tr, s_nT, s_log = sem("n3_ready"), sem("transposed3"), sem("nT3_ready"), sem("logits_ready")
        s_e, s_ed, s_sel, s_cnt, s_place = (sem("diff_ready"), sem("ratio_ready"), sem("chosen"), sem("counted"), sem("places_ready"))
        s_sc, s_tri = sem("rows_scattered"), sem("upto_set")

        block = ctx.enter_context(nc.Block())

        @block.sync
        def _(sp):
            with nc.allow_non_contiguous_dma(reason="the router's weights, transposed: 8 KB"):
                for c in range(KC):
                    sp.dma_start(rw[:, c, :], a["L0_ffn_router_w"][:, c * P:(c + 1) * P].rearrange("e p -> p e")).then_inc(s_in, 16)

        @block.gpsimd
        def _(pool):
            nc.gpsimd.memset(ones[:, :], 1.0).then_inc(s_set, 1)
            nc.gpsimd.memset(upto[:, :], 1.0).then_inc(s_set, 1)
            nc.gpsimd.memset(one_nt[:, :], 1.0).then_inc(s_set, 1)
            nc.gpsimd.iota(experts[:, :], pattern=[[1, E]], base=0, channel_multiplier=0,
                           allow_small_or_imprecise_dtypes=True).then_inc(s_set, 1)
            pool.wait_ge(s_set, 4)
            nc.gpsimd.affine_select(out=upto[:, :], in_=upto[:, :], compare_op=ALU.is_ge, fill=0.0, base=0,
                                    pattern=[[1, P]], channel_multiplier=-1).then_inc(s_tri, 1)
            pool.wait_ge(s_place, 1)
            for t in range(NT):
                for i in range(TOPK):
                    pool.indirect_dma_start(xp, bass.IndirectOffsetOnAxis(ap=keep.place[:, i, t:t + 1], axis=0),
                                            normed[:, t, :], None).then_inc(s_sc, 16)
            pool.wait_ge(s_sc, 16 * NT * TOPK)

        @block.vector
        def _(dve):
            dve.wait_ge(s_set, 4)
            links = 8
            with dve.Fori(0, B) as b:
                chain = Count(dve, s_c, b * links)
                tiles = ds(b * T, T)

                def root(last):
                    last.then_inc(s_var, 1)
                    dve.wait_ge(s_root, b + 1)

                chain.link(nc.vector.tensor_copy(n[:, :, :], rows[:, tiles, :]))
                layernorm_rows(nc, chain.link, lambda last: last.then_inc(s_n, 1), n, n, T, stats, mv, rstd, root,
                               lambda: nc.vector.tensor_copy(rstd[:, 0:1], stats[:, T - 1, 0:1]))
                dve.wait_ge(s_n, b + 1)
                nc.vector.tensor_copy(normed[:, tiles, :], n[:, :, :])
                dve.wait_ge(s_log, b + 1)
                chain.link(nc.vector.tensor_copy(logit[:, :, :], plog[:, 0:T * E].rearrange("p (t e) -> p t e", t=T)))
                nc.vector.tensor_copy(den[:, 0:1], logit[:, T - 1, 0:1])
                for t in range(T):
                    last = nc.vector.max(best[:, t, :], logit[:, t, :])
                chain.link(last)
                nc.vector.tensor_copy(den[:, 0:1], best[:, T - 1, 0:1])
                for t in range(T):
                    last = nc.vector.max_index(best_i[:, t, :], best[:, t, :], logit[:, t, :])
                nc.vector.tensor_tensor(diff[:, :], best[:, :, 1], best[:, :, 0], ALU.subtract).then_inc(s_e, 1)
                dve.wait_ge(s_e, b + 1)
                chain.link(nc.vector.tensor_copy(best_f[:, :, :], best_i[:, :, 0:TOPK]))
                for i in range(TOPK):
                    last = nc.vector.tensor_tensor(hot[i][:, tiles, :], experts[:, :].rearrange("p (o e) -> p o e", o=1).to_broadcast([P, T, E]),
                                                   best_f[:, :, i:i + 1].to_broadcast([P, T, E]), ALU.is_equal)
                dve.wait_ge(s_ed, b + 1)
                chain.link(nc.vector.tensor_scalar(den[:, :], ratio[:, :], 1.0, None, ALU.add))
                chain.link(nc.vector.reciprocal(den[:, :], den[:, :]))
                nc.vector.tensor_copy(keep.weight[:, 0:1, tiles].rearrange("p o t -> p (o t)"), den[:, :])
                nc.vector.tensor_tensor(keep.weight[:, 1:2, tiles].rearrange("p o t -> p (o t)"), den[:, :], ratio[:, :], ALU.mult)
                assert chain.n == links
            chain = Count(dve, s_c, B * links)
            nc.vector.tensor_tensor(both[:, :, :], hot[0][:, :, :], hot[1][:, :, :], ALU.add).then_inc(s_sel, 1)
            dve.wait_ge(s_cnt, 1)
            nc.vector.tensor_copy(before[:, :, :], pcount[0][:, 0:NT * E].rearrange("p (t e) -> p t e", t=NT))
            chain.link(nc.vector.tensor_copy(total[:, :, :], pcount[1][:, 0:NT * E].rearrange("p (t e) -> p t e", t=NT)))
            for e in range(E):
                last = nc.vector.tensor_tensor_scan(run[:, e, :], one_nt[:, :], total[:, :, e], 0.0, ALU.mult, ALU.add)
            chain.link(last)
            chain.link(nc.vector.tensor_tensor_scan(ends[:, :], one_nt[:, 0:E], run[:, :, NT - 1], 0.0, ALU.mult, ALU.add))
            chain.link(nc.vector.tensor_tensor(before[:, :, :], before[:, :, :], total[:, :, :], ALU.subtract))
            chain.link(nc.vector.tensor_tensor(before[:, :, :], before[:, :, :], run[:, :, :].rearrange("p e t -> p t e"), ALU.add))
            chain.link(nc.vector.tensor_tensor(before[:, :, :], ends[:, :].rearrange("p (o e) -> p o e", o=1).to_broadcast([P, NT, E]),
                                               before[:, :, :], ALU.subtract))
            for i in range(TOPK):
                chain.link(nc.vector.tensor_tensor(picked[:, :, :], hot[i][:, :, :], before[:, :, :], ALU.mult))
                chain.link(nc.vector.tensor_reduce(place_f[:, i, :], picked[:, :, :], AX, ALU.add))
            nc.vector.tensor_copy(keep.place[:, :, :], place_f[:, :, :]).then_inc(s_place, 1)

        @block.scalar
        def _(act):
            with act.Fori(0, B) as b:
                act.wait_ge(s_var, b + 1)
                nc.scalar.activation(rstd[:, :], mv[:, :, 1], ACT.Sqrt, bias=keep.eps[:, :]).then_inc(s_root, 1)
                for i in range(4):
                    c, h = divmod(i, 2)
                    act.wait_ge(s_tr, b * 4 + i + 1)
                    nc.scalar.activation(nT[:, c, h * HB:(h + 1) * HB], work[i][:, :], ACT.Copy).then_inc(s_nT, 1)
                act.wait_ge(s_e, b + 1)
                nc.scalar.activation(ratio[:, :], diff[:, :], ACT.Exp).then_inc(s_ed, 1)

        @block.tensor
        def _(pe):
            pe.wait_ge(s_in, 16 * KC)
            pe.wait_ge(s_tri, 1)
            pe.wait_ge(s_set, 4)
            with pe.Fori(0, B) as b:
                pe.wait_ge(s_n, b + 1)
                pe.wait_ge(s_nT, b * 4)
                for i in range(4):
                    c, h = divmod(i, 2)
                    for j in range(4):
                        last = nc.tensor.transpose(work[i][:, j * P:(j + 1) * P], n[:, 4 * h + j, c * P:(c + 1) * P], keep.ident[:, :])
                    last.then_inc(s_tr, 1)
                pe.wait_ge(s_nT, b * 4 + 4)
                pe.wait_ge(s_e, b)
                for t in range(T):
                    for c in range(KC):
                        last = nc.tensor.matmul(plog[:, t * E:(t + 1) * E], nT[:, c, t * P:(t + 1) * P], rw[:, c, :],
                                                start=(c == 0), stop=(c == KC - 1))
                last.then_inc(s_log, 1)
            pe.wait_ge(s_sel, 1)
            nc.tensor.matmul(pcount[0][:, 0:NT * E], upto[:, :], both[:, :, :].rearrange("p t e -> p (t e)"), start=True, stop=True)
            nc.tensor.matmul(pcount[1][:, 0:NT * E], ones[:, :], both[:, :, :].rearrange("p t e -> p (t e)"),
                             start=True, stop=True).then_inc(s_cnt, 1)


def expert_stage(nc, keep, a, xp, yp):
    with ExitStack() as ctx:
        def sb(name, shape, dt=F32):
            return ctx.enter_context(nc.sbuf_tensor(name, shape, dt))

        def sem(name):
            return ctx.enter_context(nc.semaphore(name))

        CR = NR // E
        CT = CR // P
        x = [sb(f"x4_{i}", [P, CT, D]) for i in range(2)]
        xT = sb("xT4", [P, KC, CR])
        w1 = [sb(f"w1_{i}", [P, KC, FF]) for i in range(2)]
        w2 = [sb(f"w2_{i}", [P, FC, D]) for i in range(2)]
        hT = sb("hT4", [P, FC, CR])
        y = [sb(f"y4_{i}", [P, CT, D]) for i in range(2)]
        pt = [ctx.enter_context(nc.psum_tensor(f"pt{i}", [P, HB], F32)) for i in range(2)]
        ph = [ctx.enter_context(nc.psum_tensor(f"ph{i}", [P, HB], F32)) for i in range(3)]
        py = [ctx.enter_context(nc.psum_tensor(f"py{i}", [P, HB], F32)) for i in range(3)]
        s_in = [sem(f"expert_in{i}") for i in range(2)]
        s_tr, s_xT, s_h, s_g, s_y, s_ys, s_out = (sem("x_transposed"), sem("xT_ready"), sem("h_ready4"), sem("gelu_ready"),
                                                  sem("y_ready"), sem("y_copied"), sem("y_written"))
        NH, NY = FC * CR // HB, CT // 2
        block = ctx.enter_context(nc.Block())
        xv = xp.rearrange("(e t p) d -> e p t d", p=P, t=CT)
        yv = yp.rearrange("(e t p) d -> e p t d", p=P, t=CT)

        @block.sync
        def _(sp):
            def load(e, i):
                at = slice(e, e + 1) if isinstance(e, int) else ds(e, 1)
                sp.dma_start(x[i][:, :, :], xv[at].rearrange("o p t d -> p (o t) d")).then_inc(s_in[i], 16)
                sp.dma_start(w1[i][:, :, :], a["L0_ffn_w1"][at].rearrange("o (c p) f -> p (o c) f", p=P)).then_inc(s_in[i], 16)
                sp.dma_start(w2[i][:, :, :], a["L0_ffn_w2"][at].rearrange("o (c p) f -> p (o c) f", p=P)).then_inc(s_in[i], 16)

            load(0, 0)
            load(1, 1)
            with sp.Fori(0, E // 2 - 1) as it:
                for i in range(2):
                    e = sp.snap(it * 2 + i + 2)
                    sp.wait_ge(s_ys, it * (2 * NY) + (i + 1) * NY)
                    load(e, i)

        @block.gpsimd
        def _(pool):
            with pool.Fori(0, E // 2) as it:
                for i in range(2):
                    e = pool.snap(it * 2 + i)
                    pool.wait_ge(s_ys, it * (2 * NY) + (i + 1) * NY)
                    pool.dma_start(yv[ds(e, 1)].rearrange("o p t d -> p (o t) d"), y[i][:, :, :]).then_inc(s_out, 16)
            pool.wait_ge(s_out, 16 * E)

        @block.tensor
        def _(pe):
            with pe.Fori(0, E // 2) as it:
                for i in range(2):
                    pe.wait_ge(s_in[i], it * 48 + 48)
                    nx, nh, ny = it * 8 + i * 4, it * (2 * NH) + i * NH, it * (2 * NY) + i * NY
                    for j in range(4):
                        c, h = divmod(j, 2)
                        pe.wait_ge(s_xT, nx + j - 1 if j >= 1 else nx)
                        for k in range(4):
                            last = nc.tensor.transpose(pt[j % 2][:, k * P:(k + 1) * P], x[i][:, 4 * h + k, c * P:(c + 1) * P], keep.ident[:, :])
                        last.then_inc(s_tr, 1)
                    pe.wait_ge(s_xT, nx + 4)
                    for j in range(NH):
                        f, h = divmod(j, CR // HB)
                        pe.wait_ge(s_g, nh + max(j - 2, 0))
                        for c in range(KC):
                            last = nc.tensor.matmul(ph[j % 3][:, :], w1[i][:, c, f * P:(f + 1) * P], xT[:, c, h * HB:(h + 1) * HB],
                                                    start=(c == 0), stop=(c == KC - 1))
                        last.then_inc(s_h, 1)
                    pe.wait_ge(s_g, nh + NH)
                    for j in range(NY):
                        pe.wait_ge(s_ys, ny + max(j - 2, 0))
                        for k in range(2):
                            t = 2 * j + k
                            for f in range(FC):
                                last = nc.tensor.matmul(py[j % 3][:, k * D:(k + 1) * D], hT[:, f, t * P:(t + 1) * P], w2[i][:, f, :],
                                                        start=(f == 0), stop=(f == FC - 1))
                        last.then_inc(s_y, 1)

        @block.scalar
        def _(act):
            with act.Fori(0, E // 2) as it:
                for i in range(2):
                    nh, ny = it * (2 * NH) + i * NH, it * (2 * NY) + i * NY
                    act.wait_ge(s_y, ny)
                    for j in range(NH):
                        f, h = divmod(j, CR // HB)
                        act.wait_ge(s_h, nh + j + 1)
                        nc.scalar.activation(hT[:, f, h * HB:(h + 1) * HB], ph[j % 3][:, :], ACT.Gelu).then_inc(s_g, 1)

        @block.vector
        def _(dve):
            with dve.Fori(0, E // 2) as it:
                for i in range(2):
                    nx, ny = it * 8 + i * 4, it * (2 * NY) + i * NY
                    for j in range(4):
                        c, h = divmod(j, 2)
                        dve.wait_ge(s_tr, nx + j + 1)
                        nc.vector.tensor_copy(xT[:, c, h * HB:(h + 1) * HB], pt[j % 2][:, :]).then_inc(s_xT, 1)
                    dve.wait_ge(s_out, it * 32 + max(i - 1, 0) * 16)
                    for j in range(NY):
                        dve.wait_ge(s_y, ny + j + 1)
                        nc.vector.tensor_copy(y[i][:, 2 * j:2 * j + 2, :], py[j % 3][:, :].rearrange("p (k d) -> p k d", k=2)).then_inc(s_ys, 1)


def combine_stage(nc, keep, yp, out):
    with ExitStack() as ctx:
        RG = 6
        got = [ctx.enter_context(nc.sbuf_tensor(f"got{i}", [P, TOPK, D], F32)) for i in range(RG)]
        s_got = [ctx.enter_context(nc.semaphore(f"gathered{i}")) for i in range(RG)]
        s_sum, s_first, s_out = (ctx.enter_context(nc.semaphore(x)) for x in ("summed", "first_added", "out_written"))
        block = ctx.enter_context(nc.Block())

        @block.gpsimd
        def _(pool):
            for t in range(NT):
                if t >= RG:
                    pool.wait_ge(s_sum, t - RG + 1)
                for i in range(TOPK):
                    pool.indirect_dma_start(got[t % RG][:, i, :], None, yp,
                                            bass.IndirectOffsetOnAxis(ap=keep.place[:, i, t:t + 1], axis=0)).then_inc(s_got[t % RG], 16)

        @block.vector
        def _(dve):
            for t in range(NT):
                dve.wait_ge(s_got[t % RG], 32 * (t // RG + 1))
                row = keep.rows[:, t, :]
                nc.vector.scalar_tensor_tensor(row, got[t % RG][:, 0, :], keep.weight[:, 0, t:t + 1], row, ALU.mult, ALU.add).then_inc(s_first, 1)
                dve.wait_ge(s_first, t + 1)
                nc.vector.scalar_tensor_tensor(row, got[t % RG][:, 1, :], keep.weight[:, 1, t:t + 1], row, ALU.mult, ALU.add).then_inc(s_sum, 1)

        @block.sync
        def _(sp):
            for t in range(0, NT, 4):
                sp.wait_ge(s_sum, t + 4)
                sp.dma_start(out[t * P:(t + 4) * P, :].rearrange("(t p) d -> p t d", p=P), keep.rows[:, t:t + 4, :]).then_inc(s_out, 16)
            sp.wait_ge(s_out, 16 * (NT // 4))


class Keep:
    pass


def program(nc, a, out):
    with ExitStack() as ctx:
        def sb(name, shape, dt=F32):
            return ctx.enter_context(nc.sbuf_tensor(name, shape, dt))

        keep = Keep()
        keep.ident = sb("ident", [P, P])
        keep.eps = sb("eps", [P, 1])
        keep.bout = sb("bout", [P, D])
        keep.excess = sb("excess", [P, 1])
        keep.minus = sb("minus", [P, 32])
        keep.flag = sb("flag", [1, 1], I32)
        keep.rows = sb("rows", [P, NT, D])
        with nc.sbuf_tensor("hT", [P, KC, R], F32) as keep.hT:
            constants(nc, keep)
            token_stage(nc, keep, a["ids"], a["L0_tok_emb_table"], a["pos"], a["L0_tok_Wq"], a["L0_tok_bq"],
                        a["L0_tok_Wk"], a["L0_tok_bk"], a["L0_tok_Wv"], a["L0_tok_bv"], a["L0_tok_Wf"],
                        a["L0_tok_bf"], a["L0_attn_b_out"])
            saved = nc.dram_tensor("saved_rows", [R, D], F32, kind="Internal").ap()
            cope_stage(nc, keep, a, saved)
            verdict_stage(nc, keep)
            general_cope_stage(nc, keep, a, saved)
        keep.place = sb("place", [P, TOPK, NT], I32)
        keep.weight = sb("weight", [P, TOPK, NT])
        xp = nc.dram_tensor("sorted_rows", [NR, D], F32, kind="Internal").ap()
        yp = nc.dram_tensor("sorted_results", [NR, D], F32, kind="Internal").ap()
        route_stage(nc, keep, a, xp)
        expert_stage(nc, keep, a, xp, yp)
        combine_stage(nc, keep, yp, out)


def constants(nc, keep):
    with nc.semaphore("zeros_set") as s_zero, nc.semaphore("const_set") as s_set, nc.Block() as block:
        @block.gpsimd
        def _(pool):
            nc.gpsimd.memset(keep.ident[:, :], 0.0).then_inc(s_zero, 1)
            nc.gpsimd.memset(keep.eps[:, :], EPS).then_inc(s_zero, 1)
            pool.wait_ge(s_zero, 2)
            nc.gpsimd.affine_select(out=keep.ident[:, :], in_=keep.ident[:, :], compare_op=ALU.not_equal, fill=1.0,
                                    base=0, pattern=[[-1, P]], channel_multiplier=1).then_inc(s_set, 1)
            pool.wait_ge(s_set, 1)


def kernel(**inputs):
    import numpy as _np
    import concourse.bacc as _bacc
    from concourse.bass_utils import run_bass_kernel_spmd as _run

    nc = _bacc.Bacc("TRN2", target_bir_lowering=False, num_devices=1)
    arrays = {k: _np.ascontiguousarray(v) for k, v in inputs.items() if k != "x"}
    x = _np.asarray(inputs["x"])
    arrays["ids"] = _np.ascontiguousarray(x.reshape(R)[::-1].reshape(NT, P).T)
    div = _np.exp(_np.arange(0, D, 2, dtype=_np.float32) * _np.float32(-_np.log(10000.0) / D))
    angle = _np.arange(S, dtype=_np.float32)[:, None] * div.astype(_np.float32)
    pos = _np.zeros((S, D), _np.float32)
    pos[:, 0::2], pos[:, 1::2] = _np.sin(angle), _np.cos(angle)
    arrays["pos"] = _np.ascontiguousarray(pos[::-1])
    arrays["tables"] = cope_tables()
    arrays["number"] = _np.arange(TMAX, dtype=_np.float32)
    arrays["minus"] = -_np.arange(32, dtype=_np.float32)
    feed, aps = {}, {}
    for name, v in arrays.items():
        feed[f"in_{name}"] = v
        aps[name] = nc.dram_tensor(f"in_{name}", v.shape, I32 if v.dtype.kind == "i" else F32, kind="ExternalInput").ap()
    out = nc.dram_tensor("out_rows", [R, D], F32, kind="ExternalOutput").ap()
    program(nc, aps, out)
    r = _run(nc, [feed], core_ids=[0])
    return _np.ascontiguousarray(r.results[0]["out_rows"][::-1].reshape(B, S, D))
```

```python
from contextlib import ExitStack

import concourse.bass as bass
from concourse import mybir

F32 = mybir.dt.float32
I32 = mybir.dt.int32
U32 = mybir.dt.uint32
ALU = mybir.AluOpType
ACT = mybir.ActivationFunctionType
AX = mybir.AxisListType.X
ds = bass.ds

P = 128
B, S, D = 4, 1024, 256
R = B * S
T = S // P
NT = R // P
KC = D // P
HB = 512
H1, DH = 4, 64
H2 = 16
NPAIR = B * H2 // 2
EPS = 1e-5
TMAX = DH
E, FF, TOPK = 8, 1024, 2
NR = R * TOPK
FC = FF // P


class Count:

    def __init__(self, eng, sem, base=0):
        self.eng, self.sem, self.base, self.n = eng, sem, base, 0

    def inc(self, instruction):
        self.n += 1
        instruction.then_inc(self.sem, 1)

    def link(self, instruction):
        self.inc(instruction)
        self.eng.wait_ge(self.sem, self.base + self.n)


def bcast(ap, shape):
    return ap.to_broadcast(shape)


def layernorm_rows(nc, link, inc_last, x, out, n, stats, mv, rstd, act_sqrt, settled):
    for i in range(n):
        last = nc.vector.bn_stats(stats[:, i, :], x[:, i, :])
    link(last)
    settled()
    for i in range(n):
        last = nc.vector.bn_aggr(mv[:, i, :], stats[:, i, :])
    act_sqrt(last)
    link(nc.vector.reciprocal(rstd[:, 0:n], rstd[:, 0:n]))
    for i in range(n):
        last = nc.vector.tensor_scalar(out[:, i, :], x[:, i, :], mv[:, i, 0:1], rstd[:, i:i + 1],
                                       ALU.subtract, ALU.mult)
    inc_last(last)


def token_stage(nc, keep, ids, emb, pos, wq, bq, wk, bk, wv, bv, wf, bf, b_out):
    with ExitStack() as ctx:
        def sb(name, shape, dt=F32):
            return ctx.enter_context(nc.sbuf_tensor(name, shape, dt))

        def sem(name):
            return ctx.enter_context(nc.semaphore(name))

        rows, hT = keep.rows, keep.hT
        ids_sb = sb("ids_sb", [P, NT], I32)
        pos_sb = sb("pos_sb", [P, T, D])
        wq_sb, wk_sb, wv_sb, wf_sb = (sb(n, [P, KC, D]) for n in ("wq1", "wk1", "wv1", "wf1"))
        bq_sb, bk_sb = sb("bq1", [P, 2]), sb("bk1", [P, 2])
        bv_sb, bf_sb = sb("bv1", [P, D]), sb("bf1", [P, D])
        bout = sb("bout", [P, D])
        x = sb("x1", [P, T, D])
        xT = sb("xT1", [P, KC, S])
        qT, kT = sb("qT1", [P, 2, S]), sb("kT1", [P, 2, S])
        v = sb("v1", [P, T, D])
        vs = sb("vs1", [P, 2, T, DH])
        probs = sb("probs1", [P, 2, T, S])
        z = sb("z1", [P, T, D])
        mx, nmx = sb("mx1", [P, T]), sb("nmx1", [P, 2, T])
        ssum, rsum = sb("ssum1", [P, 2, T]), sb("rsum1", [P, T])
        stats, mv, rstd = sb("stats1", [P, T, 6]), sb("mv1", [P, T, 2]), sb("rstd1", [P, T])

        work = [ctx.enter_context(nc.psum_tensor(f"work1_{i}", [P, HB], F32)) for i in range(3)]
        score = [ctx.enter_context(nc.psum_tensor(f"score1_{i}", [P, S], F32)) for i in range(2)]
        zp = ctx.enter_context(nc.psum_tensor("zp1", [P, HB], F32))

        s_w, s_ids, s_gather = sem("weights_in"), sem("ids_in"), sem("rows_gathered")
        s_x, s_tr, s_xT = sem("x_ready"), sem("work_full_for_act"), sem("work_copied_by_act")
        s_vp, s_v = sem("work_full_for_dve"), sem("work_read_by_dve")
        s_score, s_mx, s_max, s_exp = sem("score_ready"), sem("max_found"), sem("minus_max_ready"), sem("exp_ready")
        s_vs, s_z, s_zread = sem("scaled_v_ready"), sem("z_ready"), sem("z_read")
        s_zz, s_var, s_root, s_c = sem("zn_ready"), sem("var_ready"), sem("root_ready"), sem("dve_chain1")
        s_h = sem("h_ready")

        jobs = ([("xT", c, h, "act") for c in range(KC) for h in range(2)]
                + [(n, g, h, "act") for n in ("q", "k") for g in range(2) for h in range(2)]
                + [("v", t, 0, "dve") for t in range(T // 2)]
                + [("zT", c, h, "act") for c in range(KC) for h in range(2)]
                + [("ff", t, 0, "dve") for t in range(T // 2)]
                + [("hT", c, h, "act") for c in range(KC) for h in range(2)])
        n_act = sum(j[3] == "act" for j in jobs)
        n_dve = len(jobs) - n_act
        nb = len(work)

        def done_before(j, who):
            return sum(k[3] == who for k in jobs[:j])

        def first(name):
            return next(j for j, k in enumerate(jobs) if k[0] == name)

        block = ctx.enter_context(nc.Block())

        @block.sync
        def _(sp):
            sp.dma_start(ids_sb[:, :], ids).then_inc(s_ids, 16)
            sp.dma_start(pos_sb[:, :, :], pos.rearrange("(t p) d -> p t d", p=P)).then_inc(s_w, 16)
            for dst, src in ((wq_sb, wq), (wk_sb, wk), (wv_sb, wv)):
                for h in range(H1):
                    sp.dma_start(dst[:, :, h * DH:(h + 1) * DH],
                                 src[h].rearrange("(c p) d -> p c d", p=P)).then_inc(s_w, 16)
            sp.dma_start(wf_sb[:, :, :], wf.rearrange("(c p) n -> p c n", p=P)).then_inc(s_w, 16)
            for dst, src in ((bq_sb, bq), (bk_sb, bk)):
                for g in range(2):
                    sp.dma_start(dst[:, g:g + 1], src[2 * g:2 * g + 2, :].rearrange("h (d o) -> (h d) o", o=1)).then_inc(s_w, 16)
            sp.dma_start(bv_sb[:, :], bv.rearrange("h d -> (h d)").partition_broadcast(P)).then_inc(s_w, 16)
            sp.dma_start(bf_sb[:, :], bf.partition_broadcast(P)).then_inc(s_w, 16)
            sp.dma_start(bout[:, :], b_out.partition_broadcast(P)).then_inc(s_w, 16)
        n_w = 16 * (1 + 3 * H1 + 1 + 4 + 3)

        @block.gpsimd
        def _(pool):
            pool.wait_ge(s_ids, 16)
            for t in range(NT):
                pool.indirect_dma_start(rows[:, t, :], None, emb,
                                        bass.IndirectOffsetOnAxis(ap=ids_sb[:, t:t + 1], axis=0)).then_inc(s_gather, 16)
            pool.wait_ge(s_gather, 16 * NT)

        @block.vector
        def _(dve):
            dve.wait_ge(s_w, n_w)
            dve.wait_ge(s_gather, 16 * NT)
            with dve.Fori(0, B) as b:
                dve_links = Count(dve, s_c, b * N_LINKS1)
                nc.vector.tensor_tensor(x[:, :, :], rows[:, ds(b * T, T), :], pos_sb[:, :, :], ALU.add).then_inc(s_x, 1)
                for t in range(T // 2):
                    dve.wait_ge(s_vp, b * n_dve + t + 1)
                    nc.vector.tensor_tensor(
                        v[:, 2 * t:2 * t + 2, :],
                        work[(first("v") + t) % nb][:, :].rearrange("p (a d) -> p a d", a=2),
                        bv_sb[:, :].rearrange("p (o d) -> p o d", o=1).to_broadcast([P, 2, D]),
                        ALU.add).then_inc(s_v, 1)
                dve.wait_ge(s_v, b * n_dve + T // 2)

                def head_max(h):
                    for t in range(T):
                        k = h * T + t
                        dve.wait_ge(s_score, b * H1 * T + k + 1)
                        nc.vector.reduce_max(mx[:, t:t + 1], score[k % 2][:, :], AX).then_inc(s_mx, 1)
                        dve.wait_ge(s_mx, b * H1 * T + k + 1)
                        nc.vector.tensor_scalar(nmx[:, h % 2, t:t + 1], mx[:, t:t + 1], -0.25, None, ALU.mult).then_inc(s_max, 1)

                def head_values(h):
                    dve.wait_ge(s_exp, b * H1 * T + (h + 1) * T)
                    dve_links.link(nc.vector.reciprocal(rsum[:, :], ssum[:, h % 2, :]))
                    nc.vector.tensor_tensor(
                        vs[:, h % 2, :, :], v[:, :, h * DH:(h + 1) * DH],
                        rsum[:, :].rearrange("p (t o) -> p t o", o=1).to_broadcast([P, T, DH]), ALU.mult).then_inc(s_vs, 1)

                def head_z(h):
                    dve.wait_ge(s_z, b * H1 + h + 1)
                    nc.vector.tensor_tensor(z[:, :, h * DH:(h + 1) * DH], zp[:, :].rearrange("p (t d) -> p t d", t=T),
                                            x[:, :, h * DH:(h + 1) * DH], ALU.add).then_inc(s_zread, 1)

                for h in range(H1):
                    head_max(h)
                    if h >= 1:
                        head_z(h - 1)
                    head_values(h)
                head_z(H1 - 1)
                dve.wait_ge(s_zread, (b + 1) * H1)

                def norm(i, src, dst, done):
                    def root(last):
                        last.then_inc(s_var, 1)
                        dve.wait_ge(s_root, b * 3 + i + 1)
                    layernorm_rows(nc, dve_links.link, done, src, dst, T, stats, mv, rstd, root, lambda: nc.vector.tensor_copy(rstd[:, 0:1], stats[:, T - 1, 0:1]))

                norm(0, z, z, lambda last: last.then_inc(s_zz, 1))
                dve.wait_ge(s_zz, b * 3 + 1)
                dve_links.link(nc.vector.tensor_tensor(
                    v[:, :, :], z[:, :, :], bf_sb[:, :].rearrange("p (o d) -> p o d", o=1).to_broadcast([P, T, D]), ALU.add))
                for t in range(T // 2):
                    dve.wait_ge(s_vp, b * n_dve + T // 2 + t + 1)
                    nc.vector.tensor_tensor(v[:, 2 * t:2 * t + 2, :], v[:, 2 * t:2 * t + 2, :],
                                            work[(first("ff") + t) % nb][:, :].rearrange("p (a d) -> p a d", a=2),
                                            ALU.add).then_inc(s_v, 1)
                dve.wait_ge(s_v, b * n_dve + T)
                norm(1, v, z, lambda last: last.then_inc(s_zz, 1))
                dve.wait_ge(s_zz, b * 3 + 2)
                nc.vector.tensor_tensor(rows[:, ds(b * T, T), :], z[:, :, :],
                                        bout[:, :].rearrange("p (o d) -> p o d", o=1).to_broadcast([P, T, D]), ALU.add)
                norm(2, z, z, lambda last: last.then_inc(s_zz, 1))
                dve.wait_ge(s_xT, (b + 1) * n_act)
                assert dve_links.n == N_LINKS1, dve_links.n

        @block.scalar
        def _(act):
            act.wait_ge(s_w, n_w)
            with act.Fori(0, B) as b:
                def empty(j, dst, func=ACT.Copy, **kw):
                    act.wait_ge(s_tr, b * n_act + done_before(j, "act") + 1)
                    nc.scalar.activation(dst, work[j % nb][:, :], func, **kw).then_inc(s_xT, 1)

                for j, (name, g, h, who) in enumerate(jobs[:first("zT")]):
                    half = slice(h * HB, (h + 1) * HB)
                    if name == "xT":
                        empty(j, xT[:, g, half])
                    elif name == "q":
                        empty(j, qT[:, g, half], ACT.Identity, bias=bq_sb[:, g:g + 1])
                    elif name == "k":
                        empty(j, kT[:, g, half], ACT.Identity, bias=bk_sb[:, g:g + 1])
                for h in range(H1):
                    if h >= 2:
                        act.wait_ge(s_z, b * H1 + h - 1)
                    for t in range(T):
                        k = h * T + t
                        act.wait_ge(s_max, b * H1 * T + k + 1)
                        nc.scalar.activation(probs[:, h % 2, t, :], score[k % 2][:, :], ACT.Exp,
                                             bias=nmx[:, h % 2, t:t + 1], scale=0.25,
                                             accum_out=ssum[:, h % 2, t:t + 1]).then_inc(s_exp, 1)

                def root(i):
                    act.wait_ge(s_var, b * 3 + i + 1)
                    nc.scalar.activation(rstd[:, :], mv[:, :, 1], ACT.Sqrt, bias=keep.eps[:, :]).then_inc(s_root, 1)

                root(0)
                for j, (name, g, h, who) in enumerate(jobs):
                    half = slice(h * HB, (h + 1) * HB)
                    if name == "zT":
                        empty(j, xT[:, g, half], ACT.Relu)
                root(1)
                root(2)
                for j, (name, g, h, who) in enumerate(jobs):
                    if name == "hT":
                        empty(j, hT[:, g, ds(b * S + h * HB, HB)])

        @block.tensor
        def _(pe):
            pe.wait_ge(s_w, n_w)
            with pe.Fori(0, B) as b:
                def bank(j):
                    k = j - nb
                    if k >= 0:
                        who = jobs[k][3]
                        pe.wait_ge(s_xT if who == "act" else s_v,
                                   b * (n_act if who == "act" else n_dve) + done_before(k, who) + 1)
                    return work[j % nb]

                def full(j, last):
                    last.then_inc(s_tr if jobs[j][3] == "act" else s_vp, 1)

                def transposes(j, src, c, h):
                    w = bank(j)
                    for i in range(4):
                        last = nc.tensor.transpose(w[:, i * P:(i + 1) * P],
                                                   src[:, 4 * h + i, c * P:(c + 1) * P], keep.ident[:, :])
                    full(j, last)

                pe.wait_ge(s_x, b + 1)
                pe.wait_ge(s_xT, b * n_act)
                for j, (name, g, h, who) in enumerate(jobs[:first("zT")]):
                    if name == "xT":
                        transposes(j, x, g, h)
                    elif name in "qk":
                        pe.wait_ge(s_xT, b * n_act + 2 * KC)
                        w = bank(j)
                        for c in range(KC):
                            last = nc.tensor.matmul(w[:, :], (wq_sb if name == "q" else wk_sb)[:, c, g * P:(g + 1) * P],
                                                    xT[:, c, h * HB:(h + 1) * HB], start=(c == 0), stop=(c == KC - 1))
                        full(j, last)
                    else:
                        w = bank(j)
                        for a in range(2):
                            for c in range(KC):
                                t = 2 * g + a
                                last = nc.tensor.matmul(w[:, a * D:(a + 1) * D], xT[:, c, t * P:(t + 1) * P],
                                                        wv_sb[:, c, :], start=(c == 0), stop=(c == KC - 1))
                        full(j, last)
                pe.wait_ge(s_xT, b * n_act + 2 * KC + 8)

                def scores(h):
                    g, o = h // 2, DH * (h % 2)
                    for t in range(T):
                        k = h * T + t
                        if k >= 2:
                            pe.wait_ge(s_exp, b * H1 * T + k - 1)
                        for n in range(2):
                            last = nc.tensor.matmul(score[k % 2][:, n * HB:(n + 1) * HB], kT[o:o + DH, g, t * P:(t + 1) * P],
                                                    qT[o:o + DH, g, n * HB:(n + 1) * HB], start=True, stop=True)
                        last.then_inc(s_score, 1)

                def products(h):
                    pe.wait_ge(s_vs, b * H1 + h + 1)
                    pe.wait_ge(s_zread, b * H1 + h)
                    for s in range(T):
                        for t in range(T):
                            last = nc.tensor.matmul(zp[:, s * DH:(s + 1) * DH], probs[:, h % 2, t, s * P:(s + 1) * P],
                                                    vs[:, h % 2, t, :], start=(t == 0), stop=(t == T - 1))
                    last.then_inc(s_z, 1)

                for h in range(H1):
                    scores(h)
                    if h >= 1:
                        products(h - 1)
                products(H1 - 1)
                pe.wait_ge(s_zz, b * 3 + 1)
                for j, (name, g, h, who) in enumerate(jobs):
                    if name == "zT":
                        transposes(j, z, g, h)
                    elif name == "ff":
                        if g == 0:
                            pe.wait_ge(s_xT, b * n_act + 2 * KC + 8 + 2 * KC)
                        w = bank(j)
                        for a in range(2):
                            for c in range(KC):
                                t = 2 * g + a
                                last = nc.tensor.matmul(w[:, a * D:(a + 1) * D], xT[:, c, t * P:(t + 1) * P],
                                                        wf_sb[:, c, :], start=(c == 0), stop=(c == KC - 1))
                        full(j, last)
                pe.wait_ge(s_zz, b * 3 + 3)
                for j, (name, g, h, who) in enumerate(jobs):
                    if name == "hT":
                        transposes(j, z, g, h)


N_LINKS1 = H1 + 3 * 2 + 1


PER, RISE = 5, 2
BLOCKS = (TMAX // RISE)
TAIL = BLOCKS * PER
BODY = S - TAIL


def hinge_blocks():
    out = []
    l = 1
    while True:
        a0 = next((a for a in range(BLOCKS) if 0.61 * PER * (a + 1) + 0.3 > RISE * a + l), BLOCKS)
        a1 = (TMAX - 1 - l) // RISE
        if a0 > a1:
            return out
        out.append((l, a0, a1 + 1))
        l += 1


HINGES = hinge_blocks()
N_RELU = 4
POOL = [n for n in range(1, 18) if n % 3]
N_POOL = len(POOL)
CHECK_AT = 2
GROUPS = T
RING = 4
NBANK = 6
SLOTS = 4


def cope_tables():
    import numpy as np
    low = RISE * (np.arange(TAIL) // PER)
    most = np.full(TAIL, 1e30, np.float32)
    for a in range(BLOCKS):
        covered = max((l for l, a0, a1 in HINGES if a0 <= a < a1), default=0)
        if RISE * a + covered < TMAX - 1:
            most[a * PER:(a + 1) * PER] = covered + 1
    return np.stack([(0.5 * (np.arange(TAIL) + 1) - low).astype(np.float32), most])


def cope_stage(nc, keep, a, saved):
    with ExitStack() as ctx:
        def sb(name, shape, dt=F32):
            return ctx.enter_context(nc.sbuf_tensor(name, shape, dt))

        def sem(name):
            return ctx.enter_context(nc.semaphore(name))

        rows, hT, ident = keep.rows, keep.hT, keep.ident
        w_in = sb("w_in", [P, 3, KC, P])
        wout = [sb(f"wout{s}", [P, D]) for s in range(SLOTS)]
        pos = sb("pos2", [P, TMAX])
        zero, lack = sb("zero", [P, 1]), sb("lack", [P, 1])
        found = sb("found", [P, 3])
        q = [sb(f"q{s}", [P, S]) for s in range(SLOTS)]
        k = [sb(f"k{s}", [P, S]) for s in range(SLOTS)]
        vT = sb("vT", [P, S])
        v1 = [sb(f"v1_{s}", [P, T, P]) for s in range(SLOTS)]
        ex = [sb(f"ex{i}", [P, S]) for i in range(RING)]
        nsum = sb("nsum", [P, S])
        rcol = sb("rcol", [P, T])
        pick = sb("pick", [P, 1])
        gate = sb("gate", [P, T, TAIL])
        above = sb("above_low", [P, T, TAIL])
        f = [sb(f"f{i}", [P, T, TAIL]) for i in range(2)]
        relu = [sb(f"relu{i}", [P, T * PER * max(a1 - a0 for l, a0, a1 in HINGES[i::N_RELU])]) for i in range(N_RELU)]
        pieces = sb("pieces", [P, T, TAIL])
        table = sb("table", [P, 2, TAIL])
        carry = sb("carry", [P, T, TAIL], mybir.dt.bfloat16)
        over = sb("over", [P, T, TAIL], mybir.dt.bfloat16)
        breach = sb("breach", [P, 2, 3])
        ent = [sb(f"ent{i}", [P, T, TMAX]) for i in range(2)]
        slope, bend = sb("slope", [P, T, TMAX]), sb("bend", [P, T, TMAX])
        bmax, tmax = sb("bmax", [P, T, 2]), sb("tmax", [P, T])
        shift = [sb(f"shift{i}", [P, T]) for i in range(2)]
        bm = sb("bm", [P, T])
        nmax = [sb(f"nmax{i}", [P, T]) for i in range(2)]

        bank = [ctx.enter_context(nc.psum_tensor(f"bank{i}", [P, HB], F32)) for i in range(NBANK)]
        pv = ctx.enter_context(nc.psum_tensor("pv", [P, S], F32))

        s_const, s_w = sem("consts_in"), sem("pair_weights_in")
        s_wo = sem("output_weights_in")
        s_set, s_ones = sem("memsets_done"), sem("ones_set")
        s_fa, s_fd = sem("bank_full_for_act"), sem("bank_full_for_dve")
        s_ra, s_rd = sem("bank_read_by_act"), sem("bank_read_by_dve")
        s_zero = sem("shift_row_zeroed")
        s_p, s_over, s_seen, s_relu = sem("p_ready"), sem("over_ready"), sem("p_checked"), sem("relu_ready")
        s_part, s_padd, s_dadd = sem("hinge_for_pool"), sem("hinge_added_by_pool"), sem("hinge_added_by_dve")
        s_gate = sem("gate_used")
        s_m, s_xt, s_pvm, s_copied = sem("max_known"), sem("tail_exp_ready"), sem("product_done"), sem("products_copied")
        s_saved = sem("rows_saved")
        s_c, s_rev = sem("dve_chain2"), sem("breach_known")

        def tail_jobs(s):
            return [("tail", s, i, "act") for i in range(3)] + [("ent", s, 0, "act")]

        def pair_jobs(s):
            return [[("pq", s, h, "act") for h in range(2)], [("pk", s, h, "act") for h in range(2)],
                    [("pv", s, h, "act") for h in range(2)], [("vtr", s, h, "act") for h in range(2)]]

        def body_jobs(m):
            first = [0, 2, 5, 8, 11, 14, 16, 16, 16]
            return range(first[m], first[m + 1])

        def slot_plan(s):
            nxt, nnxt = (s + 1) % SLOTS, (s + 2) % SLOTS
            plan = [[("row", s, h, "act") for h in range(2)] + [("tt", s, i, "act") for i in range(2)]
                    + [("body", nxt, i, "dve") for i in body_jobs(0)]]
            for m in range(1, GROUPS):
                g = [("sT", s, 2 * m + h, "act") for h in range(2)]
                if m == 1:
                    g += [("tt", s, i, "act") for i in (2, 3)]
                else:
                    g += [("PV", s, m - 2)]
                g += [("body", nxt, i, "dve") for i in body_jobs(m)]
                if s % 2 == 0 and 1 <= m <= 4:
                    g += pair_jobs(nnxt)[m - 1]
                if m == GROUPS - 1:
                    tails = tail_jobs(nnxt)
                    g += tails[:3] + [("PV", s, m - 1), ("PV", s, m)] + tails[3:]
                    g += [("sum", s, 0, "dve")] + [("out", s, i, "dve") for i in range(4)]
                plan.append(g)
            return plan

        pro_plan = [[j for js in pair_jobs(0) for j in js] + tail_jobs(0)]
        pro_plan += [[("body", 0, i, "dve") for i in body_jobs(m)] for m in range(GROUPS)]
        pro_plan[5][0:0] = tail_jobs(1)
        body_plan = [slot_plan(s) for s in range(SLOTS)]

        def is_job(x):
            return x[0] != "PV"

        pro = [j for g in pro_plan for j in g]
        turn = [j for p in body_plan for g in p for j in g if is_job(j)]
        pad = -len(turn) % NBANK
        index = {}
        counts = {"act": 0, "dve": 0}
        last_of_bank = {}
        info = {}

        def place(part, jobs, first):
            n = {"act": 0, "dve": 0}
            pos = first
            for i, j in enumerate(jobs):
                n[j[3]] += 1
                info[(part, j)] = (pos % NBANK, n[j[3]], last_of_bank.get(pos % NBANK))
                last_of_bank[pos % NBANK] = (part, j)
                pos += 1
                if part == "turn" and i == len(jobs) // 2:
                    pos += pad
            return n

        n_pro = place("pro", pro, -len(pro))
        n_turn = place("turn", turn, 0)
        assert [j[3] for j in pro[-NBANK:]] == [j[3] for j in turn[-NBANK:]]

        class Place:

            def __init__(self, eng, part, it):
                self.eng, self.part, self.it = eng, part, it

            def at(self, who, n, part=None):
                part = part or self.part
                if part == "pro":
                    return n
                return n_pro[who] + self.it * n_turn[who] + n

            def job(self, j):
                return info[(self.part, j)]

            def head(self, sem, s, per, n):
                n += s * per + (T if sem is s_pvm else 1 if sem in (s_copied, s_zero) else 0)
                assert n > 0
                self.eng.wait_ge(sem, n if self.part == "pro" else self.it * (SLOTS * per) + n)

        def pe_take(w, j):
            b, _, before = w.job(j)
            if before is None and w.part == "pro":
                return bank[b]
            part, prev = before
            who, n = prev[3], info[before][1]
            if part == w.part:
                w.eng.wait_ge(s_ra if who == "act" else s_rd, w.at(who, n))
            else:
                total = (n_pro if part == "pro" else n_turn)[who]
                w.eng.wait_ge(s_ra if who == "act" else s_rd, w.at(who, n - total))
            return bank[b]

        def pe_need(w, part, j):
            who, n = j[3], info[(part, j)][1]
            w.eng.wait_ge(s_ra if who == "act" else s_rd, w.at(who, n, part))

        def pe_job(w, j, b_of):
            kind, s, i, who = j
            ps = pe_take(w, j)
            if kind in ("pq", "pk", "pv"):
                x = ("pq", "pk", "pv").index(kind)
                for c in range(KC):
                    last = nc.tensor.matmul(ps[:, :], w_in[:, x, c, :], hT[:, c, ds(b_of * S + i * HB, HB)],
                                            start=(c == 0), stop=(c == KC - 1))
            elif kind == "vtr":
                pe_need(w, w.part, ("pv", s, 1, "act"))
                for n in range(4):
                    last = nc.tensor.transpose(ps[:, n * P:(n + 1) * P], vT[:, (4 * i + n) * P:(4 * i + n + 1) * P], ident[:, :])
            elif kind == "tail":
                for n, t in enumerate(range(3 * i, min(3 * i + 3, T))):
                    last = nc.tensor.matmul(ps[:, n * TAIL:(n + 1) * TAIL], q[s][:, t * P:(t + 1) * P], k[s][:, 0:TAIL],
                                            start=True, stop=True)
            elif kind == "ent":
                for t in range(T):
                    last = nc.tensor.matmul(ps[:, t * TMAX:(t + 1) * TMAX], q[s][:, t * P:(t + 1) * P], pos[:, :],
                                            start=True, stop=True)
            elif kind == "body":
                t, h = divmod(i, 2)
                last = nc.tensor.matmul(ps[:, 0:BODY // 2], q[s][:, t * P:(t + 1) * P],
                                        k[s][:, TAIL + h * (BODY // 2):TAIL + (h + 1) * (BODY // 2)], start=True, stop=True)
            elif kind == "row":
                for n in range(4):
                    last = nc.tensor.matmul(ps[DH:DH + 1, n * P:(n + 1) * P], shift[s % 2][:, 4 * i + n:4 * i + n + 1],
                                            ident[:, :], start=True, stop=True)
            elif kind == "tt":
                part, half = divmod(i, 2)
                c0, c1 = (0, P) if part == 0 else (P, TAIL)
                for n in range(4):
                    last = nc.tensor.transpose(ps[0:c1 - c0, n * P:(n + 1) * P], f[s % 2][:, 4 * half + n, c0:c1], ident[:, :])
            elif kind == "sT":
                m, h = divmod(i, 2)
                last = nc.tensor.matmul(ps[:, :], k[s][:, m * P:(m + 1) * P], q[s][:, h * HB:(h + 1) * HB], start=True, stop=True)
            elif kind == "sum":
                for t in range(T):
                    last = nc.tensor.matmul(ps[:, t:t + 1], nsum[:, t * P:(t + 1) * P], pick[:, :], start=True, stop=True)
            elif kind == "out":
                for n in range(2):
                    t = 2 * i + n
                    last = nc.tensor.matmul(ps[:, n * D:(n + 1) * D], nsum[:, t * P:(t + 1) * P], wout[s][:, :], start=True, stop=True)
            last.then_inc(s_fa if who == "act" else s_fd, 1)
            return last

        block = ctx.enter_context(nc.Block())

        def pair_place(it, s):
            if s == 0:
                n = it * 2 + 1
            else:
                n = ((it + 1) % (NPAIR // 2)) * 2
            return n // (H2 // 2), n % (H2 // 2)

        @block.tensor
        def _(pe):
            pe.wait_ge(s_const, 16 * 3)
            pe.wait_ge(s_set, N_SET2)
            w = Place(pe, "pro", 0)
            for g in pro_plan:
                for j in g:
                    if j[0] == "pq" and j[2] == 0:
                        pe.wait_ge(s_w, 48)
                    if j[0] == "tail" and j[2] == 0:
                        pe_need(w, "pro", ("pk", 0, 1, "act"))
                    pe_job(w, j, 0)
            with pe.Fori(0, NPAIR // 2) as it:
                w = Place(pe, "turn", it)
                for s in range(SLOTS):
                    for gi, g in enumerate(body_plan[s]):
                        for j in g:
                            if j[0] == "PV":
                                m = j[2]
                                pe_need(w, "turn", ("sT", s, 2 * m + 1, "act") if m > 1 else ("tt", s, 2 * m + 1, "act"))
                                if m == 0:
                                    w.head(s_copied, s, 1, 0)
                                for h in range(2):
                                    last = nc.tensor.matmul(pv[:, h * HB:(h + 1) * HB], v1[s][:, m, :], ex[m % RING][:, h * HB:(h + 1) * HB],
                                                            start=(m == 0), stop=(m == T - 1))
                                last.then_inc(s_pvm, 1)
                                continue
                            if j[0] == "row" and j[2] == 0:
                                w.head(s_m, s, 1, 1)
                            if j[0] == "tt" and j[2] == 0:
                                w.head(s_xt, s, 1, 1)
                            if j[0] == "sT" and j[2] == 2:
                                pe_need(w, "turn", ("row", s, 1, "act"))
                            if j[0] == "pq" and j[2] == 0:
                                pe.wait_ge(s_w, it * (2 * 48) + 48 * (2 + s // 2))
                            if j[0] == "tail" and j[2] == 0:
                                if s % 2 == 0:
                                    pe_need(w, "turn", ("pk", (s + 2) % SLOTS, 1, "act"))
                                w.head(s_zero, s, 1, 0)
                            if j[0] == "out" and j[2] == 0:
                                pe.wait_ge(s_wo, it * (2 * 32) + 32 * (1 + s // 2))
                            if j[0] == "sum":
                                w.head(s_copied, s, 1, 1)
                            b_of = pe.snap(pair_place(it, s)[0]) if j[0] in ("pq", "pk", "pv") else 0
                            pe_job(w, j, b_of)

        def act_read(w, j):
            b, n, _ = w.job(j)
            w.eng.wait_ge(s_fa, w.at("act", n))
            return bank[b]

        def act_job(w, j):
            kind, s, i, _ = j
            ps = act_read(w, j)
            half = slice(i % 2 * HB, (i % 2 + 1) * HB)
            if kind in ("pq", "pk"):
                dst, scale = (q, 1.0) if kind == "pq" else (k, DH ** -0.5)
                for e in range(2):
                    last = nc.scalar.activation(dst[s + e][0:DH, half], ps[e * DH:(e + 1) * DH, :], ACT.Copy, scale=scale)
            elif kind == "pv":
                last = nc.scalar.activation(vT[:, half], ps[:, :], ACT.Copy)
            elif kind == "vtr":
                for e in range(2):
                    last = nc.scalar.activation(v1[s + e][:, 4 * i:4 * i + 4, 0:DH],
                                                ps[:, :].rearrange("p (n d) -> p n d", n=4)[:, :, e * DH:(e + 1) * DH], ACT.Copy)
            elif kind == "tail":
                t0, t1 = 3 * i, min(3 * i + 3, T)
                src = ps[:, 0:(t1 - t0) * TAIL].rearrange("p (t c) -> p t c", t=t1 - t0)
                nc.scalar.activation(gate[:, t0:t1, :], src, ACT.Tanh, scale=0.5)
                last = nc.scalar.activation(f[s % 2][:, t0:t1, :], src, ACT.Copy)
            elif kind == "ent":
                last = nc.scalar.activation(ent[s % 2][:, :, :], ps[:, :].rearrange("p (t c) -> p t c", t=T), ACT.Copy)
            elif kind == "row":
                last = nc.scalar.activation(q[s][DH:DH + 1, half], ps[DH:DH + 1, :], ACT.Copy)
            elif kind == "tt":
                if i < 2:
                    last = nc.scalar.activation(ex[0][:, half], ps[:, :], ACT.Copy)
                else:
                    last = nc.scalar.activation(ex[1][0:TAIL - P, half], ps[0:TAIL - P, :], ACT.Copy)
            elif kind == "sT":
                m = i // 2
                last = nc.scalar.activation(ex[m % RING][:, half], ps[:, :], ACT.Exp)
            last.then_inc(s_ra, 1)

        def groups_of_hinges(m):
            cuts = [0, 0, 2, 5, 8, 12, 17, len(HINGES), len(HINGES)]
            return range(cuts[m], cuts[m + 1])

        N_PART = N_POOL + 1
        OWN = [n for n in range(1, len(HINGES)) if n not in POOL]
        N_DVE = len(OWN)

        def buffer_free(w, s, n):
            p, before = n - N_RELU, 0
            if p < 0:
                if w.part == "pro":
                    return
                before = 1
                p = max(x for x in range(len(HINGES)) if x % N_RELU == n % N_RELU)
            if p == 0:
                w.head(s_part, s - before, N_PART, 1)
            elif p in POOL:
                w.head(s_padd, s - before, N_POOL, POOL.index(p) + 1)
            else:
                w.head(s_dadd, s - before, N_DVE, OWN.index(p) + 1)

        def act_hinges(w, s, m):
            for n in groups_of_hinges(m):
                l, a0, a1 = HINGES[n]
                if n == 0:
                    w.head(s_p, s, 1, 1)
                buffer_free(w, s, n)
                cols = (a1 - a0) * PER
                nc.scalar.activation(relu[n % N_RELU][:, 0:T * cols].rearrange("p (t c) -> p t c", t=T),
                                     above[:, :, a0 * PER:a1 * PER], ACT.Relu, bias=keep.minus[:, l:l + 1]).then_inc(s_relu, 1)

        def act_check(w, s):
            w.head(s_over, s, 1, 1)
            w.head(s_gate, s, 1, 1)
            nc.scalar.activation(gate[:, :, :], above[:, :, :], ACT.Relu, scale=-1.0, accum_out=breach[:, s % 2, 0:1]).then_inc(s_seen, 1)
            w.head(s_seen, s, 3, 1)
            nc.scalar.activation(gate[:, :, :], over[:, :, :], ACT.Relu, accum_out=breach[:, s % 2, 1:2]).then_inc(s_seen, 1)
            w.head(s_seen, s, 3, 2)
            nc.scalar.activation(gate[:, :, 0], above[:, :, TAIL - 1], ACT.Relu, scale=-1.0, bias=lack[:, :],
                                 accum_out=breach[:, s % 2, 2:3]).then_inc(s_seen, 1)

        def tail_exp(w, s):
            w.head(s_m, s, 1, 1)
            for t in range(T):
                last = nc.scalar.activation(f[s % 2][:, t, :], f[s % 2][:, t, :], ACT.Exp, bias=nmax[s % 2][:, t:t + 1])
            last.then_inc(s_xt, 1)

        @block.scalar
        def _(act):
            act.wait_ge(s_set, N_SET2)
            w = Place(act, "pro", 0)
            for gi, g in enumerate(pro_plan):
                for j in g:
                    if j[3] == "act":
                        if j[0] == "tail" and j[1] == 1 and j[2] == 0:
                            act.wait_ge(s_gate, 1)
                            act.wait_ge(s_seen, 3)
                        act_job(w, j)
                if gi:
                    act_hinges(w, 0, gi - 1)
                if gi - 1 == CHECK_AT:
                    act_check(w, 0)
            tail_exp(w, 0)
            with act.Fori(0, NPAIR // 2) as it:
                w = Place(act, "turn", it)
                for s in range(SLOTS):
                    for gi, g in enumerate(body_plan[s]):
                        for j in g:
                            if j[0] == "PV" or j[3] != "act":
                                continue
                            if j[0] == "tt" and j[2] in (0, 2):
                                w.head(s_pvm, s, T, j[2] // 2 + 1 - RING)
                            if j[0] == "sT" and j[2] % 2 == 0:
                                m = j[2] // 2
                                w.head(s_pvm, s, T, m + 1 - RING)
                            if j[0] == "tail" and j[2] == 0:
                                w.head(s_gate, s, 1, 2)
                                w.head(s_seen, s, 3, 6)
                            if j[0] == "tt" and j[2] == 2:
                                w.eng.wait_ge(s_ra, w.at("act", w.job(("sT", s, 3, "act"))[1]))
                            act_job(w, j)
                            if j[0] == "tail" and j[2] == 2:
                                w.head(s_pvm, s, T, T)
                                n = info[("turn", ("out", (s - 1) % SLOTS, 3, "dve"))][1]
                                act.wait_ge(s_rd, w.at("dve", n if s else n - n_turn["dve"]))
                                nc.scalar.activation(nsum[:, :], pv[:, :], ACT.Copy).then_inc(s_copied, 1)
                        act_hinges(w, s + 1, gi)
                        if gi == CHECK_AT:
                            act_check(w, s + 1)
                    tail_exp(w, s + 1)

        def low_of(tab, a0, a1, l):
            first = RISE * a0 + l
            return tab[:, :, first:RISE * (a1 - 1) + l + 1:RISE].rearrange("p t (a o) -> p t a o", o=1)\
                .to_broadcast([P, T, a1 - a0, PER])

        def blocks(ap, a0, a1):
            return ap[:, :, a0 * PER:a1 * PER].rearrange("p t (a r) -> p t a r", r=PER)

        def dve_first(w, s, part, link):
            e = s % 2
            if part == 0:
                w.eng.wait_ge(s_ra, after_ent(w, s))
                link(nc.vector.tensor_tensor(slope[:, :, 0:TMAX - 1], ent[e][:, :, 1:TMAX], ent[e][:, :, 0:TMAX - 1], ALU.subtract))
                if w.part == "turn":
                    w.head(s_seen, s, 3, 0)
                    w.head(s_over, s, 1, 0)
                link(nc.vector.tensor_tensor_scan(above[:, :, :].rearrange("p t c -> p (t c)"),
                                                  carry[:, :, :].rearrange("p t c -> p (t c)"),
                                                  gate[:, :, :].rearrange("p t c -> p (t c)"), 0.0, ALU.mult, ALU.add))
                nc.vector.scalar_tensor_tensor(above[:, :, :], above[:, :, :], 0.5,
                                               table[:, 0:1, :].to_broadcast([P, T, TAIL]), ALU.mult, ALU.add).then_inc(s_p, 1)
                link(nc.vector.tensor_tensor(bend[:, :, 1:TMAX], slope[:, :, 1:TMAX], slope[:, :, 0:TMAX - 1], ALU.subtract))
                w.head(s_p, s, 1, 1)
            else:
                link(nc.vector.tensor_tensor(blocks(gate, 0, BLOCKS), blocks(above, 0, BLOCKS), low_of(slope, 0, BLOCKS, 0), ALU.mult))
                nc.vector.tensor_tensor(f[e][:, :, :], f[e][:, :, :], gate[:, :, :], ALU.add).then_inc(s_gate, 1)
                w.head(s_gate, s, 1, 1)
                link(nc.vector.tensor_tensor(blocks(f[e], 0, BLOCKS), blocks(f[e], 0, BLOCKS), low_of(ent[e], 0, BLOCKS, 0), ALU.add))

        N_FIRST = 5

        def after_ent(w, s):
            if w.part == "pro":
                return w.at("act", info[("pro", ("ent", 0, 0, "act"))][1])
            if s == 1:
                n = info[("turn", ("ent", 1, 0, "act"))][1]
                return w.at("act", n - n_turn["act"])
            return w.at("act", info[("turn", ("ent", s % SLOTS, 0, "act"))][1])

        def dve_hinges(w, s, m, link):
            for n in groups_of_hinges(m):
                l, a0, a1 = HINGES[n]
                cols = (a1 - a0) * PER
                w.head(s_relu, s, len(HINGES), n + 1)
                line = relu[n % N_RELU][:, 0:T * cols]
                by_block = line.rearrange("p (t a r) -> p t a r", t=T, r=PER)
                if n not in OWN:
                    nc.vector.tensor_tensor(by_block if n else blocks(pieces, a0, a1), by_block,
                                            low_of(bend, a0, a1, l), ALU.mult).then_inc(s_part, 1)
                else:
                    link(nc.vector.tensor_tensor(by_block, by_block, low_of(bend, a0, a1, l), ALU.mult))
                    nc.vector.tensor_tensor(f[s % 2][:, :, a0 * PER:a1 * PER], f[s % 2][:, :, a0 * PER:a1 * PER],
                                            line.rearrange("p (t c) -> p t c", t=T), ALU.add).then_inc(s_dadd, 1)
                    w.head(s_dadd, s, N_DVE, OWN.index(n) + 1)

        def dve_full(w, j):
            b, n, _ = w.job(j)
            w.eng.wait_ge(s_fd, w.at("dve", n))
            return bank[b]

        def dve_job(w, j, rows_at=None):
            kind, s, i, _ = j
            ps = dve_full(w, j)
            if kind == "body":
                t, h = divmod(i, 2)
                last = nc.vector.reduce_max(bmax[:, t, h:h + 1], ps[:, 0:BODY // 2], AX)
            elif kind == "sum":
                last = nc.vector.reciprocal(rcol[:, :], ps[:, 0:T])
            elif kind == "out":
                for n in range(2):
                    row = rows[:, ds(rows_at[n], 1), :].rearrange("p o d -> p (o d)")
                    last = nc.vector.scalar_tensor_tensor(row, ps[:, n * D:(n + 1) * D], rcol[:, 2 * i + n:2 * i + n + 1], row,
                                                          ALU.mult, ALU.add)
            last.then_inc(s_rd, 1)

        def dve_last(w, s, link):
            e = s % 2
            w.head(s_padd, s, N_POOL, N_POOL)
            link(nc.vector.tensor_tensor(f[e][:, :, :], f[e][:, :, :], pieces[:, :, :], ALU.add))
            w.head(s_seen, s, 3, 3)
            nc.vector.tensor_tensor(found[:, :], found[:, :], breach[:, e, :], ALU.add)
            link(nc.vector.tensor_reduce(tmax[:, :], f[e][:, :, :], AX, ALU.max))
            w.eng.wait_ge(s_rd, w.at("dve", w.job(("body", s % SLOTS, 2 * T - 1, "dve"))[1]))
            link(nc.vector.tensor_tensor(bm[:, :], bmax[:, :, 0], bmax[:, :, 1], ALU.max))
            link(nc.vector.tensor_tensor(bm[:, :], bm[:, :], ent[e][:, :, TMAX - 1], ALU.add))
            link(nc.vector.tensor_tensor(bm[:, :], bm[:, :], tmax[:, :], ALU.max))
            link(nc.vector.tensor_scalar(nmax[e][:, :], bm[:, :], -1.0, None, ALU.mult))
            nc.vector.tensor_tensor(shift[e][:, :], ent[e][:, :, TMAX - 1], bm[:, :], ALU.subtract).then_inc(s_m, 1)

        N_LAST = 6
        per_head = N_FIRST + N_DVE + N_LAST

        @block.vector
        def _(dve):
            for s in range(SLOTS):
                nc.vector.memset(q[s][DH:P, :], 0.0).then_inc(s_set, 1)
                nc.vector.memset(k[s][DH:P, :], 0.0).then_inc(s_ones, 1)
                nc.vector.memset(v1[s][:, :, DH:P], 1.0).then_inc(s_set, 1)
                nc.vector.memset(wout[s][DH:P, :], 0.0).then_inc(s_set, 1)
            for ap, val in ((zero[:, :], 0.0), (slope[:, :, TMAX - 1:TMAX], 0.0),
                            (found[:, :], 0.0), (pos[DH:P, :], 0.0),
                            (lack[:, :], float(TMAX - 1 - RISE * (BLOCKS - 1)))):
                nc.vector.memset(ap, val).then_inc(s_set, 1)
            nc.vector.memset(carry[:, :, :], 1.0).then_inc(s_ones, 1)
            nc.vector.memset(pick[:, :], 0.0).then_inc(s_ones, 1)
            dve.wait_ge(s_ones, SLOTS + 2)
            for s in range(SLOTS):
                nc.vector.memset(k[s][DH:DH + 1, :], 1.0).then_inc(s_set, 1)
            nc.vector.memset(pick[DH:DH + 1, :], 1.0).then_inc(s_set, 1)
            nc.vector.memset(carry[:, :, 0:1], 0.0).then_inc(s_set, 1)
            dve.wait_ge(s_const, 16 * 3)
            dve.wait_ge(s_set, N_SET2)
            w = Place(dve, "pro", 0)
            chain = Count(dve, s_c)
            for gi, g in enumerate(pro_plan):
                if gi:
                    for j in g:
                        if j[3] == "dve":
                            dve_job(w, j)
                    if gi <= 2:
                        dve_first(w, 0, gi - 1, chain.link)
                    dve_hinges(w, 0, gi - 1, chain.link)
            dve_last(w, 0, chain.link)
            assert chain.n == per_head, (chain.n, per_head)
            with dve.Fori(0, NPAIR // 2) as it:
                w = Place(dve, "turn", it)
                for s in range(SLOTS):
                    chain = Count(dve, s_c, it * (SLOTS * per_head) + (s + 1) * per_head)
                    for gi, g in enumerate(body_plan[s]):
                        if gi == 0:
                            dve_first(w, s + 1, 0, chain.link)
                        for j in g:
                            if j[0] == "body":
                                dve_job(w, j)
                        if gi == 1:
                            dve_first(w, s + 1, 1, chain.link)
                        dve_hinges(w, s + 1, gi, chain.link)
                        if gi == GROUPS - 2:
                            dve_last(w, s + 1, chain.link)
                    if s == 0:
                        dve.wait_ge(s_saved, 16)
                    for j in body_plan[s][-1]:
                        if j[0] == "sum":
                            dve_job(w, j)
                            w.eng.wait_ge(s_rd, w.at("dve", w.job(j)[1]))
                        elif j[0] == "out":
                            dve_job(w, j, [dve.snap(((it * 2 + s // 2) // (H2 // 2)) * T + 2 * j[2] + n) for n in range(2)])
            nc.vector.tensor_reduce(keep.excess[:, :], found[:, :], AX, ALU.max).then_inc(s_rev, 1)
            dve.wait_ge(s_rev, 1)

        @block.gpsimd
        def _(pool):
            def pool_hinges(w, s):
                w.head(s_p, s, 1, 1)
                if w.part == "turn":
                    w.head(s_seen, s, 3, 0)
                nc.gpsimd.tensor_tensor(over[:, :, :], above[:, :, :], table[:, 1:2, :].to_broadcast([P, T, TAIL]),
                                        ALU.subtract).then_inc(s_over, 1)
                for i, n in enumerate(POOL):
                    l, a0, a1 = HINGES[n]
                    w.head(s_part, s, N_PART, i + 2)
                    if i:
                        w.head(s_padd, s, N_POOL, i)
                    cols = slice(a0 * PER, a1 * PER)
                    nc.gpsimd.tensor_tensor(pieces[:, :, cols], pieces[:, :, cols],
                                            relu[n % N_RELU][:, 0:T * (a1 - a0) * PER].rearrange("p (t c) -> p t c", t=T),
                                            ALU.add).then_inc(s_padd, 1)

            pool.wait_ge(s_set, N_SET2)
            pool.wait_ge(s_const, 16 * 3)
            pool.sem_inc(s_zero, 1)
            pool.sem_inc(s_copied, 1)
            pool.sem_inc(s_pvm, T)
            pool_hinges(Place(pool, "pro", 0), 0)
            with pool.Fori(0, NPAIR // 2) as it:
                w = Place(pool, "turn", it)
                for s in range(SLOTS):
                    pool_hinges(w, s + 1)
                    pool.wait_ge(s_ra, w.at("act", info[("turn", ("sT", s, 2 * T - 1, "act"))][1]))
                    z = zero[DH:DH + 1, 0:1].to_broadcast([1, S])
                    nc.gpsimd.tensor_tensor(q[s][DH:DH + 1, :], z, z, ALU.add).then_inc(s_zero, 1)
                    w.head(s_zero, s, 1, 1)

        def weights_used(s):
            if s == 2:
                return info[("turn", ("pv", 2, 1, "act"))][1]
            return info[("pro", ("pv", 0, 1, "act"))][1] - n_pro["act"]

        @block.sync
        def _(sp):
            sp.dma_start(saved.rearrange("(t p) d -> p t d", p=P), rows[:, :, :]).then_inc(s_saved, 16)
            sp.dma_start(pos[0:DH, :], a["L0_attn_pos_emb"]).then_inc(s_const, 16)
            sp.dma_start(table[:, :, :].rearrange("p a c -> p (a c)"), a["tables"].rearrange("a c -> (a c)").partition_broadcast(P)).then_inc(s_const, 16)
            sp.dma_start(keep.minus[:, :], a["minus"].partition_broadcast(P)).then_inc(s_const, 16)
            wq_r = a["L0_attn_Wq"].rearrange("(c p) n -> p c n", p=P)
            wkv_r = a["L0_attn_Wkv"].rearrange("(c p) n -> p c n", p=P)

            def pair_weights(col):
                for x, src, c in ((0, wq_r, col), (1, wkv_r, col), (2, wkv_r, col + H2 * DH)):
                    sp.dma_start(w_in[:, x, :, :], src[:, :, ds(c, P)]).then_inc(s_w, 16)

            def out_weights(even, odd, s):
                for e, at in enumerate((even, odd)):
                    sp.dma_start(wout[s + e][0:DH, :], a["L0_attn_Wout"][ds(at, DH), :]).then_inc(s_wo, 16)

            pair_weights(0)
            out_weights(0, DH, 0)
            with sp.Fori(0, NPAIR // 2) as it:
                w = Place(sp, "turn", it)
                for s in (0, 2):
                    _, hp = pair_place(it, s)
                    col, odd = sp.snap(hp * P), sp.snap(hp * P + DH)
                    sp.wait_ge(s_ra, w.at("act", weights_used(s)))
                    pair_weights(col)
                    sp.wait_ge(s_ra, w.at("act", info[("turn", ("row", s, 1, "act"))][1]))
                    out_weights(col, odd, (s + 2) % SLOTS)
            sp.wait_ge(s_saved, 16)
            sp.wait_ge(s_wo, 32 * (NPAIR + 1))
            sp.wait_ge(s_w, 48 * (NPAIR + 1))


N_SET2 = 4 * SLOTS + 5 + 2


def verdict_stage(nc, keep):
    with ExitStack() as ctx:
        line = ctx.enter_context(nc.psum_tensor("line", [1, P], F32))
        low = ctx.enter_context(nc.sbuf_tensor("lowest", [1, 2], F32))
        s_line, s_low, s_is, s_flag = (ctx.enter_context(nc.semaphore(x)) for x in
                                       ("breach_in_line", "lowest_found", "breach_judged", "flag_set"))
        block = ctx.enter_context(nc.Block())

        @block.tensor
        def _(pe):
            nc.tensor.matmul(line[:, :], keep.excess[:, :], keep.ident[:, :], start=True, stop=True).then_inc(s_line, 1)

        @block.vector
        def _(dve):
            dve.wait_ge(s_line, 1)
            nc.vector.tensor_reduce(low[:, 0:1], line[:, :], AX, ALU.max).then_inc(s_low, 1)
            dve.wait_ge(s_low, 1)
            nc.vector.tensor_scalar(low[:, 1:2], low[:, 0:1], 0.0, None, ALU.is_gt).then_inc(s_is, 1)
            dve.wait_ge(s_is, 1)
            nc.vector.tensor_copy(keep.flag[:, :], low[:, 1:2]).then_inc(s_flag, 1)
            dve.wait_ge(s_flag, 1)


def general_cope_stage(nc, keep, a, saved):
    with ExitStack() as ctx:
        def sb(name, shape, dt=F32):
            return ctx.enter_context(nc.sbuf_tensor(name, shape, dt))

        def sem(name):
            return ctx.enter_context(nc.semaphore(name))

        rows, hT, ident = keep.rows, keep.hT, keep.ident
        w_in, wout = sb("gw_in", [P, 3, KC, P]), sb("gwout", [P, D])
        pos, number = sb("gpos", [DH, TMAX]), sb("gnumber", [P, TMAX])
        q, k = [sb(f"gq{e}", [DH, S]) for e in range(2)], [sb(f"gk{e}", [DH, S]) for e in range(2)]
        vT, v = sb("gvT", [P, S]), sb("gv", [P, T, P])
        qt, ent, slope = sb("gqt", [DH, P]), sb("gent", [P, TMAX]), sb("gslope", [P, TMAX])
        gate, p, f, part, ones = (sb(n, [P, S]) for n in ("ggate", "gp", "gf", "gpart", "gones"))
        prob, probT = sb("gprob", [P, S]), sb("gprobT", [P, T, P])
        top, ntop, total, recip = (sb(n, [P, 1]) for n in ("gtop", "gntop", "gtotal", "grecip"))
        o, oT = sb("go", [P, P]), sb("goT", [P, P])

        bank = [ctx.enter_context(nc.psum_tensor(f"gbank{i}", [P, HB], F32)) for i in range(8)]
        s_const, s_w, s_set = sem("g_consts_in"), sem("g_weights_in"), sem("g_set")
        s_pj, s_pjc, s_vt, s_vc = sem("g_projected"), sem("g_qkv_copied"), sem("g_v_turned"), sem("g_v_copied")
        s_qt, s_sc, s_cp, s_f, s_c = sem("g_q_tile"), sem("g_scores"), sem("g_scores_copied"), sem("g_max"), sem("g_dve_chain")
        s_ex, s_nr, s_tp, s_tc = sem("g_exp"), sem("g_normalised"), sem("g_probs_turned"), sem("g_probsT_copied")
        s_o, s_oc, s_at, s_ac = sem("g_product"), sem("g_product_copied"), sem("g_product_turned"), sem("g_productT_copied")
        s_y, s_add = sem("g_out"), sem("g_added")

        block = ctx.enter_context(nc.Block())
        PB = H2 // 2
        CHAIN = 5 + 3 * (TMAX - 1) + 3

        @block.sync
        def _(sp):
            flag = sp.value_load(keep.flag[0:1, 0:1], min_val=0, max_val=1)
            with sp.If(flag == 1):
                sp.dma_start(pos[:, :], a["L0_attn_pos_emb"]).then_inc(s_const, 16)
                sp.dma_start(number[:, :], a["number"].partition_broadcast(P)).then_inc(s_const, 16)
                sp.dma_start(rows[:, :, :], saved.rearrange("(t p) d -> p t d", p=P)).then_inc(s_const, 16)
                wq_r = a["L0_attn_Wq"].rearrange("(c p) n -> p c n", p=P)
                wkv_r = a["L0_attn_Wkv"].rearrange("(c p) n -> p c n", p=P)
                with sp.Fori(0, B) as b:
                    with sp.Fori(0, PB) as hp:
                        col = sp.snap(hp * P)
                        colv = sp.snap(hp * P + H2 * DH)
                        sp.wait_ge(s_add, (b * PB + hp) * T)
                        sp.dma_start(w_in[:, 0, :, :], wq_r[:, :, ds(col, P)]).then_inc(s_w, 16)
                        sp.dma_start(w_in[:, 1, :, :], wkv_r[:, :, ds(col, P)]).then_inc(s_w, 16)
                        sp.dma_start(w_in[:, 2, :, :], wkv_r[:, :, ds(colv, P)]).then_inc(s_w, 16)
                        sp.dma_start(wout[:, :], a["L0_attn_Wout"][ds(col, P), :]).then_inc(s_w, 16)
            with sp.Else():
                sp.nop()

        @block.tensor
        def _(pe):
            flag = pe.value_load(keep.flag[0:1, 0:1], min_val=0, max_val=1)
            with pe.If(flag == 1):
                pe.wait_ge(s_const, 48)
                with pe.Fori(0, B) as b:
                    with pe.Fori(0, PB) as hp:
                        pe.wait_ge(s_w, (b * PB + hp) * 64 + 64)
                        for x in range(3):
                            for h in range(2):
                                for c in range(KC):
                                    last = nc.tensor.matmul(bank[2 * x + h][:, :], w_in[:, x, c, :], hT[:, c, ds(b * S + h * HB, HB)],
                                                            start=(c == 0), stop=(c == KC - 1))
                        last.then_inc(s_pj, 1)
                        pe.wait_ge(s_pjc, (b * PB + hp) + 1)
                        for t in range(T):
                            last = nc.tensor.transpose(bank[t // 4][:, t % 4 * P:(t % 4 + 1) * P], vT[:, t * P:(t + 1) * P], ident[:, :])
                        last.then_inc(s_vt, 1)
                        with pe.Fori(0, T) as i:
                            pe.wait_ge(s_vc, (b * PB + hp) + 1)
                            for e in range(2):
                                n = ((b * PB + hp) * T + i) * 2 + e
                                pe.wait_ge(s_qt, n + 1)
                                for h in range(2):
                                    nc.tensor.matmul(bank[h][:, :], qt[:, :], k[e][:, h * HB:(h + 1) * HB], start=True, stop=True)
                                nc.tensor.matmul(bank[2][:, 0:TMAX], qt[:, :], pos[:, :], start=True, stop=True).then_inc(s_sc, 1)
                                pe.wait_ge(s_nr, n + 1)
                                for t in range(T):
                                    last = nc.tensor.transpose(bank[3 + t // 4][:, t % 4 * P:(t % 4 + 1) * P],
                                                               prob[:, t * P:(t + 1) * P], ident[:, :])
                                last.then_inc(s_tp, 1)
                                pe.wait_ge(s_tc, n + 1)
                                for t in range(T):
                                    last = nc.tensor.matmul(bank[5][:, 0:DH], probT[:, t, :], v[:, t, e * DH:(e + 1) * DH],
                                                            start=(t == 0), stop=(t == T - 1))
                                last.then_inc(s_o, 1)
                            m = (b * PB + hp) * T + i
                            pe.wait_ge(s_oc, m * 2 + 2)
                            nc.tensor.transpose(bank[6][:, 0:P], o[:, :], ident[:, :]).then_inc(s_at, 1)
                            pe.wait_ge(s_ac, m + 1)
                            nc.tensor.matmul(bank[7][:, 0:D], oT[:, :], wout[:, :], start=True, stop=True).then_inc(s_y, 1)
                            pe.wait_ge(s_add, m + 1)
            with pe.Else():
                pe.nop()

        @block.scalar
        def _(act):
            flag = act.value_load(keep.flag[0:1, 0:1], min_val=0, max_val=1)
            with act.If(flag == 1):
                with act.Fori(0, B) as b:
                    with act.Fori(0, PB) as hp:
                        act.wait_ge(s_pj, (b * PB + hp) + 1)
                        for h in range(2):
                            half = slice(h * HB, (h + 1) * HB)
                            for e in range(2):
                                nc.scalar.activation(q[e][:, half], bank[h][e * DH:(e + 1) * DH, :], ACT.Copy)
                                nc.scalar.activation(k[e][:, half], bank[2 + h][e * DH:(e + 1) * DH, :], ACT.Copy, scale=DH ** -0.5)
                            last = nc.scalar.activation(vT[:, half], bank[4 + h][:, :], ACT.Copy)
                        last.then_inc(s_pjc, 1)
                        act.wait_ge(s_pjc, (b * PB + hp) + 1)
                        act.wait_ge(s_vt, (b * PB + hp) + 1)
                        for h in range(2):
                            last = nc.scalar.activation(v[:, 4 * h:4 * h + 4, :], bank[h][:, :].rearrange("p (t d) -> p t d", t=4), ACT.Copy)
                        last.then_inc(s_vc, 1)
                        with act.Fori(0, T) as i:
                            for e in range(2):
                                n = ((b * PB + hp) * T + i) * 2 + e
                                act.wait_ge(s_oc, n)
                                nc.scalar.activation(qt[:, :], q[e][:, ds(i * P, P)], ACT.Copy).then_inc(s_qt, 1)
                                act.wait_ge(s_sc, n + 1)
                                for h in range(2):
                                    half = slice(h * HB, (h + 1) * HB)
                                    nc.scalar.activation(gate[:, half], bank[h][:, :], ACT.Tanh, scale=0.5)
                                    nc.scalar.activation(f[:, half], bank[h][:, :], ACT.Copy)
                                nc.scalar.activation(ent[:, :], bank[2][:, 0:TMAX], ACT.Copy).then_inc(s_cp, 1)
                                act.wait_ge(s_f, n + 1)
                                nc.scalar.activation(prob[:, :], f[:, :], ACT.Exp, bias=ntop[:, :], accum_out=total[:, :]).then_inc(s_ex, 1)
                                act.wait_ge(s_tp, n + 1)
                                for h in range(2):
                                    last = nc.scalar.activation(probT[:, 4 * h:4 * h + 4, :], bank[3 + h][:, :].rearrange("p (t d) -> p t d", t=4), ACT.Copy)
                                last.then_inc(s_tc, 1)
                                act.wait_ge(s_o, n + 1)
                                nc.scalar.activation(o[:, e * DH:(e + 1) * DH], bank[5][:, 0:DH], ACT.Copy).then_inc(s_oc, 1)
                            m = (b * PB + hp) * T + i
                            act.wait_ge(s_at, m + 1)
                            nc.scalar.activation(oT[:, :], bank[6][:, 0:P], ACT.Copy).then_inc(s_ac, 1)
            with act.Else():
                act.nop()

        @block.vector
        def _(dve):
            flag = dve.value_load(keep.flag[0:1, 0:1], min_val=0, max_val=1)
            with dve.If(flag == 1):
                nc.vector.memset(ones[:, :], 1.0).then_inc(s_set, 1)
                dve.wait_ge(s_set, 1)
                dve.wait_ge(s_const, 48)
                with dve.Fori(0, B) as b:
                    with dve.Fori(0, PB) as hp:
                        with dve.Fori(0, T) as i:
                            for e in range(2):
                                n = ((b * PB + hp) * T + i) * 2 + e
                                dve.wait_ge(s_cp, n + 1)
                                chain = Count(dve, s_c, n * CHAIN)
                                chain.link(nc.vector.tensor_scalar(gate[:, :], gate[:, :], 0.5, 0.5, ALU.mult, ALU.add))
                                chain.link(nc.vector.tensor_tensor_scan(p[:, :], ones[:, :], gate[:, :], 0.0, ALU.mult, ALU.add))
                                chain.link(nc.vector.tensor_scalar(p[:, :], p[:, :], float(TMAX - 1), None, ALU.min))
                                chain.link(nc.vector.tensor_tensor(slope[:, 0:TMAX - 1], ent[:, 1:TMAX], ent[:, 0:TMAX - 1], ALU.subtract))
                                chain.inc(nc.vector.tensor_scalar(f[:, :], f[:, :], ent[:, 0:1], None, ALU.add))
                                with dve.Fori(0, TMAX - 1) as j:
                                    hinge = Count(dve, s_c, n * CHAIN + 5 + j * 3)
                                    dve.wait_ge(s_c, n * CHAIN + 5 + j * 3)
                                    hinge.link(nc.vector.tensor_scalar(part[:, :], p[:, :], number[:, ds(j, 1)], 0.0, ALU.subtract, ALU.max))
                                    hinge.link(nc.vector.tensor_scalar(part[:, :], part[:, :], 1.0, slope[:, ds(j, 1)], ALU.min, ALU.mult))
                                    hinge.inc(nc.vector.tensor_tensor(f[:, :], f[:, :], part[:, :], ALU.add))
                                chain.n += 3 * (TMAX - 1)
                                dve.wait_ge(s_c, n * CHAIN + 5 + 3 * (TMAX - 1))
                                chain.link(nc.vector.reduce_max(top[:, :], f[:, :], AX))
                                nc.vector.tensor_scalar(ntop[:, :], top[:, :], -1.0, None, ALU.mult).then_inc(s_f, 1)
                                dve.wait_ge(s_ex, n + 1)
                                chain.link(nc.vector.reciprocal(recip[:, :], total[:, :]))
                                chain.link(nc.vector.tensor_copy(part[:, 0:1], recip[:, :]))
                                nc.vector.tensor_scalar(prob[:, :], prob[:, :], recip[:, :], None, ALU.mult).then_inc(s_nr, 1)
                                assert chain.n == CHAIN
                            m = (b * PB + hp) * T + i
                            at = dve.snap(b * T + i)
                            dve.wait_ge(s_y, m + 1)
                            nc.vector.tensor_tensor(rows[:, ds(at, 1), :].rearrange("p o d -> p (o d)"),
                                                    rows[:, ds(at, 1), :].rearrange("p o d -> p (o d)"), bank[7][:, 0:D], ALU.add).then_inc(s_add, 1)
            with dve.Else():
                dve.nop()


def route_stage(nc, keep, a, xp):
    with ExitStack() as ctx:
        def sb(name, shape, dt=F32):
            return ctx.enter_context(nc.sbuf_tensor(name, shape, dt))

        def sem(name):
            return ctx.enter_context(nc.semaphore(name))

        rows = keep.rows
        normed = sb("normed", [P, NT, D])
        n = sb("n3", [P, T, D])
        nT = sb("nT3", [P, KC, S])
        rw = sb("rw", [P, KC, E])
        experts = sb("experts", [P, E])
        upto = sb("upto", [P, P])
        ones = sb("ones3", [P, P])
        logit, best = sb("logit", [P, T, E]), sb("best", [P, T, 8])
        best_i, best_f = sb("best_i", [P, T, 8], U32), sb("best_f", [P, T, TOPK])
        diff, ratio, den = sb("diff", [P, T]), sb("ratio", [P, T]), sb("den", [P, T])
        hot = [sb(f"hot{i}", [P, NT, E]) for i in range(TOPK)]
        both = sb("both", [P, NT, E])
        before, total = sb("before", [P, NT, E]), sb("total", [P, NT, E])
        run = sb("run", [P, E, NT])
        ends = sb("ends", [P, E])
        one_nt = sb("one_nt", [P, NT])
        picked = sb("picked", [P, NT, E])
        place_f = sb("place_f", [P, TOPK, NT])
        stats, mv, rstd = sb("stats3", [P, T, 6]), sb("mv3", [P, T, 2]), sb("rstd3", [P, T])
        work = [ctx.enter_context(nc.psum_tensor(f"work3_{i}", [P, HB], F32)) for i in range(4)]
        plog = ctx.enter_context(nc.psum_tensor("plog", [P, HB], F32))
        pcount = [ctx.enter_context(nc.psum_tensor(f"pcount{i}", [P, HB], F32)) for i in range(2)]

        s_in, s_set, s_var, s_root, s_c = sem("router_in"), sem("set3"), sem("var3"), sem("root3"), sem("dve_chain3")
        s_n, s_tr, s_nT, s_log = sem("n3_ready"), sem("transposed3"), sem("nT3_ready"), sem("logits_ready")
        s_e, s_ed, s_sel, s_cnt, s_place = (sem("diff_ready"), sem("ratio_ready"), sem("chosen"), sem("counted"), sem("places_ready"))
        s_sc, s_tri = sem("rows_scattered"), sem("upto_set")

        block = ctx.enter_context(nc.Block())

        @block.sync
        def _(sp):
            with nc.allow_non_contiguous_dma(reason="the router's weights, transposed: 8 KB"):
                for c in range(KC):
                    sp.dma_start(rw[:, c, :], a["L0_ffn_router_w"][:, c * P:(c + 1) * P].rearrange("e p -> p e")).then_inc(s_in, 16)

        @block.gpsimd
        def _(pool):
            nc.gpsimd.memset(ones[:, :], 1.0).then_inc(s_set, 1)
            nc.gpsimd.memset(upto[:, :], 1.0).then_inc(s_set, 1)
            nc.gpsimd.memset(one_nt[:, :], 1.0).then_inc(s_set, 1)
            nc.gpsimd.iota(experts[:, :], pattern=[[1, E]], base=0, channel_multiplier=0,
                           allow_small_or_imprecise_dtypes=True).then_inc(s_set, 1)
            pool.wait_ge(s_set, 4)
            nc.gpsimd.affine_select(out=upto[:, :], in_=upto[:, :], compare_op=ALU.is_ge, fill=0.0, base=0,
                                    pattern=[[1, P]], channel_multiplier=-1).then_inc(s_tri, 1)
            pool.wait_ge(s_place, 1)
            for t in range(NT):
                for i in range(TOPK):
                    pool.indirect_dma_start(xp, bass.IndirectOffsetOnAxis(ap=keep.place[:, i, t:t + 1], axis=0),
                                            normed[:, t, :], None).then_inc(s_sc, 16)
            pool.wait_ge(s_sc, 16 * NT * TOPK)

        @block.vector
        def _(dve):
            dve.wait_ge(s_set, 4)
            links = 8
            with dve.Fori(0, B) as b:
                chain = Count(dve, s_c, b * links)
                tiles = ds(b * T, T)

                def root(last):
                    last.then_inc(s_var, 1)
                    dve.wait_ge(s_root, b + 1)

                chain.link(nc.vector.tensor_copy(n[:, :, :], rows[:, tiles, :]))
                layernorm_rows(nc, chain.link, lambda last: last.then_inc(s_n, 1), n, n, T, stats, mv, rstd, root,
                               lambda: nc.vector.tensor_copy(rstd[:, 0:1], stats[:, T - 1, 0:1]))
                dve.wait_ge(s_n, b + 1)
                nc.vector.tensor_copy(normed[:, tiles, :], n[:, :, :])
                dve.wait_ge(s_log, b + 1)
                chain.link(nc.vector.tensor_copy(logit[:, :, :], plog[:, 0:T * E].rearrange("p (t e) -> p t e", t=T)))
                nc.vector.tensor_copy(den[:, 0:1], logit[:, T - 1, 0:1])
                for t in range(T):
                    last = nc.vector.max(best[:, t, :], logit[:, t, :])
                chain.link(last)
                nc.vector.tensor_copy(den[:, 0:1], best[:, T - 1, 0:1])
                for t in range(T):
                    last = nc.vector.max_index(best_i[:, t, :], best[:, t, :], logit[:, t, :])
                nc.vector.tensor_tensor(diff[:, :], best[:, :, 1], best[:, :, 0], ALU.subtract).then_inc(s_e, 1)
                dve.wait_ge(s_e, b + 1)
                chain.link(nc.vector.tensor_copy(best_f[:, :, :], best_i[:, :, 0:TOPK]))
                for i in range(TOPK):
                    last = nc.vector.tensor_tensor(hot[i][:, tiles, :], experts[:, :].rearrange("p (o e) -> p o e", o=1).to_broadcast([P, T, E]),
                                                   best_f[:, :, i:i + 1].to_broadcast([P, T, E]), ALU.is_equal)
                dve.wait_ge(s_ed, b + 1)
                chain.link(nc.vector.tensor_scalar(den[:, :], ratio[:, :], 1.0, None, ALU.add))
                chain.link(nc.vector.reciprocal(den[:, :], den[:, :]))
                nc.vector.tensor_copy(keep.weight[:, 0:1, tiles].rearrange("p o t -> p (o t)"), den[:, :])
                nc.vector.tensor_tensor(keep.weight[:, 1:2, tiles].rearrange("p o t -> p (o t)"), den[:, :], ratio[:, :], ALU.mult)
                assert chain.n == links
            chain = Count(dve, s_c, B * links)
            nc.vector.tensor_tensor(both[:, :, :], hot[0][:, :, :], hot[1][:, :, :], ALU.add).then_inc(s_sel, 1)
            dve.wait_ge(s_cnt, 1)
            nc.vector.tensor_copy(before[:, :, :], pcount[0][:, 0:NT * E].rearrange("p (t e) -> p t e", t=NT))
            chain.link(nc.vector.tensor_copy(total[:, :, :], pcount[1][:, 0:NT * E].rearrange("p (t e) -> p t e", t=NT)))
            for e in range(E):
                last = nc.vector.tensor_tensor_scan(run[:, e, :], one_nt[:, :], total[:, :, e], 0.0, ALU.mult, ALU.add)
            chain.link(last)
            chain.link(nc.vector.tensor_tensor_scan(ends[:, :], one_nt[:, 0:E], run[:, :, NT - 1], 0.0, ALU.mult, ALU.add))
            chain.link(nc.vector.tensor_tensor(before[:, :, :], before[:, :, :], total[:, :, :], ALU.subtract))
            chain.link(nc.vector.tensor_tensor(before[:, :, :], before[:, :, :], run[:, :, :].rearrange("p e t -> p t e"), ALU.add))
            chain.link(nc.vector.tensor_tensor(before[:, :, :], ends[:, :].rearrange("p (o e) -> p o e", o=1).to_broadcast([P, NT, E]),
                                               before[:, :, :], ALU.subtract))
            for i in range(TOPK):
                chain.link(nc.vector.tensor_tensor(picked[:, :, :], hot[i][:, :, :], before[:, :, :], ALU.mult))
                chain.link(nc.vector.tensor_reduce(place_f[:, i, :], picked[:, :, :], AX, ALU.add))
            nc.vector.tensor_copy(keep.place[:, :, :], place_f[:, :, :]).then_inc(s_place, 1)

        @block.scalar
        def _(act):
            with act.Fori(0, B) as b:
                act.wait_ge(s_var, b + 1)
                nc.scalar.activation(rstd[:, :], mv[:, :, 1], ACT.Sqrt, bias=keep.eps[:, :]).then_inc(s_root, 1)
                for i in range(4):
                    c, h = divmod(i, 2)
                    act.wait_ge(s_tr, b * 4 + i + 1)
                    nc.scalar.activation(nT[:, c, h * HB:(h + 1) * HB], work[i][:, :], ACT.Copy).then_inc(s_nT, 1)
                act.wait_ge(s_e, b + 1)
                nc.scalar.activation(ratio[:, :], diff[:, :], ACT.Exp).then_inc(s_ed, 1)

        @block.tensor
        def _(pe):
            pe.wait_ge(s_in, 16 * KC)
            pe.wait_ge(s_tri, 1)
            pe.wait_ge(s_set, 4)
            with pe.Fori(0, B) as b:
                pe.wait_ge(s_n, b + 1)
                pe.wait_ge(s_nT, b * 4)
                for i in range(4):
                    c, h = divmod(i, 2)
                    for j in range(4):
                        last = nc.tensor.transpose(work[i][:, j * P:(j + 1) * P], n[:, 4 * h + j, c * P:(c + 1) * P], keep.ident[:, :])
                    last.then_inc(s_tr, 1)
                pe.wait_ge(s_nT, b * 4 + 4)
                pe.wait_ge(s_e, b)
                for t in range(T):
                    for c in range(KC):
                        last = nc.tensor.matmul(plog[:, t * E:(t + 1) * E], nT[:, c, t * P:(t + 1) * P], rw[:, c, :],
                                                start=(c == 0), stop=(c == KC - 1))
                last.then_inc(s_log, 1)
            pe.wait_ge(s_sel, 1)
            nc.tensor.matmul(pcount[0][:, 0:NT * E], upto[:, :], both[:, :, :].rearrange("p t e -> p (t e)"), start=True, stop=True)
            nc.tensor.matmul(pcount[1][:, 0:NT * E], ones[:, :], both[:, :, :].rearrange("p t e -> p (t e)"),
                             start=True, stop=True).then_inc(s_cnt, 1)


def expert_stage(nc, keep, a, xp, yp):
    with ExitStack() as ctx:
        def sb(name, shape, dt=F32):
            return ctx.enter_context(nc.sbuf_tensor(name, shape, dt))

        def sem(name):
            return ctx.enter_context(nc.semaphore(name))

        CR = NR // E
        CT = CR // P
        x = [sb(f"x4_{i}", [P, CT, D]) for i in range(2)]
        xT = sb("xT4", [P, KC, CR])
        w1 = [sb(f"w1_{i}", [P, KC, FF]) for i in range(2)]
        w2 = [sb(f"w2_{i}", [P, FC, D]) for i in range(2)]
        hT = sb("hT4", [P, FC, CR])
        y = [sb(f"y4_{i}", [P, CT, D]) for i in range(2)]
        pt = [ctx.enter_context(nc.psum_tensor(f"pt{i}", [P, HB], F32)) for i in range(2)]
        ph = [ctx.enter_context(nc.psum_tensor(f"ph{i}", [P, HB], F32)) for i in range(3)]
        py = [ctx.enter_context(nc.psum_tensor(f"py{i}", [P, HB], F32)) for i in range(3)]
        s_in = [sem(f"expert_in{i}") for i in range(2)]
        s_tr, s_xT, s_h, s_g, s_y, s_ys, s_out = (sem("x_transposed"), sem("xT_ready"), sem("h_ready4"), sem("gelu_ready"),
                                                  sem("y_ready"), sem("y_copied"), sem("y_written"))
        NH, NY = FC * CR // HB, CT // 2
        block = ctx.enter_context(nc.Block())
        xv = xp.rearrange("(e t p) d -> e p t d", p=P, t=CT)
        yv = yp.rearrange("(e t p) d -> e p t d", p=P, t=CT)

        @block.sync
        def _(sp):
            def load(e, i):
                at = slice(e, e + 1) if isinstance(e, int) else ds(e, 1)
                sp.dma_start(x[i][:, :, :], xv[at].rearrange("o p t d -> p (o t) d")).then_inc(s_in[i], 16)
                sp.dma_start(w1[i][:, :, :], a["L0_ffn_w1"][at].rearrange("o (c p) f -> p (o c) f", p=P)).then_inc(s_in[i], 16)
                sp.dma_start(w2[i][:, :, :], a["L0_ffn_w2"][at].rearrange("o (c p) f -> p (o c) f", p=P)).then_inc(s_in[i], 16)

            load(0, 0)
            load(1, 1)
            with sp.Fori(0, E // 2 - 1) as it:
                for i in range(2):
                    e = sp.snap(it * 2 + i + 2)
                    sp.wait_ge(s_ys, it * (2 * NY) + (i + 1) * NY)
                    load(e, i)

        @block.gpsimd
        def _(pool):
            with pool.Fori(0, E // 2) as it:
                for i in range(2):
                    e = pool.snap(it * 2 + i)
                    pool.wait_ge(s_ys, it * (2 * NY) + (i + 1) * NY)
                    pool.dma_start(yv[ds(e, 1)].rearrange("o p t d -> p (o t) d"), y[i][:, :, :]).then_inc(s_out, 16)
            pool.wait_ge(s_out, 16 * E)

        @block.tensor
        def _(pe):
            with pe.Fori(0, E // 2) as it:
                for i in range(2):
                    pe.wait_ge(s_in[i], it * 48 + 48)
                    nx, nh, ny = it * 8 + i * 4, it * (2 * NH) + i * NH, it * (2 * NY) + i * NY
                    for j in range(4):
                        c, h = divmod(j, 2)
                        pe.wait_ge(s_xT, nx + j - 1 if j >= 1 else nx)
                        for k in range(4):
                            last = nc.tensor.transpose(pt[j % 2][:, k * P:(k + 1) * P], x[i][:, 4 * h + k, c * P:(c + 1) * P], keep.ident[:, :])
                        last.then_inc(s_tr, 1)
                    pe.wait_ge(s_xT, nx + 4)
                    for j in range(NH):
                        f, h = divmod(j, CR // HB)
                        pe.wait_ge(s_g, nh + max(j - 2, 0))
                        for c in range(KC):
                            last = nc.tensor.matmul(ph[j % 3][:, :], w1[i][:, c, f * P:(f + 1) * P], xT[:, c, h * HB:(h + 1) * HB],
                                                    start=(c == 0), stop=(c == KC - 1))
                        last.then_inc(s_h, 1)
                    pe.wait_ge(s_g, nh + NH)
                    for j in range(NY):
                        pe.wait_ge(s_ys, ny + max(j - 2, 0))
                        for k in range(2):
                            t = 2 * j + k
                            for f in range(FC):
                                last = nc.tensor.matmul(py[j % 3][:, k * D:(k + 1) * D], hT[:, f, t * P:(t + 1) * P], w2[i][:, f, :],
                                                        start=(f == 0), stop=(f == FC - 1))
                        last.then_inc(s_y, 1)

        @block.scalar
        def _(act):
            with act.Fori(0, E // 2) as it:
                for i in range(2):
                    nh, ny = it * (2 * NH) + i * NH, it * (2 * NY) + i * NY
                    act.wait_ge(s_y, ny)
                    for j in range(NH):
                        f, h = divmod(j, CR // HB)
                        act.wait_ge(s_h, nh + j + 1)
                        nc.scalar.activation(hT[:, f, h * HB:(h + 1) * HB], ph[j % 3][:, :], ACT.Gelu).then_inc(s_g, 1)

        @block.vector
        def _(dve):
            with dve.Fori(0, E // 2) as it:
                for i in range(2):
                    nx, ny = it * 8 + i * 4, it * (2 * NY) + i * NY
                    for j in range(4):
                        c, h = divmod(j, 2)
                        dve.wait_ge(s_tr, nx + j + 1)
                        nc.vector.tensor_copy(xT[:, c, h * HB:(h + 1) * HB], pt[j % 2][:, :]).then_inc(s_xT, 1)
                    dve.wait_ge(s_out, it * 32 + max(i - 1, 0) * 16)
                    for j in range(NY):
                        dve.wait_ge(s_y, ny + j + 1)
                        nc.vector.tensor_copy(y[i][:, 2 * j:2 * j + 2, :], py[j % 3][:, :].rearrange("p (k d) -> p k d", k=2)).then_inc(s_ys, 1)


def combine_stage(nc, keep, yp, out):
    with ExitStack() as ctx:
        RG = 6
        got = [ctx.enter_context(nc.sbuf_tensor(f"got{i}", [P, TOPK, D], F32)) for i in range(RG)]
        s_got = [ctx.enter_context(nc.semaphore(f"gathered{i}")) for i in range(RG)]
        s_sum, s_first, s_out = (ctx.enter_context(nc.semaphore(x)) for x in ("summed", "first_added", "out_written"))
        block = ctx.enter_context(nc.Block())

        @block.gpsimd
        def _(pool):
            for t in range(NT):
                if t >= RG:
                    pool.wait_ge(s_sum, t - RG + 1)
                for i in range(TOPK):
                    pool.indirect_dma_start(got[t % RG][:, i, :], None, yp,
                                            bass.IndirectOffsetOnAxis(ap=keep.place[:, i, t:t + 1], axis=0)).then_inc(s_got[t % RG], 16)

        @block.vector
        def _(dve):
            for t in range(NT):
                dve.wait_ge(s_got[t % RG], 32 * (t // RG + 1))
                row = keep.rows[:, t, :]
                nc.vector.scalar_tensor_tensor(row, got[t % RG][:, 0, :], keep.weight[:, 0, t:t + 1], row, ALU.mult, ALU.add).then_inc(s_first, 1)
                dve.wait_ge(s_first, t + 1)
                nc.vector.scalar_tensor_tensor(row, got[t % RG][:, 1, :], keep.weight[:, 1, t:t + 1], row, ALU.mult, ALU.add).then_inc(s_sum, 1)

        @block.sync
        def _(sp):
            for t in range(0, NT, 4):
                sp.wait_ge(s_sum, t + 4)
                sp.dma_start(out[t * P:(t + 4) * P, :].rearrange("(t p) d -> p t d", p=P), keep.rows[:, t:t + 4, :]).then_inc(s_out, 16)
            sp.wait_ge(s_out, 16 * (NT // 4))


class Keep:
    pass


def program(nc, a, out):
    with ExitStack() as ctx:
        def sb(name, shape, dt=F32):
            return ctx.enter_context(nc.sbuf_tensor(name, shape, dt))

        keep = Keep()
        keep.ident = sb("ident", [P, P])
        keep.eps = sb("eps", [P, 1])
        keep.excess = sb("excess", [P, 1])
        keep.minus = sb("minus", [P, 32])
        keep.flag = sb("flag", [1, 1], I32)
        keep.rows = sb("rows", [P, NT, D])
        with nc.sbuf_tensor("hT", [P, KC, R], F32) as keep.hT:
            constants(nc, keep)
            token_stage(nc, keep, a["ids"], a["L0_tok_emb_table"], a["pos"], a["L0_tok_Wq"], a["L0_tok_bq"],
                        a["L0_tok_Wk"], a["L0_tok_bk"], a["L0_tok_Wv"], a["L0_tok_bv"], a["L0_tok_Wf"],
                        a["L0_tok_bf"], a["L0_attn_b_out"])
            saved = nc.dram_tensor("saved_rows", [R, D], F32, kind="Internal").ap()
            cope_stage(nc, keep, a, saved)
            verdict_stage(nc, keep)
            general_cope_stage(nc, keep, a, saved)
        keep.place = sb("place", [P, TOPK, NT], I32)
        keep.weight = sb("weight", [P, TOPK, NT])
        xp = nc.dram_tensor("sorted_rows", [NR, D], F32, kind="Internal").ap()
        yp = nc.dram_tensor("sorted_results", [NR, D], F32, kind="Internal").ap()
        route_stage(nc, keep, a, xp)
        expert_stage(nc, keep, a, xp, yp)
        combine_stage(nc, keep, yp, out)


def constants(nc, keep):
    with nc.semaphore("zeros_set") as s_zero, nc.semaphore("const_set") as s_set, nc.Block() as block:
        @block.gpsimd
        def _(pool):
            nc.gpsimd.memset(keep.ident[:, :], 0.0).then_inc(s_zero, 1)
            nc.gpsimd.memset(keep.eps[:, :], EPS).then_inc(s_zero, 1)
            pool.wait_ge(s_zero, 2)
            nc.gpsimd.affine_select(out=keep.ident[:, :], in_=keep.ident[:, :], compare_op=ALU.not_equal, fill=1.0,
                                    base=0, pattern=[[-1, P]], channel_multiplier=1).then_inc(s_set, 1)
            pool.wait_ge(s_set, 1)


def kernel(**inputs):
    import numpy as _np
    import concourse.bacc as _bacc
    from concourse.bass_utils import run_bass_kernel_spmd as _run

    nc = _bacc.Bacc("TRN2", target_bir_lowering=False, num_devices=1)
    arrays = {k: _np.ascontiguousarray(v) for k, v in inputs.items() if k != "x"}
    x = _np.asarray(inputs["x"])
    arrays["ids"] = _np.ascontiguousarray(x.reshape(R)[::-1].reshape(NT, P).T)
    div = _np.exp(_np.arange(0, D, 2, dtype=_np.float32) * _np.float32(-_np.log(10000.0) / D))
    angle = _np.arange(S, dtype=_np.float32)[:, None] * div.astype(_np.float32)
    pos = _np.zeros((S, D), _np.float32)
    pos[:, 0::2], pos[:, 1::2] = _np.sin(angle), _np.cos(angle)
    arrays["pos"] = _np.ascontiguousarray(pos[::-1])
    arrays["tables"] = cope_tables()
    arrays["number"] = _np.arange(TMAX, dtype=_np.float32)
    arrays["minus"] = -_np.arange(32, dtype=_np.float32)
    feed, aps = {}, {}
    for name, v in arrays.items():
        feed[f"in_{name}"] = v
        aps[name] = nc.dram_tensor(f"in_{name}", v.shape, I32 if v.dtype.kind == "i" else F32, kind="ExternalInput").ap()
    out = nc.dram_tensor("out_rows", [R, D], F32, kind="ExternalOutput").ap()
    program(nc, aps, out)
    r = _run(nc, [feed], core_ids=[0])
    return _np.ascontiguousarray(r.results[0]["out_rows"][::-1].reshape(B, S, D))
```

```python
from contextlib import ExitStack

import concourse.bass as bass
from concourse import mybir

F32 = mybir.dt.float32
I32 = mybir.dt.int32
U32 = mybir.dt.uint32
ALU = mybir.AluOpType
ACT = mybir.ActivationFunctionType
AX = mybir.AxisListType.X
ds = bass.ds

P = 128
B, S, D = 4, 1024, 256
R = B * S
T = S // P
NT = R // P
KC = D // P
HB = 512
H1, DH = 4, 64
H2 = 16
NPAIR = B * H2 // 2
EPS = 1e-5
TMAX = DH
E, FF, TOPK = 8, 1024, 2
NR = R * TOPK
FC = FF // P


class Count:

    def __init__(self, eng, sem, base=0):
        self.eng, self.sem, self.base, self.n = eng, sem, base, 0

    def inc(self, instruction):
        self.n += 1
        instruction.then_inc(self.sem, 1)

    def link(self, instruction):
        self.inc(instruction)
        self.eng.wait_ge(self.sem, self.base + self.n)


def bcast(ap, shape):
    return ap.to_broadcast(shape)


def layernorm_rows(nc, link, inc_last, x, out, n, stats, mv, rstd, act_sqrt, settled):
    for i in range(n):
        last = nc.vector.bn_stats(stats[:, i, :], x[:, i, :])
    link(last)
    settled()
    for i in range(n):
        last = nc.vector.bn_aggr(mv[:, i, :], stats[:, i, :])
    act_sqrt(last)
    link(nc.vector.reciprocal(rstd[:, 0:n], rstd[:, 0:n]))
    for i in range(n):
        last = nc.vector.tensor_scalar(out[:, i, :], x[:, i, :], mv[:, i, 0:1], rstd[:, i:i + 1],
                                       ALU.subtract, ALU.mult)
    inc_last(last)


def token_stage(nc, keep, ids, emb, pos, wq, bq, wk, bk, wv, bv, wf, bf, b_out):
    with ExitStack() as ctx:
        def sb(name, shape, dt=F32):
            return ctx.enter_context(nc.sbuf_tensor(name, shape, dt))

        def sem(name):
            return ctx.enter_context(nc.semaphore(name))

        rows, hT = keep.rows, keep.hT
        ids_sb = sb("ids_sb", [P, NT], I32)
        pos_sb = sb("pos_sb", [P, T, D])
        wq_sb, wk_sb, wv_sb, wf_sb = (sb(n, [P, KC, D]) for n in ("wq1", "wk1", "wv1", "wf1"))
        bq_sb, bk_sb = sb("bq1", [P, 2]), sb("bk1", [P, 2])
        bv_sb, bf_sb = sb("bv1", [P, D]), sb("bf1", [P, D])
        bout = sb("bout", [P, D])
        x = sb("x1", [P, T, D])
        xT = sb("xT1", [P, KC, S])
        qT = sb("qT1", [P, 2, S])
        kT = sb("kT1", [P, H1, S])
        v = sb("v1", [P, T, D])
        vs = sb("vs1", [P, 2, T, DH])
        probs = sb("probs1", [P, 2, T, S])
        z = x
        nmx = sb("nmx1", [P, 2, T])
        ssum, rsum = sb("ssum1", [P, 2, T]), sb("rsum1", [P, T])
        stats, mv, rstd = sb("stats1", [P, T, 6]), sb("mv1", [P, T, 2]), sb("rstd1", [P, T])

        work = [ctx.enter_context(nc.psum_tensor(f"work1_{i}", [P, HB], F32)) for i in range(2)]
        score = [ctx.enter_context(nc.psum_tensor(f"score1_{i}", [P, S], F32)) for i in range(2)]
        zp = ctx.enter_context(nc.psum_tensor("zp1", [P, S], F32))

        s_w, s_ids, s_gather = sem("weights_in"), sem("ids_in"), sem("rows_gathered")
        s_x, s_tr, s_xT = sem("x_ready"), sem("work_full_for_act"), sem("work_copied_by_act")
        s_vp, s_v = sem("work_full_for_dve"), sem("work_read_by_dve")
        s_score, s_quarter, s_max, s_exp = sem("score_ready"), sem("bias_scaled"), sem("minus_max_ready"), sem("exp_ready")
        s_vs, s_z, s_zc = sem("scaled_v_ready"), sem("key_tile_multiplied"), sem("zp_copied")
        s_zeros, s_batch = sem("k_zeros_set"), sem("batch_gathered")
        s_zz, s_var, s_root, s_c = sem("zn_ready"), sem("var_ready"), sem("root_ready"), sem("dve_chain1")
        s_h = sem("h_ready")

        jobs = ([("xT", c, h, "act") for c in range(KC) for h in range(2)]
                + [(n, g, h, "act") for n in ("q", "k") for g in range(2) for h in range(2)]
                + [("v", t, 0, "dve") for t in range(T // 2)]
                + [("back", g, h, "dve") for g in range(2) for h in range(2)]
                + [("zT", c, h, "act") for c in range(KC) for h in range(2)]
                + [("ff", t, 0, "dve") for t in range(T // 2)]
                + [("hT", c, h, "act") for c in range(KC) for h in range(2)])
        n_act = sum(j[3] == "act" for j in jobs)
        n_dve = len(jobs) - n_act
        nb = len(work)

        def done_before(j, who):
            return sum(k[3] == who for k in jobs[:j])

        def first(name):
            return next(j for j, k in enumerate(jobs) if k[0] == name)

        block = ctx.enter_context(nc.Block())

        @block.sync
        def _(sp):
            sp.dma_start(ids_sb[:, :], ids).then_inc(s_ids, 16)
            sp.dma_start(pos_sb[:, :, :], pos.rearrange("(t p) d -> p t d", p=P)).then_inc(s_w, 16)
            for dst, src in ((wq_sb, wq), (wk_sb, wk), (wv_sb, wv)):
                for h in range(H1):
                    sp.dma_start(dst[:, :, h * DH:(h + 1) * DH],
                                 src[h].rearrange("(c p) d -> p c d", p=P)).then_inc(s_w, 16)
            sp.dma_start(wf_sb[:, :, :], wf.rearrange("(c p) n -> p c n", p=P)).then_inc(s_w, 16)
            for dst, src in ((bq_sb, bq), (bk_sb, bk)):
                for g in range(2):
                    sp.dma_start(dst[:, g:g + 1], src[2 * g:2 * g + 2, :].rearrange("h (d o) -> (h d) o", o=1)).then_inc(s_w, 16)
            sp.dma_start(bv_sb[:, :], bv.rearrange("h d -> (h d)").partition_broadcast(P)).then_inc(s_w, 16)
            sp.dma_start(bf_sb[:, :], bf.partition_broadcast(P)).then_inc(s_w, 16)
            sp.dma_start(bout[:, :], b_out.partition_broadcast(P)).then_inc(s_w, 16)
        n_w = 16 * (1 + 3 * H1 + 1 + 4 + 3)

        @block.gpsimd
        def _(pool):
            pool.wait_ge(s_ids, 16)
            for b in range(B):
                for t in range(b * T, (b + 1) * T):
                    pool.indirect_dma_start(rows[:, t, :], None, emb,
                                            bass.IndirectOffsetOnAxis(ap=ids_sb[:, t:t + 1], axis=0)).then_inc(s_gather, 16)
                pool.wait_ge(s_gather, 16 * (b + 1) * T)
                pool.sem_inc(s_batch, 1)

        @block.vector
        def _(dve):
            for h in range(H1):
                other = DH * (1 - h % 2)
                nc.vector.memset(kT[other:other + DH, h, :], 0.0).then_inc(s_zeros, 1)
            dve.wait_ge(s_w, n_w)
            with dve.Fori(0, B) as b:
                dve_links = Count(dve, s_c, b * N_LINKS1)
                dve.wait_ge(s_batch, b + 1)
                nc.vector.tensor_tensor(x[:, :, :], rows[:, ds(b * T, T), :], pos_sb[:, :, :], ALU.add).then_inc(s_x, 1)
                for t in range(T // 2):
                    dve.wait_ge(s_vp, b * n_dve + t + 1)
                    nc.vector.tensor_tensor(
                        v[:, 2 * t:2 * t + 2, :],
                        work[(first("v") + t) % nb][:, :].rearrange("p (a d) -> p a d", a=2),
                        bv_sb[:, :].rearrange("p (o d) -> p o d", o=1).to_broadcast([P, 2, D]),
                        ALU.add).then_inc(s_v, 1)
                dve.wait_ge(s_v, b * n_dve + T // 2)

                def head_max(h):
                    for t in range(T):
                        k = h * T + t
                        dve.wait_ge(s_score, b * H1 * T + k + 1)
                        nc.vector.reduce_max(nmx[:, h % 2, t:t + 1], score[k % 2][:, :], AX, negate=True).then_inc(s_max, 1)

                def head_values(h):
                    dve.wait_ge(s_exp, b * H1 * T + (h + 1) * T)
                    dve_links.link(nc.vector.reciprocal(rsum[:, :], ssum[:, h % 2, :]))
                    nc.vector.tensor_tensor(
                        vs[:, h % 2, :, :], v[:, :, h * DH:(h + 1) * DH],
                        rsum[:, :].rearrange("p (t o) -> p t o", o=1).to_broadcast([P, T, DH]), ALU.mult).then_inc(s_vs, 1)

                for h in range(H1):
                    head_max(h)
                    head_values(h)
                for g in range(2):
                    for h in range(2):
                        j = first("back") + 2 * g + h
                        dve.wait_ge(s_vp, b * n_dve + done_before(j, "dve") + 1)
                        nc.vector.tensor_tensor(z[:, 4 * h:4 * h + 4, g * P:(g + 1) * P], work[j % nb][:, :].rearrange("p (t d) -> p t d", t=4),
                                                x[:, 4 * h:4 * h + 4, g * P:(g + 1) * P], ALU.add).then_inc(s_v, 1)
                dve.wait_ge(s_v, b * n_dve + done_before(first("zT"), "dve"))

                def norm(i, src, dst, done):
                    def root(last):
                        last.then_inc(s_var, 1)
                        dve.wait_ge(s_root, b * 3 + i + 1)
                    layernorm_rows(nc, dve_links.link, done, src, dst, T, stats, mv, rstd, root, lambda: nc.vector.tensor_copy(rstd[:, 0:1], stats[:, T - 1, 0:1]))

                norm(0, z, z, lambda last: last.then_inc(s_zz, 1))
                dve.wait_ge(s_zz, b * 3 + 1)
                dve_links.link(nc.vector.tensor_tensor(
                    v[:, :, :], z[:, :, :], bf_sb[:, :].rearrange("p (o d) -> p o d", o=1).to_broadcast([P, T, D]), ALU.add))
                for t in range(T // 2):
                    dve.wait_ge(s_vp, b * n_dve + done_before(first("ff") + t, "dve") + 1)
                    nc.vector.tensor_tensor(v[:, 2 * t:2 * t + 2, :], v[:, 2 * t:2 * t + 2, :],
                                            work[(first("ff") + t) % nb][:, :].rearrange("p (a d) -> p a d", a=2),
                                            ALU.add).then_inc(s_v, 1)
                dve.wait_ge(s_v, (b + 1) * n_dve)
                norm(1, v, z, lambda last: last.then_inc(s_zz, 1))
                dve.wait_ge(s_zz, b * 3 + 2)
                nc.vector.tensor_tensor(rows[:, ds(b * T, T), :], z[:, :, :],
                                        bout[:, :].rearrange("p (o d) -> p o d", o=1).to_broadcast([P, T, D]), ALU.add)
                norm(2, z, z, lambda last: last.then_inc(s_zz, 1))
                dve.wait_ge(s_xT, (b + 1) * n_act)
                assert dve_links.n == N_LINKS1, dve_links.n

        @block.scalar
        def _(act):
            act.wait_ge(s_w, n_w)
            nc.scalar.activation(bq_sb[:, :], bq_sb[:, :], ACT.Copy, scale=0.25).then_inc(s_quarter, 1)
            act.wait_ge(s_quarter, 1)
            with act.Fori(0, B) as b:
                def empty(j, dst, func=ACT.Copy, **kw):
                    act.wait_ge(s_tr, b * n_act + done_before(j, "act") + 1)
                    nc.scalar.activation(dst, work[j % nb][:, :], func, **kw).then_inc(s_xT, 1)

                for j, (name, g, h, who) in enumerate(jobs[:first("zT")]):
                    half = slice(h * HB, (h + 1) * HB)
                    if name == "xT":
                        empty(j, xT[:, g, half])
                    elif name == "q":
                        empty(j, qT[:, g, half], ACT.Identity, bias=bq_sb[:, g:g + 1], scale=0.25)
                    elif name == "k":
                        act.wait_ge(s_tr, b * n_act + done_before(j, "act") + 1)
                        for e in range(2):
                            at = slice(e * DH, (e + 1) * DH)
                            last = nc.scalar.activation(kT[at, 2 * g + e, half], work[j % nb][at, :], ACT.Identity, bias=bk_sb[at, g:g + 1])
                        last.then_inc(s_xT, 1)
                for h in range(H1):
                    for t in range(T):
                        k = h * T + t
                        act.wait_ge(s_max, b * H1 * T + k + 1)
                        if h >= 2:
                            act.wait_ge(s_z, b * 2 * T + t + 1)
                        nc.scalar.activation(probs[:, h % 2, t, :], score[k % 2][:, :], ACT.Exp,
                                             bias=nmx[:, h % 2, t:t + 1],
                                             accum_out=ssum[:, h % 2, t:t + 1]).then_inc(s_exp, 1)

                for g in range(2):
                    act.wait_ge(s_z, b * 2 * T + (g + 1) * T)
                    nc.scalar.activation(xT[:, g, :], zp[:, :], ACT.Copy).then_inc(s_zc, 1)

                def root(i):
                    act.wait_ge(s_var, b * 3 + i + 1)
                    nc.scalar.activation(rstd[:, :], mv[:, :, 1], ACT.Sqrt, bias=keep.eps[:, :]).then_inc(s_root, 1)

                root(0)
                for j, (name, g, h, who) in enumerate(jobs):
                    half = slice(h * HB, (h + 1) * HB)
                    if name == "zT":
                        empty(j, xT[:, g, half], ACT.Relu)
                root(1)
                root(2)
                for j, (name, g, h, who) in enumerate(jobs):
                    if name == "hT":
                        empty(j, hT[:, g, ds(b * S + h * HB, HB)])

        @block.tensor
        def _(pe):
            pe.wait_ge(s_w, n_w)
            with pe.Fori(0, B) as b:
                def bank(j):
                    k = j - nb
                    if k >= 0:
                        who = jobs[k][3]
                        pe.wait_ge(s_xT if who == "act" else s_v,
                                   b * (n_act if who == "act" else n_dve) + done_before(k, who) + 1)
                    return work[j % nb]

                def full(j, last):
                    last.then_inc(s_tr if jobs[j][3] == "act" else s_vp, 1)

                def transposes(j, src, c, h):
                    w = bank(j)
                    for i in range(4):
                        last = nc.tensor.transpose(w[:, i * P:(i + 1) * P],
                                                   src[:, 4 * h + i, c * P:(c + 1) * P], keep.ident[:, :])
                    full(j, last)

                pe.wait_ge(s_x, b + 1)
                for j, (name, g, h, who) in enumerate(jobs[:first("back")]):
                    if name == "xT":
                        transposes(j, x, g, h)
                    elif name in "qk":
                        pe.wait_ge(s_xT, b * n_act + 2 * KC)
                        w = bank(j)
                        for c in range(KC):
                            last = nc.tensor.matmul(w[:, :], (wq_sb if name == "q" else wk_sb)[:, c, g * P:(g + 1) * P],
                                                    xT[:, c, h * HB:(h + 1) * HB], start=(c == 0), stop=(c == KC - 1))
                        full(j, last)
                    else:
                        w = bank(j)
                        for a in range(2):
                            for c in range(KC):
                                t = 2 * g + a
                                last = nc.tensor.matmul(w[:, a * D:(a + 1) * D], xT[:, c, t * P:(t + 1) * P],
                                                        wv_sb[:, c, :], start=(c == 0), stop=(c == KC - 1))
                        full(j, last)
                pe.wait_ge(s_xT, b * n_act + 2 * KC + 8)

                def scores(h, t):
                    k = h * T + t
                    if k >= 2:
                        pe.wait_ge(s_exp, b * H1 * T + k - 1)
                    for n in range(2):
                        last = nc.tensor.matmul(score[k % 2][:, n * HB:(n + 1) * HB], kT[:, h, t * P:(t + 1) * P],
                                                qT[:, h // 2, n * HB:(n + 1) * HB], start=True, stop=True)
                    last.then_inc(s_score, 1)

                def products(t):
                    for n in range(2):
                        for e in range(2):
                            last = nc.tensor.matmul(zp[e * DH:(e + 1) * DH, n * HB:(n + 1) * HB], vs[:, e, t, :],
                                                    probs[:, e, t, n * HB:(n + 1) * HB], start=(t == 0), stop=(t == T - 1))
                    last.then_inc(s_z, 1)

                def back(g):
                    pe.wait_ge(s_zc, b * 2 + g + 1)
                    for h in range(2):
                        j = first("back") + 2 * g + h
                        w = bank(j)
                        for i in range(4):
                            t = 4 * h + i
                            last = nc.tensor.transpose(w[:, i * P:(i + 1) * P], xT[:, g, t * P:(t + 1) * P], keep.ident[:, :])
                        full(j, last)

                pe.wait_ge(s_zeros, H1)
                for h in range(2):
                    for t in range(T):
                        scores(h, t)
                scores(2, 0)
                pe.wait_ge(s_vs, b * H1 + 2)
                for t in range(1, T):
                    scores(2, t)
                    products(t - 1)
                products(T - 1)
                for t in range(T):
                    scores(3, t)
                back(0)
                pe.wait_ge(s_vs, b * H1 + 4)
                for t in range(T):
                    products(t)
                back(1)
                pe.wait_ge(s_zz, b * 3 + 1)
                for j, (name, g, h, who) in enumerate(jobs):
                    if name == "zT":
                        transposes(j, z, g, h)
                    elif name == "ff":
                        if g == 0:
                            pe.wait_ge(s_xT, b * n_act + 2 * KC + 8 + 2 * KC)
                        w = bank(j)
                        for a in range(2):
                            for c in range(KC):
                                t = 2 * g + a
                                last = nc.tensor.matmul(w[:, a * D:(a + 1) * D], xT[:, c, t * P:(t + 1) * P],
                                                        wf_sb[:, c, :], start=(c == 0), stop=(c == KC - 1))
                        full(j, last)
                pe.wait_ge(s_zz, b * 3 + 3)
                for j, (name, g, h, who) in enumerate(jobs):
                    if name == "hT":
                        transposes(j, z, g, h)


N_LINKS1 = H1 + 3 * 2 + 1


PER, RISE = 5, 2
BLOCKS = (TMAX // RISE)
TAIL = BLOCKS * PER
BODY = S - TAIL


def hinge_blocks():
    out = []
    l = 1
    while True:
        a0 = next((a for a in range(BLOCKS) if 0.61 * PER * (a + 1) + 0.3 > RISE * a + l), BLOCKS)
        a1 = (TMAX - 1 - l) // RISE
        if a0 > a1:
            return out
        out.append((l, a0, a1 + 1))
        l += 1


HINGES = hinge_blocks()
N_RELU = 4
POOL = [1, 2, 3, 5, 6, 8, 9, 11, 13, 15]
N_POOL = len(POOL)
CHECK_AT = 2
GROUPS = T
RING = 4
NBANK = 6
OUTS = T // 2
SLOTS = 4


def cope_tables():
    import numpy as np
    low = RISE * (np.arange(TAIL) // PER)
    most = np.full(TAIL, 1e30, np.float32)
    for a in range(BLOCKS):
        covered = max((l for l, a0, a1 in HINGES if a0 <= a < a1), default=0)
        if RISE * a + covered < TMAX - 1:
            most[a * PER:(a + 1) * PER] = covered + 1
    return np.stack([(0.5 * (np.arange(TAIL) + 1) - low).astype(np.float32), most])


def cope_stage(nc, keep, a, saved):
    with ExitStack() as ctx:
        def sb(name, shape, dt=F32):
            return ctx.enter_context(nc.sbuf_tensor(name, shape, dt))

        def sem(name):
            return ctx.enter_context(nc.semaphore(name))

        rows, hT, ident = keep.rows, keep.hT, keep.ident
        w_in = sb("w_in", [P, 3, KC, P])
        wout = [sb(f"wout{s}", [P, D]) for s in range(SLOTS)]
        pos = sb("pos2", [P, TMAX])
        zero, lack = sb("zero", [P, 1]), sb("lack", [P, 1])
        found = sb("found", [P, 3])
        q = [sb(f"q{s}", [P, S]) for s in range(SLOTS)]
        k = [sb(f"k{s}", [P, S]) for s in range(SLOTS)]
        vT = sb("vT", [P, S])
        v = [sb(f"values{s}", [P, T, DH]) for s in range(SLOTS)]
        ex = [sb(f"ex{i}", [P, S]) for i in range(RING)]
        prod = sb("prod", [P, S])
        esum = sb("esum", [P, S])
        rcol = sb("rcol", [P, T])
        one = sb("one", [P, 1])
        gate = sb("gate", [P, T, TAIL])
        above = sb("above_low", [P, T, TAIL])
        f = [sb(f"f{i}", [P, T, TAIL]) for i in range(2)]
        relu = [sb(f"relu{i}", [P, T * PER * max(a1 - a0 for l, a0, a1 in HINGES[i::N_RELU])]) for i in range(N_RELU)]
        pieces = sb("pieces", [P, T, TAIL])
        table = sb("table", [P, 2, TAIL])
        carry = sb("carry", [P, T, TAIL], mybir.dt.bfloat16)
        over = sb("over", [P, T, TAIL], mybir.dt.bfloat16)
        breach = sb("breach", [P, 2, 3])
        ent = [sb(f"ent{i}", [P, T, TMAX]) for i in range(2)]
        slope, bend = sb("slope", [P, T, TMAX]), sb("bend", [P, T, TMAX])
        bmax, tmax = sb("bmax", [P, T, 2]), sb("tmax", [P, T])
        shift = [sb(f"shift{i}", [P, T]) for i in range(2)]
        bm = sb("bm", [P, T])
        nmax = [sb(f"nmax{i}", [P, T]) for i in range(2)]

        bank = [ctx.enter_context(nc.psum_tensor(f"bank{i}", [P, HB], F32)) for i in range(NBANK)]
        pv = ctx.enter_context(nc.psum_tensor("pv", [P, S], F32))

        s_const, s_w = sem("consts_in"), sem("pair_weights_in")
        s_wo, s_prep = sem("output_weights_in"), sem("entries_prepared")
        s_set, s_ones = sem("memsets_done"), sem("ones_set")
        s_fa, s_fd = sem("bank_full_for_act"), sem("bank_full_for_dve")
        s_ra, s_rd = sem("bank_read_by_act"), sem("bank_read_by_dve")
        s_zero = sem("shift_row_zeroed")
        s_p, s_over, s_seen, s_relu = sem("p_ready"), sem("over_ready"), sem("p_checked"), sem("relu_ready")
        s_part, s_padd, s_dadd = sem("hinge_for_pool"), sem("hinge_added_by_pool"), sem("hinge_added_by_dve")
        s_gate = sem("gate_used")
        s_m, s_xt, s_pvm, s_copied = sem("max_known"), sem("tail_exp_ready"), sem("products_done"), sem("products_copied")
        s_es = sem("exps_summed")
        s_saved = sem("rows_saved")
        s_c, s_rev = sem("dve_chain2"), sem("breach_known")

        def tail_jobs(s):
            return [("tail", s, i, "act") for i in range(3)] + [("ent", s, 0, "act")]

        def pair_jobs(s):
            return [[("pq", s, h, "act") for h in range(2)], [("pk", s, h, "act") for h in range(2)],
                    [("pv", s, h, "act") for h in range(2)], [("vtr", s, h, "act") for h in range(2)]]

        def body_jobs(m):
            first = [0, 2, 5, 8, 11, 14, 16, 16, 16]
            return range(first[m], first[m + 1])

        def slot_plan(s):
            nxt, nnxt = (s + 1) % SLOTS, (s + 2) % SLOTS
            plan = [[("row", s, h, "act") for h in range(2)] + [("tt", s, i, "act") for i in range(2)]
                    + [("body", nxt, i, "dve") for i in body_jobs(0)]]
            for m in range(1, GROUPS):
                g = [("sT", s, 2 * m + h, "act") for h in range(2)]
                if m == 1:
                    g += [("tt", s, i, "act") for i in (2, 3)]
                g += [("body", nxt, i, "dve") for i in body_jobs(m)]
                if m in (3, 5, 7):
                    g += [("PV", s, m // 2 - 1)]
                if m in (1, 3):
                    g += pair_jobs(nnxt)[m // 2] if s % 2 == 0 else pair_jobs(nxt)[2 + m // 2]
                if m == GROUPS - 1:
                    tails = tail_jobs(nnxt)
                    g += tails[:2] + [("PV", s, T // 2 - 1)] + tails[2:]
                    g += [("out", s, i, "dve") for i in range(OUTS)] + [("sum", s, 0, "dve")]
                plan.append(g)
            return plan

        pro_plan = [[j for js in pair_jobs(0) for j in js] + tail_jobs(0)]
        pro_plan += [[("body", 0, i, "dve") for i in body_jobs(m)] for m in range(GROUPS)]
        pro_plan[5][0:0] = tail_jobs(1)
        body_plan = [slot_plan(s) for s in range(SLOTS)]

        def is_job(x):
            return x[0] != "PV"

        pro = [j for g in pro_plan for j in g]
        turn = [j for p in body_plan for g in p for j in g if is_job(j)]
        pad = -len(turn) % NBANK
        last_of_bank = {}
        info = {}

        def place(part, jobs, first):
            n = {"act": 0, "dve": 0}
            pos = first
            for i, j in enumerate(jobs):
                n[j[3]] += 1
                info[(part, j)] = (pos % NBANK, n[j[3]], last_of_bank.get(pos % NBANK))
                last_of_bank[pos % NBANK] = (part, j)
                pos += 1
                if part == "turn" and i == len(jobs) // 2:
                    pos += pad
            return n

        n_pro = place("pro", pro, -len(pro))
        n_turn = place("turn", turn, 0)
        assert [j[3] for j in pro[-NBANK:]] == [j[3] for j in turn[-NBANK:]]

        class Place:

            def __init__(self, eng, part, it):
                self.eng, self.part, self.it = eng, part, it

            def at(self, who, n, part=None):
                part = part or self.part
                if part == "pro":
                    return n
                return n_pro[who] + self.it * n_turn[who] + n

            def job(self, j):
                return info[(self.part, j)]

            def head(self, sem, s, per, n):
                n += s * per + (per if sem in (s_pvm, s_es, s_copied, s_zero) else 0)
                assert n > 0
                self.eng.wait_ge(sem, n if self.part == "pro" else self.it * (SLOTS * per) + n)

        def read_count(part, j):
            return info[(part, j)][1] + (1 if j[0] == "out" else -OUTS if j[0] == "sum" else 0)

        def pe_take(w, j):
            b, _, before = w.job(j)
            if before is None and w.part == "pro":
                return bank[b]
            part, prev = before
            who = prev[3]
            if part == w.part:
                w.eng.wait_ge(s_ra if who == "act" else s_rd, w.at(who, read_count(part, prev)))
            else:
                w.eng.wait_ge(s_ra if who == "act" else s_rd, w.at(who, min(info[before][1] - n_pro[who] + 1, 0)))
            return bank[b]

        def pe_need(w, part, j):
            who = j[3]
            w.eng.wait_ge(s_ra if who == "act" else s_rd, w.at(who, read_count(part, j), part))

        def pe_job(w, j, b_of):
            kind, s, i, who = j
            ps = pe_take(w, j)
            if kind in ("pq", "pk", "pv"):
                x = ("pq", "pk", "pv").index(kind)
                for c in range(KC):
                    last = nc.tensor.matmul(ps[:, :], w_in[:, x, c, :], hT[:, c, ds(b_of * S + i * HB, HB)],
                                            start=(c == 0), stop=(c == KC - 1))
            elif kind == "vtr":
                pe_need(w, w.part, ("pv", s, 1, "act"))
                for n in range(4):
                    last = nc.tensor.transpose(ps[:, n * P:(n + 1) * P], vT[:, (4 * i + n) * P:(4 * i + n + 1) * P], ident[:, :])
            elif kind == "tail":
                for n, t in enumerate(range(3 * i, min(3 * i + 3, T))):
                    last = nc.tensor.matmul(ps[:, n * TAIL:(n + 1) * TAIL], q[s][:, t * P:(t + 1) * P], k[s][:, 0:TAIL],
                                            start=True, stop=True)
            elif kind == "ent":
                for t in range(T):
                    last = nc.tensor.matmul(ps[:, t * TMAX:(t + 1) * TMAX], q[s][:, t * P:(t + 1) * P], pos[:, :],
                                            start=True, stop=True)
            elif kind == "body":
                t, h = divmod(i, 2)
                last = nc.tensor.matmul(ps[:, 0:BODY // 2], q[s][:, t * P:(t + 1) * P],
                                        k[s][:, TAIL + h * (BODY // 2):TAIL + (h + 1) * (BODY // 2)], start=True, stop=True)
            elif kind == "row":
                for n in range(4):
                    last = nc.tensor.matmul(ps[DH:DH + 1, n * P:(n + 1) * P], shift[s % 2][:, 4 * i + n:4 * i + n + 1],
                                            ident[:, :], start=True, stop=True)
            elif kind == "tt":
                part, half = divmod(i, 2)
                c0, c1 = (0, P) if part == 0 else (P, TAIL)
                for n in range(4):
                    last = nc.tensor.transpose(ps[0:c1 - c0, n * P:(n + 1) * P], f[s % 2][:, 4 * half + n, c0:c1], ident[:, :])
            elif kind == "sT":
                m, h = divmod(i, 2)
                last = nc.tensor.matmul(ps[:, :], k[s][:, m * P:(m + 1) * P], q[s][:, h * HB:(h + 1) * HB], start=True, stop=True)
            elif kind == "sum":
                for t in range(T):
                    last = nc.tensor.matmul(ps[:, t:t + 1], esum[:, t * P:(t + 1) * P], one[:, :], start=True, stop=True)
            elif kind == "out":
                for n in range(2):
                    t = 2 * i + n
                    last = nc.tensor.matmul(ps[:, n * D:(n + 1) * D], prod[:, t * P:(t + 1) * P], wout[s][:, :], start=True, stop=True)
            last.then_inc(s_fa if who == "act" else s_fd, 1)
            return last

        block = ctx.enter_context(nc.Block())

        def pair_place(it, s):
            if s < 2:
                n = it * 2 + 1
            else:
                n = ((it + 1) % (NPAIR // 2)) * 2
            return n // (H2 // 2), n % (H2 // 2)

        @block.tensor
        def _(pe):
            pe.wait_ge(s_const, 16 * 3)
            pe.wait_ge(s_set, N_SET2)
            w = Place(pe, "pro", 0)
            for g in pro_plan:
                for j in g:
                    if j[0] == "pq" and j[2] == 0:
                        pe.wait_ge(s_w, 48)
                    if j[0] == "tail" and j[2] == 0:
                        pe_need(w, "pro", ("pk", 0, 1, "act"))
                    pe_job(w, j, 0)
            with pe.Fori(0, NPAIR // 2) as it:
                w = Place(pe, "turn", it)
                for s in range(SLOTS):
                    for gi, g in enumerate(body_plan[s]):
                        for j in g:
                            if j[0] == "PV":
                                p = j[2]
                                pe_need(w, "turn", ("sT", s, 4 * p + 3, "act") if p else ("tt", s, 3, "act"))
                                if p == 0:
                                    w.head(s_copied, s, 1, 0)
                                for h in range(2):
                                    for e in range(2):
                                        last = nc.tensor.matmul(pv[e * DH:(e + 1) * DH, h * HB:(h + 1) * HB], v[s][:, 2 * p + e, :],
                                                                ex[(2 * p + e) % RING][:, h * HB:(h + 1) * HB],
                                                                start=(p == 0), stop=(p == T // 2 - 1))
                                last.then_inc(s_pvm, 1)
                                continue
                            if j[0] == "row" and j[2] == 0:
                                w.head(s_m, s, 1, 1)
                            if j[0] == "tt" and j[2] == 0:
                                w.head(s_xt, s, 1, 1)
                            if j[0] == "sT" and j[2] == 2:
                                pe_need(w, "turn", ("row", s, 1, "act"))
                            if j[0] == "pq" and j[2] == 0:
                                pe.wait_ge(s_w, it * (2 * 48) + 48 * (2 + s // 2))
                            if j[0] == "tail" and j[2] == 0:
                                if s % 2 == 0:
                                    pe_need(w, "turn", ("pk", (s + 2) % SLOTS, 1, "act"))
                                w.head(s_zero, s, 1, 0)
                            if j[0] == "out" and j[2] == 0:
                                pe.wait_ge(s_wo, it * (2 * 64) + 64 * (1 + s // 2))
                                w.head(s_copied, s, 1, 1)
                            if j[0] == "sum":
                                w.head(s_es, s, T - 1, T - 1)
                            b_of = pe.snap(pair_place(it, s)[0]) if j[0] in ("pq", "pk", "pv") else 0
                            pe_job(w, j, b_of)

        def act_read(w, j):
            b, n, _ = w.job(j)
            w.eng.wait_ge(s_fa, w.at("act", n))
            return bank[b]

        def act_job(w, j):
            kind, s, i, _ = j
            ps = act_read(w, j)
            half = slice(i % 2 * HB, (i % 2 + 1) * HB)
            if kind in ("pq", "pk"):
                dst, scale = (q, 1.0) if kind == "pq" else (k, DH ** -0.5)
                for e in range(2):
                    last = nc.scalar.activation(dst[s + e][0:DH, half], ps[e * DH:(e + 1) * DH, :], ACT.Copy, scale=scale)
            elif kind == "pv":
                last = nc.scalar.activation(vT[:, half], ps[:, :], ACT.Copy)
            elif kind == "vtr":
                for e in range(2):
                    last = nc.scalar.activation(v[s + e][:, 4 * i:4 * i + 4, :],
                                                ps[:, :].rearrange("p (n d) -> p n d", n=4)[:, :, e * DH:(e + 1) * DH], ACT.Copy)
            elif kind == "tail":
                t0, t1 = 3 * i, min(3 * i + 3, T)
                src = ps[:, 0:(t1 - t0) * TAIL].rearrange("p (t c) -> p t c", t=t1 - t0)
                nc.scalar.activation(gate[:, t0:t1, :], src, ACT.Tanh, scale=0.5)
                last = nc.scalar.activation(f[s % 2][:, t0:t1, :], src, ACT.Copy)
            elif kind == "ent":
                last = nc.scalar.activation(ent[s % 2][:, :, :], ps[:, :].rearrange("p (t c) -> p t c", t=T), ACT.Copy)
            elif kind == "row":
                last = nc.scalar.activation(q[s][DH:DH + 1, half], ps[DH:DH + 1, :], ACT.Copy)
            elif kind == "tt":
                if i < 2:
                    last = nc.scalar.activation(ex[0][:, half], ps[:, :], ACT.Copy)
                else:
                    last = nc.scalar.activation(ex[1][0:TAIL - P, half], ps[0:TAIL - P, :], ACT.Copy)
            elif kind == "sT":
                m = i // 2
                last = nc.scalar.activation(ex[m % RING][:, half], ps[:, :], ACT.Exp)
            last.then_inc(s_ra, 1)

        def groups_of_hinges(m):
            cuts = [0, 3, 5, 8, 11, 15, 19, len(HINGES), len(HINGES)]
            return range(cuts[m], cuts[m + 1])

        N_PART = N_POOL + 1
        OWN = [n for n in range(1, len(HINGES)) if n not in POOL]
        N_DVE = len(OWN)

        def buffer_free(w, s, n):
            p, before = n - N_RELU, 0
            if p < 0:
                if w.part == "pro":
                    return
                before = 1
                p = max(x for x in range(len(HINGES)) if x % N_RELU == n % N_RELU)
            if p == 0:
                w.head(s_part, s - before, N_PART, 1)
            elif p in POOL:
                w.head(s_padd, s - before, N_POOL, POOL.index(p) + 1)
            else:
                w.head(s_dadd, s - before, N_DVE, OWN.index(p) + 1)

        def act_hinges(w, s, m):
            for n in groups_of_hinges(m):
                l, a0, a1 = HINGES[n]
                if n == 0:
                    w.head(s_p, s, 1, 1)
                buffer_free(w, s, n)
                cols = (a1 - a0) * PER
                nc.scalar.activation(relu[n % N_RELU][:, 0:T * cols].rearrange("p (t c) -> p t c", t=T),
                                     above[:, :, a0 * PER:a1 * PER], ACT.Relu, bias=keep.minus[:, l:l + 1]).then_inc(s_relu, 1)

        def act_check(w, s):
            w.head(s_over, s, 1, 1)
            w.head(s_gate, s, 1, 1)
            nc.scalar.activation(gate[:, :, :], above[:, :, :], ACT.Relu, scale=-1.0, accum_out=breach[:, s % 2, 0:1]).then_inc(s_seen, 1)
            w.head(s_seen, s, 3, 1)
            nc.scalar.activation(gate[:, :, :], over[:, :, :], ACT.Relu, accum_out=breach[:, s % 2, 1:2]).then_inc(s_seen, 1)
            w.head(s_seen, s, 3, 2)
            nc.scalar.activation(gate[:, :, 0], above[:, :, TAIL - 1], ACT.Relu, scale=-1.0, bias=lack[:, :],
                                 accum_out=breach[:, s % 2, 2:3]).then_inc(s_seen, 1)

        def copy_products(w, s):
            w.head(s_pvm, s, T // 2, T // 2)
            n = read_count("turn", ("out", (s - 1) % SLOTS, OUTS - 1, "dve"))
            w.eng.wait_ge(s_rd, w.at("dve", n if s else n - n_turn["dve"]))
            nc.scalar.activation(prod[:, :], pv[:, :], ACT.Copy).then_inc(s_copied, 1)

        def ring_free(w, s, m):
            w.head(s_pvm, s, T // 2, (m - RING) // 2 + 1)
            w.head(s_es, s, T - 1, max(m - RING, 1) if m >= RING else m + 1 - RING)

        def tail_exp(w, s):
            w.head(s_m, s, 1, 1)
            for t in range(T):
                last = nc.scalar.activation(f[s % 2][:, t, :], f[s % 2][:, t, :], ACT.Exp, bias=nmax[s % 2][:, t:t + 1])
            last.then_inc(s_xt, 1)

        @block.scalar
        def _(act):
            act.wait_ge(s_set, N_SET2)
            w = Place(act, "pro", 0)
            for gi, g in enumerate(pro_plan):
                for j in g:
                    if j[3] == "act":
                        if j[0] == "tail" and j[1] == 1 and j[2] == 0:
                            act.wait_ge(s_gate, 1)
                            act.wait_ge(s_seen, 3)
                        act_job(w, j)
                if gi:
                    act_hinges(w, 0, gi - 1)
                if gi - 1 == CHECK_AT:
                    act_check(w, 0)
            tail_exp(w, 0)
            with act.Fori(0, NPAIR // 2) as it:
                w = Place(act, "turn", it)
                for s in range(SLOTS):
                    for gi, g in enumerate(body_plan[s]):
                        for j in g:
                            if j[0] == "PV" or j[3] != "act":
                                continue
                            if j[2] % 2 == 0 and (j[0] == "sT" or j[0] == "tt"):
                                ring_free(w, s, j[2] // 2)
                            if j[0] == "tail" and j[2] == 0:
                                act_hinges(w, s + 1, GROUPS - 2)
                                copy_products(w, s)
                            if j[0] == "tail" and j[2] == 0:
                                w.head(s_gate, s, 1, 2)
                                w.head(s_seen, s, 3, 6)
                            if j[0] == "tt" and j[2] == 2:
                                w.eng.wait_ge(s_ra, w.at("act", w.job(("sT", s, 3, "act"))[1]))
                            act_job(w, j)
                        if gi != GROUPS - 2:
                            act_hinges(w, s + 1, gi)
                        if gi == CHECK_AT:
                            act_check(w, s + 1)
                    nc.scalar.activation(q[s][DH:DH + 1, :], zero[DH:DH + 1, 0:1].to_broadcast([1, S]), ACT.Copy).then_inc(s_zero, 1)
                    tail_exp(w, s + 1)

        def low_of(tab, a0, a1, l):
            first = RISE * a0 + l
            return tab[:, :, first:RISE * (a1 - 1) + l + 1:RISE].rearrange("p t (a o) -> p t a o", o=1)\
                .to_broadcast([P, T, a1 - a0, PER])

        def blocks(ap, a0, a1):
            return ap[:, :, a0 * PER:a1 * PER].rearrange("p t (a r) -> p t a r", r=PER)

        def dve_first(w, s, part, link):
            e = s % 2
            if part == 0:
                w.eng.wait_ge(s_ra, after_copy(w, s, ("tail", s % SLOTS, 2, "act")))
                if s:
                    w.head(s_seen, s, 3, 0)
                    w.head(s_over, s, 1, 0)
                link(nc.vector.tensor_tensor_scan(above[:, :, :].rearrange("p t c -> p (t c)"),
                                                  carry[:, :, :].rearrange("p t c -> p (t c)"),
                                                  gate[:, :, :].rearrange("p t c -> p (t c)"), 0.0, ALU.mult, ALU.add))
                nc.vector.scalar_tensor_tensor(above[:, :, :], above[:, :, :], 0.5,
                                               table[:, 0:1, :].to_broadcast([P, T, TAIL]), ALU.mult, ALU.add).then_inc(s_p, 1)
            else:
                w.head(s_p, s, 1, 1)
                w.head(s_prep, s, 3, 3)
                link(nc.vector.tensor_tensor(blocks(gate, 0, BLOCKS), blocks(above, 0, BLOCKS), low_of(slope, 0, BLOCKS, 0), ALU.mult))
                nc.vector.tensor_tensor(f[e][:, :, :], f[e][:, :, :], gate[:, :, :], ALU.add).then_inc(s_gate, 1)
                w.head(s_gate, s, 1, 1)

        N_FIRST = 2

        def after_copy(w, s, j):
            if w.part == "pro":
                return w.at("act", info[("pro", j)][1])
            return w.at("act", info[("turn", j)][1] - (n_turn["act"] if s == 1 else 0))

        def dve_hinges(w, s, m, link):
            for n in groups_of_hinges(m):
                l, a0, a1 = HINGES[n]
                cols = (a1 - a0) * PER
                w.head(s_relu, s, len(HINGES), n + 1)
                line = relu[n % N_RELU][:, 0:T * cols]
                by_block = line.rearrange("p (t a r) -> p t a r", t=T, r=PER)
                if n not in OWN:
                    nc.vector.tensor_tensor(by_block if n else blocks(pieces, a0, a1), by_block,
                                            low_of(bend, a0, a1, l), ALU.mult).then_inc(s_part, 1)
                else:
                    link(nc.vector.tensor_tensor(by_block, by_block, low_of(bend, a0, a1, l), ALU.mult))
                    nc.vector.tensor_tensor(f[s % 2][:, :, a0 * PER:a1 * PER], f[s % 2][:, :, a0 * PER:a1 * PER],
                                            line.rearrange("p (t c) -> p t c", t=T), ALU.add).then_inc(s_dadd, 1)
                    w.head(s_dadd, s, N_DVE, OWN.index(n) + 1)

        def dve_full(w, j):
            b, n, _ = w.job(j)
            w.eng.wait_ge(s_fd, w.at("dve", n))
            return bank[b]

        def dve_job(w, j, rows_at=None):
            kind, s, i, _ = j
            ps = dve_full(w, j)
            if kind == "body":
                t, h = divmod(i, 2)
                last = nc.vector.reduce_max(bmax[:, t, h:h + 1], ps[:, 0:BODY // 2], AX)
            elif kind == "sum":
                last = nc.vector.reciprocal(rcol[:, :], ps[:, 0:T])
            elif kind == "out":
                for n in range(2):
                    row = rows[:, ds(rows_at[n], 1), :].rearrange("p o d -> p (o d)")
                    last = nc.vector.scalar_tensor_tensor(row, ps[:, n * D:(n + 1) * D], rcol[:, 2 * i + n:2 * i + n + 1], row,
                                                          ALU.mult, ALU.add)
            last.then_inc(s_rd, 1)

        def dve_last(w, s, link):
            e = s % 2
            w.head(s_padd, s, N_POOL, N_POOL)
            link(nc.vector.tensor_tensor(f[e][:, :, :], f[e][:, :, :], pieces[:, :, :], ALU.add))
            w.head(s_seen, s, 3, 3)
            nc.vector.tensor_tensor(found[:, :], found[:, :], breach[:, e, :], ALU.add)
            link(nc.vector.tensor_reduce(tmax[:, :], f[e][:, :, :], AX, ALU.max))
            w.eng.wait_ge(s_rd, w.at("dve", w.job(("body", s % SLOTS, 2 * T - 1, "dve"))[1]))
            link(nc.vector.tensor_tensor(bm[:, :], bmax[:, :, 0], bmax[:, :, 1], ALU.max))
            link(nc.vector.tensor_tensor(bm[:, :], bm[:, :], ent[e][:, :, TMAX - 1], ALU.add))
            link(nc.vector.tensor_tensor(bm[:, :], bm[:, :], tmax[:, :], ALU.max))
            link(nc.vector.tensor_scalar(nmax[e][:, :], bm[:, :], -1.0, None, ALU.mult))
            nc.vector.tensor_tensor(shift[e][:, :], ent[e][:, :, TMAX - 1], bm[:, :], ALU.subtract).then_inc(s_m, 1)

        N_LAST = 6
        per_head = N_FIRST + N_DVE + N_LAST

        @block.vector
        def _(dve):
            for s in range(SLOTS):
                nc.vector.memset(q[s][DH:P, :], 0.0).then_inc(s_set, 1)
                nc.vector.memset(k[s][DH:P, :], 0.0).then_inc(s_ones, 1)
            for ap, val in ((one[:, :], 1.0), (zero[:, :], 0.0), (slope[:, :, TMAX - 1:TMAX], 0.0),
                            (found[:, :], 0.0), (pos[DH:P, :], 0.0),
                            (lack[:, :], float(TMAX - 1 - RISE * (BLOCKS - 1)))):
                nc.vector.memset(ap, val).then_inc(s_set, 1)
            nc.vector.memset(carry[:, :, :], 1.0).then_inc(s_ones, 1)
            dve.wait_ge(s_ones, SLOTS + 1)
            for s in range(SLOTS):
                nc.vector.memset(k[s][DH:DH + 1, :], 1.0).then_inc(s_set, 1)
            nc.vector.memset(carry[:, :, 0:1], 0.0).then_inc(s_set, 1)
            dve.wait_ge(s_const, 16 * 3)
            dve.wait_ge(s_set, N_SET2)
            w = Place(dve, "pro", 0)
            chain = Count(dve, s_c)
            for gi, g in enumerate(pro_plan):
                if gi:
                    for j in g:
                        if j[3] == "dve":
                            dve_job(w, j)
                    if gi == 1:
                        dve_first(w, 0, 0, chain.link)
                        dve_first(w, 0, 1, chain.link)
                    dve_hinges(w, 0, gi - 1, chain.link)
            dve_last(w, 0, chain.link)
            dve_first(w, 1, 0, chain.link)
            assert chain.n == per_head + 1
            with dve.Fori(0, NPAIR // 2) as it:
                w = Place(dve, "turn", it)
                for s in range(SLOTS):
                    chain = Count(dve, s_c, it * (SLOTS * per_head) + (s + 1) * per_head + 1)
                    for gi, g in enumerate(body_plan[s]):
                        for j in g:
                            if j[0] == "body":
                                dve_job(w, j)
                        if gi == 0:
                            dve_first(w, s + 1, 1, chain.link)
                        dve_hinges(w, s + 1, gi, chain.link)
                        if gi == GROUPS - 2:
                            dve_last(w, s + 1, chain.link)
                    if s == 0:
                        dve.wait_ge(s_saved, 16)
                    j = ("sum", s, 0, "dve")
                    dve_job(w, j)
                    dve.wait_ge(s_rd, w.at("dve", read_count("turn", j)))
                    for i in range(OUTS):
                        dve_job(w, ("out", s, i, "dve"), [dve.snap(((it * 2 + s // 2) // (H2 // 2)) * T + 2 * i + n) for n in range(2)])
                    dve_first(w, s + 2, 0, chain.link)
            nc.vector.tensor_reduce(keep.excess[:, :], found[:, :], AX, ALU.max).then_inc(s_rev, 1)
            dve.wait_ge(s_rev, 1)

        @block.gpsimd
        def _(pool):
            def prepare(w, s):
                e = s % 2
                w.eng.wait_ge(s_ra, after_copy(w, s, ("ent", s % SLOTS, 0, "act")))
                if w.part == "turn":
                    w.head(s_dadd, s, N_DVE, 0)
                nc.gpsimd.tensor_tensor(slope[:, :, 0:TMAX - 1], ent[e][:, :, 1:TMAX], ent[e][:, :, 0:TMAX - 1],
                                        ALU.subtract).then_inc(s_prep, 1)
                w.head(s_prep, s, 3, 1)
                nc.gpsimd.tensor_tensor(bend[:, :, 1:TMAX], slope[:, :, 1:TMAX], slope[:, :, 0:TMAX - 1],
                                        ALU.subtract).then_inc(s_prep, 1)
                w.head(s_prep, s, 3, 2)
                nc.gpsimd.tensor_tensor(blocks(f[e], 0, BLOCKS), blocks(f[e], 0, BLOCKS), low_of(ent[e], 0, BLOCKS, 0),
                                        ALU.add).then_inc(s_prep, 1)

            def pool_hinges(w, s):
                w.head(s_p, s, 1, 1)
                if w.part == "turn":
                    w.head(s_seen, s, 3, 0)
                nc.gpsimd.tensor_tensor(over[:, :, :], above[:, :, :], table[:, 1:2, :].to_broadcast([P, T, TAIL]),
                                        ALU.subtract).then_inc(s_over, 1)
                for m in range(GROUPS):
                    for n in groups_of_hinges(m):
                        if n not in POOL:
                            continue
                        l, a0, a1 = HINGES[n]
                        i = POOL.index(n)
                        w.head(s_part, s, N_PART, i + 2)
                        if i:
                            w.head(s_padd, s, N_POOL, i)
                        cols = slice(a0 * PER, a1 * PER)
                        nc.gpsimd.tensor_tensor(pieces[:, :, cols], pieces[:, :, cols],
                                                relu[n % N_RELU][:, 0:T * (a1 - a0) * PER].rearrange("p (t c) -> p t c", t=T),
                                                ALU.add).then_inc(s_padd, 1)
                    if m and w.part == "turn":
                        add_exp(w, s - 1, m)

            def add_exp(w, s, m):
                w.eng.wait_ge(s_ra, w.at("act", info[("turn", ("tt", s, 3, "act") if m == 1 else ("sT", s, 2 * m + 1, "act"))][1]))
                if m == 1:
                    n = read_count("turn", ("sum", (s - 1) % SLOTS, 0, "dve"))
                    w.eng.wait_ge(s_rd, w.at("dve", n if s else n - n_turn["dve"]))
                    nc.gpsimd.tensor_tensor(esum[:, :], ex[0][:, :], ex[1][:, :], ALU.add).then_inc(s_es, 1)
                else:
                    w.head(s_es, s, T - 1, m - 1)
                    nc.gpsimd.tensor_tensor(esum[:, :], esum[:, :], ex[m % RING][:, :], ALU.add).then_inc(s_es, 1)

            pool.wait_ge(s_set, N_SET2)
            pool.wait_ge(s_const, 16 * 3)
            pool.sem_inc(s_zero, 1)
            pool.sem_inc(s_copied, 1)
            pool.sem_inc(s_pvm, T // 2)
            pool.sem_inc(s_es, T - 1)
            prepare(Place(pool, "pro", 0), 0)
            pool_hinges(Place(pool, "pro", 0), 0)
            with pool.Fori(0, NPAIR // 2) as it:
                w = Place(pool, "turn", it)
                for s in range(SLOTS):
                    prepare(w, s + 1)
                    pool_hinges(w, s + 1)

        def weights_used(s):
            if s == 2:
                return info[("turn", ("pv", 2, 1, "act"))][1]
            return info[("pro", ("pv", 0, 1, "act"))][1] - n_pro["act"]

        @block.sync
        def _(sp):
            sp.dma_start(saved.rearrange("(t p) d -> p t d", p=P), rows[:, :, :]).then_inc(s_saved, 16)
            sp.dma_start(pos[0:DH, :], a["L0_attn_pos_emb"]).then_inc(s_const, 16)
            sp.dma_start(table[:, :, :].rearrange("p a c -> p (a c)"), a["tables"].rearrange("a c -> (a c)").partition_broadcast(P)).then_inc(s_const, 16)
            sp.dma_start(keep.minus[:, :], a["minus"].partition_broadcast(P)).then_inc(s_const, 16)
            wq_r = a["L0_attn_Wq"].rearrange("(c p) n -> p c n", p=P)
            wkv_r = a["L0_attn_Wkv"].rearrange("(c p) n -> p c n", p=P)

            def pair_weights(col):
                for x, src, c in ((0, wq_r, col), (1, wkv_r, col), (2, wkv_r, col + H2 * DH)):
                    sp.dma_start(w_in[:, x, :, :], src[:, :, ds(c, P)]).then_inc(s_w, 16)

            def out_weights(even, odd, s):
                for e, at in enumerate((even, odd)):
                    for half in (slice(0, DH), slice(DH, P)):
                        sp.dma_start(wout[s + e][half, :], a["L0_attn_Wout"][ds(at, DH), :]).then_inc(s_wo, 16)

            pair_weights(0)
            out_weights(0, DH, 0)
            with sp.Fori(0, NPAIR // 2) as it:
                w = Place(sp, "turn", it)
                for s in (0, 2):
                    _, hp = pair_place(it, s)
                    col, odd = sp.snap(hp * P), sp.snap(hp * P + DH)
                    sp.wait_ge(s_ra, w.at("act", weights_used(s)))
                    pair_weights(col)
                    sp.wait_ge(s_ra, w.at("act", info[("turn", ("row", s, 1, "act"))][1]))
                    out_weights(col, odd, (s + 2) % SLOTS)
            sp.wait_ge(s_saved, 16)
            sp.wait_ge(s_wo, 64 * (NPAIR + 1))
            sp.wait_ge(s_w, 48 * (NPAIR + 1))


N_SET2 = 2 * SLOTS + 6 + 1


def verdict_stage(nc, keep):
    with ExitStack() as ctx:
        line = ctx.enter_context(nc.psum_tensor("line", [1, P], F32))
        low = ctx.enter_context(nc.sbuf_tensor("lowest", [1, 2], F32))
        s_line, s_low, s_is, s_flag = (ctx.enter_context(nc.semaphore(x)) for x in
                                       ("breach_in_line", "lowest_found", "breach_judged", "flag_set"))
        block = ctx.enter_context(nc.Block())

        @block.tensor
        def _(pe):
            nc.tensor.matmul(line[:, :], keep.excess[:, :], keep.ident[:, :], start=True, stop=True).then_inc(s_line, 1)

        @block.vector
        def _(dve):
            dve.wait_ge(s_line, 1)
            nc.vector.tensor_reduce(low[:, 0:1], line[:, :], AX, ALU.max).then_inc(s_low, 1)
            dve.wait_ge(s_low, 1)
            nc.vector.tensor_scalar(low[:, 1:2], low[:, 0:1], 0.0, None, ALU.is_gt).then_inc(s_is, 1)
            dve.wait_ge(s_is, 1)
            nc.vector.tensor_copy(keep.flag[:, :], low[:, 1:2]).then_inc(s_flag, 1)
            dve.wait_ge(s_flag, 1)


def general_cope_stage(nc, keep, a, saved):
    with ExitStack() as ctx:
        def sb(name, shape, dt=F32):
            return ctx.enter_context(nc.sbuf_tensor(name, shape, dt))

        def sem(name):
            return ctx.enter_context(nc.semaphore(name))

        rows, hT, ident = keep.rows, keep.hT, keep.ident
        w_in, wout = sb("gw_in", [P, 3, KC, P]), sb("gwout", [P, D])
        pos, number = sb("gpos", [DH, TMAX]), sb("gnumber", [P, TMAX])
        q, k = [sb(f"gq{e}", [DH, S]) for e in range(2)], [sb(f"gk{e}", [DH, S]) for e in range(2)]
        vT, v = sb("gvT", [P, S]), sb("gv", [P, T, P])
        qt, ent, slope = sb("gqt", [DH, P]), sb("gent", [P, TMAX]), sb("gslope", [P, TMAX])
        gate, p, f, part, ones = (sb(n, [P, S]) for n in ("ggate", "gp", "gf", "gpart", "gones"))
        prob, probT = sb("gprob", [P, S]), sb("gprobT", [P, T, P])
        top, ntop, total, recip = (sb(n, [P, 1]) for n in ("gtop", "gntop", "gtotal", "grecip"))
        o, oT = sb("go", [P, P]), sb("goT", [P, P])

        bank = [ctx.enter_context(nc.psum_tensor(f"gbank{i}", [P, HB], F32)) for i in range(8)]
        s_const, s_w, s_set = sem("g_consts_in"), sem("g_weights_in"), sem("g_set")
        s_pj, s_pjc, s_vt, s_vc = sem("g_projected"), sem("g_qkv_copied"), sem("g_v_turned"), sem("g_v_copied")
        s_qt, s_sc, s_cp, s_f, s_c = sem("g_q_tile"), sem("g_scores"), sem("g_scores_copied"), sem("g_max"), sem("g_dve_chain")
        s_ex, s_nr, s_tp, s_tc = sem("g_exp"), sem("g_normalised"), sem("g_probs_turned"), sem("g_probsT_copied")
        s_o, s_oc, s_at, s_ac = sem("g_product"), sem("g_product_copied"), sem("g_product_turned"), sem("g_productT_copied")
        s_y, s_add = sem("g_out"), sem("g_added")

        block = ctx.enter_context(nc.Block())
        PB = H2 // 2
        CHAIN = 5 + 3 * (TMAX - 1) + 3

        @block.gpsimd
        def _(pool):
            pool.sem_inc(s_add, 1)
            pool.sem_inc(s_oc, 1)

        @block.sync
        def _(sp):
            flag = sp.value_load(keep.flag[0:1, 0:1], min_val=0, max_val=1)
            with sp.If(flag == 1):
                sp.dma_start(pos[:, :], a["L0_attn_pos_emb"]).then_inc(s_const, 16)
                sp.dma_start(number[:, :], a["number"].partition_broadcast(P)).then_inc(s_const, 16)
                sp.dma_start(rows[:, :, :], saved.rearrange("(t p) d -> p t d", p=P)).then_inc(s_const, 16)
                wq_r = a["L0_attn_Wq"].rearrange("(c p) n -> p c n", p=P)
                wkv_r = a["L0_attn_Wkv"].rearrange("(c p) n -> p c n", p=P)
                with sp.Fori(0, B) as b:
                    with sp.Fori(0, PB) as hp:
                        col = sp.snap(hp * P)
                        colv = sp.snap(hp * P + H2 * DH)
                        sp.wait_ge(s_add, (b * PB + hp) * T + 1)
                        sp.dma_start(w_in[:, 0, :, :], wq_r[:, :, ds(col, P)]).then_inc(s_w, 16)
                        sp.dma_start(w_in[:, 1, :, :], wkv_r[:, :, ds(col, P)]).then_inc(s_w, 16)
                        sp.dma_start(w_in[:, 2, :, :], wkv_r[:, :, ds(colv, P)]).then_inc(s_w, 16)
                        sp.dma_start(wout[:, :], a["L0_attn_Wout"][ds(col, P), :]).then_inc(s_w, 16)
            with sp.Else():
                sp.nop()

        @block.tensor
        def _(pe):
            flag = pe.value_load(keep.flag[0:1, 0:1], min_val=0, max_val=1)
            with pe.If(flag == 1):
                pe.wait_ge(s_const, 48)
                with pe.Fori(0, B) as b:
                    with pe.Fori(0, PB) as hp:
                        pe.wait_ge(s_w, (b * PB + hp) * 64 + 64)
                        for x in range(3):
                            for h in range(2):
                                for c in range(KC):
                                    last = nc.tensor.matmul(bank[2 * x + h][:, :], w_in[:, x, c, :], hT[:, c, ds(b * S + h * HB, HB)],
                                                            start=(c == 0), stop=(c == KC - 1))
                        last.then_inc(s_pj, 1)
                        pe.wait_ge(s_pjc, (b * PB + hp) + 1)
                        for t in range(T):
                            last = nc.tensor.transpose(bank[t // 4][:, t % 4 * P:(t % 4 + 1) * P], vT[:, t * P:(t + 1) * P], ident[:, :])
                        last.then_inc(s_vt, 1)
                        with pe.Fori(0, T) as i:
                            pe.wait_ge(s_vc, (b * PB + hp) + 1)
                            for e in range(2):
                                n = ((b * PB + hp) * T + i) * 2 + e
                                pe.wait_ge(s_qt, n + 1)
                                for h in range(2):
                                    nc.tensor.matmul(bank[h][:, :], qt[:, :], k[e][:, h * HB:(h + 1) * HB], start=True, stop=True)
                                nc.tensor.matmul(bank[2][:, 0:TMAX], qt[:, :], pos[:, :], start=True, stop=True).then_inc(s_sc, 1)
                                pe.wait_ge(s_nr, n + 1)
                                for t in range(T):
                                    last = nc.tensor.transpose(bank[3 + t // 4][:, t % 4 * P:(t % 4 + 1) * P],
                                                               prob[:, t * P:(t + 1) * P], ident[:, :])
                                last.then_inc(s_tp, 1)
                                pe.wait_ge(s_tc, n + 1)
                                for t in range(T):
                                    last = nc.tensor.matmul(bank[5][:, 0:DH], probT[:, t, :], v[:, t, e * DH:(e + 1) * DH],
                                                            start=(t == 0), stop=(t == T - 1))
                                last.then_inc(s_o, 1)
                            m = (b * PB + hp) * T + i
                            pe.wait_ge(s_oc, m * 2 + 3)
                            nc.tensor.transpose(bank[6][:, 0:P], o[:, :], ident[:, :]).then_inc(s_at, 1)
                            pe.wait_ge(s_ac, m + 1)
                            nc.tensor.matmul(bank[7][:, 0:D], oT[:, :], wout[:, :], start=True, stop=True).then_inc(s_y, 1)
                            pe.wait_ge(s_add, m + 2)
            with pe.Else():
                pe.nop()

        @block.scalar
        def _(act):
            flag = act.value_load(keep.flag[0:1, 0:1], min_val=0, max_val=1)
            with act.If(flag == 1):
                with act.Fori(0, B) as b:
                    with act.Fori(0, PB) as hp:
                        act.wait_ge(s_pj, (b * PB + hp) + 1)
                        for h in range(2):
                            half = slice(h * HB, (h + 1) * HB)
                            for e in range(2):
                                nc.scalar.activation(q[e][:, half], bank[h][e * DH:(e + 1) * DH, :], ACT.Copy)
                                nc.scalar.activation(k[e][:, half], bank[2 + h][e * DH:(e + 1) * DH, :], ACT.Copy, scale=DH ** -0.5)
                            last = nc.scalar.activation(vT[:, half], bank[4 + h][:, :], ACT.Copy)
                        last.then_inc(s_pjc, 1)
                        act.wait_ge(s_pjc, (b * PB + hp) + 1)
                        act.wait_ge(s_vt, (b * PB + hp) + 1)
                        for h in range(2):
                            last = nc.scalar.activation(v[:, 4 * h:4 * h + 4, :], bank[h][:, :].rearrange("p (t d) -> p t d", t=4), ACT.Copy)
                        last.then_inc(s_vc, 1)
                        with act.Fori(0, T) as i:
                            for e in range(2):
                                n = ((b * PB + hp) * T + i) * 2 + e
                                act.wait_ge(s_oc, n + 1)
                                nc.scalar.activation(qt[:, :], q[e][:, ds(i * P, P)], ACT.Copy).then_inc(s_qt, 1)
                                act.wait_ge(s_sc, n + 1)
                                for h in range(2):
                                    half = slice(h * HB, (h + 1) * HB)
                                    nc.scalar.activation(gate[:, half], bank[h][:, :], ACT.Tanh, scale=0.5)
                                    nc.scalar.activation(f[:, half], bank[h][:, :], ACT.Copy)
                                nc.scalar.activation(ent[:, :], bank[2][:, 0:TMAX], ACT.Copy).then_inc(s_cp, 1)
                                act.wait_ge(s_f, n + 1)
                                nc.scalar.activation(prob[:, :], f[:, :], ACT.Exp, bias=ntop[:, :], accum_out=total[:, :]).then_inc(s_ex, 1)
                                act.wait_ge(s_tp, n + 1)
                                for h in range(2):
                                    last = nc.scalar.activation(probT[:, 4 * h:4 * h + 4, :], bank[3 + h][:, :].rearrange("p (t d) -> p t d", t=4), ACT.Copy)
                                last.then_inc(s_tc, 1)
                                act.wait_ge(s_o, n + 1)
                                nc.scalar.activation(o[:, e * DH:(e + 1) * DH], bank[5][:, 0:DH], ACT.Copy).then_inc(s_oc, 1)
                            m = (b * PB + hp) * T + i
                            act.wait_ge(s_at, m + 1)
                            nc.scalar.activation(oT[:, :], bank[6][:, 0:P], ACT.Copy).then_inc(s_ac, 1)
            with act.Else():
                act.nop()

        @block.vector
        def _(dve):
            flag = dve.value_load(keep.flag[0:1, 0:1], min_val=0, max_val=1)
            with dve.If(flag == 1):
                nc.vector.memset(ones[:, :], 1.0).then_inc(s_set, 1)
                dve.wait_ge(s_set, 1)
                dve.wait_ge(s_const, 48)
                with dve.Fori(0, B) as b:
                    with dve.Fori(0, PB) as hp:
                        with dve.Fori(0, T) as i:
                            for e in range(2):
                                n = ((b * PB + hp) * T + i) * 2 + e
                                dve.wait_ge(s_cp, n + 1)
                                chain = Count(dve, s_c, n * CHAIN)
                                chain.link(nc.vector.tensor_scalar(gate[:, :], gate[:, :], 0.5, 0.5, ALU.mult, ALU.add))
                                chain.link(nc.vector.tensor_tensor_scan(p[:, :], ones[:, :], gate[:, :], 0.0, ALU.mult, ALU.add))
                                chain.link(nc.vector.tensor_scalar(p[:, :], p[:, :], float(TMAX - 1), None, ALU.min))
                                chain.link(nc.vector.tensor_tensor(slope[:, 0:TMAX - 1], ent[:, 1:TMAX], ent[:, 0:TMAX - 1], ALU.subtract))
                                chain.inc(nc.vector.tensor_scalar(f[:, :], f[:, :], ent[:, 0:1], None, ALU.add))
                                with dve.Fori(0, TMAX - 1) as j:
                                    hinge = Count(dve, s_c, n * CHAIN + 5 + j * 3)
                                    dve.wait_ge(s_c, n * CHAIN + 5 + j * 3)
                                    hinge.link(nc.vector.tensor_scalar(part[:, :], p[:, :], number[:, ds(j, 1)], 0.0, ALU.subtract, ALU.max))
                                    hinge.link(nc.vector.tensor_scalar(part[:, :], part[:, :], 1.0, slope[:, ds(j, 1)], ALU.min, ALU.mult))
                                    hinge.inc(nc.vector.tensor_tensor(f[:, :], f[:, :], part[:, :], ALU.add))
                                chain.n += 3 * (TMAX - 1)
                                dve.wait_ge(s_c, n * CHAIN + 5 + 3 * (TMAX - 1))
                                chain.link(nc.vector.reduce_max(top[:, :], f[:, :], AX))
                                nc.vector.tensor_scalar(ntop[:, :], top[:, :], -1.0, None, ALU.mult).then_inc(s_f, 1)
                                dve.wait_ge(s_ex, n + 1)
                                chain.link(nc.vector.reciprocal(recip[:, :], total[:, :]))
                                chain.link(nc.vector.tensor_copy(part[:, 0:1], recip[:, :]))
                                nc.vector.tensor_scalar(prob[:, :], prob[:, :], recip[:, :], None, ALU.mult).then_inc(s_nr, 1)
                                assert chain.n == CHAIN
                            m = (b * PB + hp) * T + i
                            at = dve.snap(b * T + i)
                            dve.wait_ge(s_y, m + 1)
                            nc.vector.tensor_tensor(rows[:, ds(at, 1), :].rearrange("p o d -> p (o d)"),
                                                    rows[:, ds(at, 1), :].rearrange("p o d -> p (o d)"), bank[7][:, 0:D], ALU.add).then_inc(s_add, 1)
            with dve.Else():
                dve.nop()


def route_stage(nc, keep, a, xp):
    with ExitStack() as ctx:
        def sb(name, shape, dt=F32):
            return ctx.enter_context(nc.sbuf_tensor(name, shape, dt))

        def sem(name):
            return ctx.enter_context(nc.semaphore(name))

        rows = keep.rows
        normed = sb("normed", [P, NT, D])
        n = sb("n3", [P, T, D])
        nT = sb("nT3", [P, KC, S])
        rw = sb("rw", [P, KC, E])
        experts = sb("experts", [P, E])
        upto = sb("upto", [P, P])
        ones = sb("ones3", [P, P])
        logit, best = sb("logit", [P, T, E]), sb("best", [P, T, 8])
        best_i, best_f = sb("best_i", [P, T, 8], U32), sb("best_f", [P, T, TOPK])
        diff, ratio, den = sb("diff", [P, T]), sb("ratio", [P, T]), sb("den", [P, T])
        hot = [sb(f"hot{i}", [P, NT, E]) for i in range(TOPK)]
        both = sb("both", [P, NT, E])
        before, total = sb("before", [P, NT, E]), sb("total", [P, NT, E])
        run = sb("run", [P, E, NT])
        ends = sb("ends", [P, E])
        one_nt = sb("one_nt", [P, NT])
        picked = sb("picked", [P, NT, E])
        place_f = sb("place_f", [P, TOPK, NT])
        stats, mv, rstd = sb("stats3", [P, T, 6]), sb("mv3", [P, T, 2]), sb("rstd3", [P, T])
        work = [ctx.enter_context(nc.psum_tensor(f"work3_{i}", [P, HB], F32)) for i in range(4)]
        plog = ctx.enter_context(nc.psum_tensor("plog", [P, HB], F32))
        pcount = [ctx.enter_context(nc.psum_tensor(f"pcount{i}", [P, HB], F32)) for i in range(2)]

        s_in, s_set, s_var, s_root, s_c = sem("router_in"), sem("set3"), sem("var3"), sem("root3"), sem("dve_chain3")
        s_n, s_tr, s_nT, s_log = sem("n3_ready"), sem("transposed3"), sem("nT3_ready"), sem("logits_ready")
        s_e, s_ed, s_sel, s_cnt, s_place = (sem("diff_ready"), sem("ratio_ready"), sem("chosen"), sem("counted"), sem("places_ready"))
        s_sc, s_tri = sem("rows_scattered"), sem("upto_set")

        block = ctx.enter_context(nc.Block())

        @block.sync
        def _(sp):
            with nc.allow_non_contiguous_dma(reason="the router's weights, transposed: 8 KB"):
                for c in range(KC):
                    sp.dma_start(rw[:, c, :], a["L0_ffn_router_w"][:, c * P:(c + 1) * P].rearrange("e p -> p e")).then_inc(s_in, 16)

        @block.gpsimd
        def _(pool):
            nc.gpsimd.memset(ones[:, :], 1.0).then_inc(s_set, 1)
            nc.gpsimd.memset(upto[:, :], 1.0).then_inc(s_set, 1)
            nc.gpsimd.memset(one_nt[:, :], 1.0).then_inc(s_set, 1)
            nc.gpsimd.iota(experts[:, :], pattern=[[1, E]], base=0, channel_multiplier=0,
                           allow_small_or_imprecise_dtypes=True).then_inc(s_set, 1)
            pool.wait_ge(s_set, 4)
            pool.sem_inc(s_nT, 1)
            pool.sem_inc(s_e, 1)
            nc.gpsimd.affine_select(out=upto[:, :], in_=upto[:, :], compare_op=ALU.is_ge, fill=0.0, base=0,
                                    pattern=[[1, P]], channel_multiplier=-1).then_inc(s_tri, 1)
            pool.wait_ge(s_place, 1)
            for t in range(NT):
                for i in range(TOPK):
                    pool.indirect_dma_start(xp, bass.IndirectOffsetOnAxis(ap=keep.place[:, i, t:t + 1], axis=0),
                                            normed[:, t, :], None).then_inc(s_sc, 16)
            pool.wait_ge(s_sc, 16 * NT * TOPK)

        @block.vector
        def _(dve):
            dve.wait_ge(s_set, 4)
            links = 8
            with dve.Fori(0, B) as b:
                chain = Count(dve, s_c, b * links)
                tiles = ds(b * T, T)

                def root(last):
                    last.then_inc(s_var, 1)
                    dve.wait_ge(s_root, b + 1)

                chain.link(nc.vector.tensor_copy(n[:, :, :], rows[:, tiles, :]))
                layernorm_rows(nc, chain.link, lambda last: last.then_inc(s_n, 1), n, n, T, stats, mv, rstd, root,
                               lambda: nc.vector.tensor_copy(rstd[:, 0:1], stats[:, T - 1, 0:1]))
                dve.wait_ge(s_n, b + 1)
                nc.vector.tensor_copy(normed[:, tiles, :], n[:, :, :])
                dve.wait_ge(s_log, b + 1)
                chain.link(nc.vector.tensor_copy(logit[:, :, :], plog[:, 0:T * E].rearrange("p (t e) -> p t e", t=T)))
                nc.vector.tensor_copy(den[:, 0:1], logit[:, T - 1, 0:1])
                for t in range(T):
                    last = nc.vector.max(best[:, t, :], logit[:, t, :])
                chain.link(last)
                nc.vector.tensor_copy(den[:, 0:1], best[:, T - 1, 0:1])
                for t in range(T):
                    last = nc.vector.max_index(best_i[:, t, :], best[:, t, :], logit[:, t, :])
                nc.vector.tensor_tensor(diff[:, :], best[:, :, 1], best[:, :, 0], ALU.subtract).then_inc(s_e, 1)
                dve.wait_ge(s_e, b + 2)
                chain.link(nc.vector.tensor_copy(best_f[:, :, :], best_i[:, :, 0:TOPK]))
                for i in range(TOPK):
                    last = nc.vector.tensor_tensor(hot[i][:, tiles, :], experts[:, :].rearrange("p (o e) -> p o e", o=1).to_broadcast([P, T, E]),
                                                   best_f[:, :, i:i + 1].to_broadcast([P, T, E]), ALU.is_equal)
                dve.wait_ge(s_ed, b + 1)
                chain.link(nc.vector.tensor_scalar(den[:, :], ratio[:, :], 1.0, None, ALU.add))
                chain.link(nc.vector.reciprocal(den[:, :], den[:, :]))
                nc.vector.tensor_copy(keep.weight[:, 0:1, tiles].rearrange("p o t -> p (o t)"), den[:, :])
                nc.vector.tensor_tensor(keep.weight[:, 1:2, tiles].rearrange("p o t -> p (o t)"), den[:, :], ratio[:, :], ALU.mult)
                assert chain.n == links
            chain = Count(dve, s_c, B * links)
            nc.vector.tensor_tensor(both[:, :, :], hot[0][:, :, :], hot[1][:, :, :], ALU.add).then_inc(s_sel, 1)
            dve.wait_ge(s_cnt, 1)
            nc.vector.tensor_copy(before[:, :, :], pcount[0][:, 0:NT * E].rearrange("p (t e) -> p t e", t=NT))
            chain.link(nc.vector.tensor_copy(total[:, :, :], pcount[1][:, 0:NT * E].rearrange("p (t e) -> p t e", t=NT)))
            for e in range(E):
                last = nc.vector.tensor_tensor_scan(run[:, e, :], one_nt[:, :], total[:, :, e], 0.0, ALU.mult, ALU.add)
            chain.link(last)
            chain.link(nc.vector.tensor_tensor_scan(ends[:, :], one_nt[:, 0:E], run[:, :, NT - 1], 0.0, ALU.mult, ALU.add))
            chain.link(nc.vector.tensor_tensor(before[:, :, :], before[:, :, :], total[:, :, :], ALU.subtract))
            chain.link(nc.vector.tensor_tensor(before[:, :, :], before[:, :, :], run[:, :, :].rearrange("p e t -> p t e"), ALU.add))
            chain.link(nc.vector.tensor_tensor(before[:, :, :], ends[:, :].rearrange("p (o e) -> p o e", o=1).to_broadcast([P, NT, E]),
                                               before[:, :, :], ALU.subtract))
            for i in range(TOPK):
                chain.link(nc.vector.tensor_tensor(picked[:, :, :], hot[i][:, :, :], before[:, :, :], ALU.mult))
                chain.link(nc.vector.tensor_reduce(place_f[:, i, :], picked[:, :, :], AX, ALU.add))
            nc.vector.tensor_copy(keep.place[:, :, :], place_f[:, :, :]).then_inc(s_place, 1)

        @block.scalar
        def _(act):
            with act.Fori(0, B) as b:
                act.wait_ge(s_var, b + 1)
                nc.scalar.activation(rstd[:, :], mv[:, :, 1], ACT.Sqrt, bias=keep.eps[:, :]).then_inc(s_root, 1)
                for i in range(4):
                    c, h = divmod(i, 2)
                    act.wait_ge(s_tr, b * 4 + i + 1)
                    nc.scalar.activation(nT[:, c, h * HB:(h + 1) * HB], work[i][:, :], ACT.Copy).then_inc(s_nT, 1)
                act.wait_ge(s_e, b + 2)
                nc.scalar.activation(ratio[:, :], diff[:, :], ACT.Exp).then_inc(s_ed, 1)

        @block.tensor
        def _(pe):
            pe.wait_ge(s_in, 16 * KC)
            pe.wait_ge(s_tri, 1)
            pe.wait_ge(s_set, 4)
            with pe.Fori(0, B) as b:
                pe.wait_ge(s_n, b + 1)
                pe.wait_ge(s_nT, b * 4 + 1)
                for i in range(4):
                    c, h = divmod(i, 2)
                    for j in range(4):
                        last = nc.tensor.transpose(work[i][:, j * P:(j + 1) * P], n[:, 4 * h + j, c * P:(c + 1) * P], keep.ident[:, :])
                    last.then_inc(s_tr, 1)
                pe.wait_ge(s_nT, b * 4 + 5)
                pe.wait_ge(s_e, b + 1)
                for t in range(T):
                    for c in range(KC):
                        last = nc.tensor.matmul(plog[:, t * E:(t + 1) * E], nT[:, c, t * P:(t + 1) * P], rw[:, c, :],
                                                start=(c == 0), stop=(c == KC - 1))
                last.then_inc(s_log, 1)
            pe.wait_ge(s_sel, 1)
            nc.tensor.matmul(pcount[0][:, 0:NT * E], upto[:, :], both[:, :, :].rearrange("p t e -> p (t e)"), start=True, stop=True)
            nc.tensor.matmul(pcount[1][:, 0:NT * E], ones[:, :], both[:, :, :].rearrange("p t e -> p (t e)"),
                             start=True, stop=True).then_inc(s_cnt, 1)


def expert_stage(nc, keep, a, xp, yp):
    with ExitStack() as ctx:
        def sb(name, shape, dt=F32):
            return ctx.enter_context(nc.sbuf_tensor(name, shape, dt))

        def sem(name):
            return ctx.enter_context(nc.semaphore(name))

        CR = NR // E
        CT = CR // P
        x = [sb(f"x4_{i}", [P, CT, D]) for i in range(2)]
        xT = sb("xT4", [P, KC, CR])
        w1 = [sb(f"w1_{i}", [P, KC, FF]) for i in range(2)]
        w2 = [sb(f"w2_{i}", [P, FC, D]) for i in range(2)]
        hT = sb("hT4", [P, FC, CR])
        y = [sb(f"y4_{i}", [P, CT, D]) for i in range(2)]
        pt = [ctx.enter_context(nc.psum_tensor(f"pt{i}", [P, HB], F32)) for i in range(2)]
        ph = [ctx.enter_context(nc.psum_tensor(f"ph{i}", [P, HB], F32)) for i in range(3)]
        py = [ctx.enter_context(nc.psum_tensor(f"py{i}", [P, HB], F32)) for i in range(3)]
        s_in = [sem(f"expert_in{i}") for i in range(2)]
        s_tr, s_xT, s_h, s_g, s_y, s_ys, s_out = (sem("x_transposed"), sem("xT_ready"), sem("h_ready4"), sem("gelu_ready"),
                                                  sem("y_ready"), sem("y_copied"), sem("y_written"))
        s_free = sem("y_buffer_free")
        NH, NY = FC * CR // HB, CT // 2
        block = ctx.enter_context(nc.Block())
        xv = xp.rearrange("(e t p) d -> e p t d", p=P, t=CT)
        yv = yp.rearrange("(e t p) d -> e p t d", p=P, t=CT)

        @block.sync
        def _(sp):
            def load(e, i):
                at = slice(e, e + 1) if isinstance(e, int) else ds(e, 1)
                sp.dma_start(x[i][:, :, :], xv[at].rearrange("o p t d -> p (o t) d")).then_inc(s_in[i], 16)
                sp.dma_start(w1[i][:, :, :], a["L0_ffn_w1"][at].rearrange("o (c p) f -> p (o c) f", p=P)).then_inc(s_in[i], 16)
                sp.dma_start(w2[i][:, :, :], a["L0_ffn_w2"][at].rearrange("o (c p) f -> p (o c) f", p=P)).then_inc(s_in[i], 16)

            load(0, 0)
            load(1, 1)
            with sp.Fori(0, E // 2 - 1) as it:
                for i in range(2):
                    e = sp.snap(it * 2 + i + 2)
                    sp.wait_ge(s_ys, it * (2 * NY) + (i + 1) * NY + 1)
                    load(e, i)

        @block.gpsimd
        def _(pool):
            for s in (s_xT, s_g, s_y, s_ys):
                pool.sem_inc(s, 1)
            pool.sem_inc(s_free, 2)
            with pool.Fori(0, E // 2) as it:
                for i in range(2):
                    e = pool.snap(it * 2 + i)
                    pool.wait_ge(s_ys, it * (2 * NY) + (i + 1) * NY + 1)
                    pool.dma_start(yv[ds(e, 1)].rearrange("o p t d -> p (o t) d"), y[i][:, :, :]).then_inc(s_out, 16)
                    pool.wait_ge(s_out, it * 32 + (i + 1) * 16)
                    pool.sem_inc(s_free, 1)
            pool.wait_ge(s_out, 16 * E)

        @block.tensor
        def _(pe):
            with pe.Fori(0, E // 2) as it:
                for i in range(2):
                    pe.wait_ge(s_in[i], it * 48 + 48)
                    nx, nh, ny = it * 8 + i * 4, it * (2 * NH) + i * NH, it * (2 * NY) + i * NY
                    for j in range(4):
                        c, h = divmod(j, 2)
                        pe.wait_ge(s_xT, nx + max(j - 1, 0) + 1)
                        for k in range(4):
                            last = nc.tensor.transpose(pt[j % 2][:, k * P:(k + 1) * P], x[i][:, 4 * h + k, c * P:(c + 1) * P], keep.ident[:, :])
                        last.then_inc(s_tr, 1)
                    pe.wait_ge(s_xT, nx + 4 + 1)
                    for j in range(NH):
                        f, h = divmod(j, CR // HB)
                        pe.wait_ge(s_g, nh + max(j - 2, 0) + 1)
                        for c in range(KC):
                            last = nc.tensor.matmul(ph[j % 3][:, :], w1[i][:, c, f * P:(f + 1) * P], xT[:, c, h * HB:(h + 1) * HB],
                                                    start=(c == 0), stop=(c == KC - 1))
                        last.then_inc(s_h, 1)
                    pe.wait_ge(s_g, nh + NH + 1)
                    for j in range(NY):
                        pe.wait_ge(s_ys, ny + max(j - 2, 0) + 1)
                        for k in range(2):
                            t = 2 * j + k
                            for f in range(FC):
                                last = nc.tensor.matmul(py[j % 3][:, k * D:(k + 1) * D], hT[:, f, t * P:(t + 1) * P], w2[i][:, f, :],
                                                        start=(f == 0), stop=(f == FC - 1))
                        last.then_inc(s_y, 1)

        @block.scalar
        def _(act):
            with act.Fori(0, E // 2) as it:
                for i in range(2):
                    nh, ny = it * (2 * NH) + i * NH, it * (2 * NY) + i * NY
                    act.wait_ge(s_y, ny + 1)
                    for j in range(NH):
                        f, h = divmod(j, CR // HB)
                        act.wait_ge(s_h, nh + j + 1)
                        nc.scalar.activation(hT[:, f, h * HB:(h + 1) * HB], ph[j % 3][:, :], ACT.Gelu).then_inc(s_g, 1)

        @block.vector
        def _(dve):
            with dve.Fori(0, E // 2) as it:
                for i in range(2):
                    nx, ny = it * 8 + i * 4, it * (2 * NY) + i * NY
                    for j in range(4):
                        c, h = divmod(j, 2)
                        dve.wait_ge(s_tr, nx + j + 1)
                        nc.vector.tensor_copy(xT[:, c, h * HB:(h + 1) * HB], pt[j % 2][:, :]).then_inc(s_xT, 1)
                    dve.wait_ge(s_free, it * 2 + i + 1)
                    for j in range(NY):
                        dve.wait_ge(s_y, ny + j + 2)
                        nc.vector.tensor_copy(y[i][:, 2 * j:2 * j + 2, :], py[j % 3][:, :].rearrange("p (k d) -> p k d", k=2)).then_inc(s_ys, 1)


def combine_stage(nc, keep, yp, out):
    with ExitStack() as ctx:
        RG = 6
        got = [ctx.enter_context(nc.sbuf_tensor(f"got{i}", [P, TOPK, D], F32)) for i in range(RG)]
        s_got = [ctx.enter_context(nc.semaphore(f"gathered{i}")) for i in range(RG)]
        s_sum, s_first, s_out = (ctx.enter_context(nc.semaphore(x)) for x in ("summed", "first_added", "out_written"))
        block = ctx.enter_context(nc.Block())

        @block.gpsimd
        def _(pool):
            for t in range(NT):
                if t >= RG:
                    pool.wait_ge(s_sum, t - RG + 1)
                for i in range(TOPK):
                    pool.indirect_dma_start(got[t % RG][:, i, :], None, yp,
                                            bass.IndirectOffsetOnAxis(ap=keep.place[:, i, t:t + 1], axis=0)).then_inc(s_got[t % RG], 16)

        @block.vector
        def _(dve):
            for t in range(NT):
                dve.wait_ge(s_got[t % RG], 32 * (t // RG + 1))
                row = keep.rows[:, t, :]
                nc.vector.scalar_tensor_tensor(row, got[t % RG][:, 0, :], keep.weight[:, 0, t:t + 1], row, ALU.mult, ALU.add).then_inc(s_first, 1)
                dve.wait_ge(s_first, t + 1)
                nc.vector.scalar_tensor_tensor(row, got[t % RG][:, 1, :], keep.weight[:, 1, t:t + 1], row, ALU.mult, ALU.add).then_inc(s_sum, 1)

        @block.sync
        def _(sp):
            for t in range(0, NT, 4):
                sp.wait_ge(s_sum, t + 4)
                sp.dma_start(out[t * P:(t + 4) * P, :].rearrange("(t p) d -> p t d", p=P), keep.rows[:, t:t + 4, :]).then_inc(s_out, 16)
            sp.wait_ge(s_out, 16 * (NT // 4))


class Keep:
    pass


def program(nc, a, out):
    with ExitStack() as ctx:
        def sb(name, shape, dt=F32):
            return ctx.enter_context(nc.sbuf_tensor(name, shape, dt))

        keep = Keep()
        keep.ident = sb("ident", [P, P])
        keep.eps = sb("eps", [P, 1])
        keep.excess = sb("excess", [P, 1])
        keep.minus = sb("minus", [P, 32])
        keep.flag = sb("flag", [1, 1], I32)
        keep.rows = sb("rows", [P, NT, D])
        with nc.sbuf_tensor("hT", [P, KC, R], F32) as keep.hT:
            constants(nc, keep)
            token_stage(nc, keep, a["ids"], a["L0_tok_emb_table"], a["pos"], a["L0_tok_Wq"], a["L0_tok_bq"],
                        a["L0_tok_Wk"], a["L0_tok_bk"], a["L0_tok_Wv"], a["L0_tok_bv"], a["L0_tok_Wf"],
                        a["L0_tok_bf"], a["L0_attn_b_out"])
            saved = nc.dram_tensor("saved_rows", [R, D], F32, kind="Internal").ap()
            cope_stage(nc, keep, a, saved)
            verdict_stage(nc, keep)
            general_cope_stage(nc, keep, a, saved)
        keep.place = sb("place", [P, TOPK, NT], I32)
        keep.weight = sb("weight", [P, TOPK, NT])
        xp = nc.dram_tensor("sorted_rows", [NR, D], F32, kind="Internal").ap()
        yp = nc.dram_tensor("sorted_results", [NR, D], F32, kind="Internal").ap()
        route_stage(nc, keep, a, xp)
        expert_stage(nc, keep, a, xp, yp)
        combine_stage(nc, keep, yp, out)


def constants(nc, keep):
    with nc.semaphore("zeros_set") as s_zero, nc.semaphore("const_set") as s_set, nc.Block() as block:
        @block.gpsimd
        def _(pool):
            nc.gpsimd.memset(keep.ident[:, :], 0.0).then_inc(s_zero, 1)
            nc.gpsimd.memset(keep.eps[:, :], EPS).then_inc(s_zero, 1)
            pool.wait_ge(s_zero, 2)
            nc.gpsimd.affine_select(out=keep.ident[:, :], in_=keep.ident[:, :], compare_op=ALU.not_equal, fill=1.0,
                                    base=0, pattern=[[-1, P]], channel_multiplier=1).then_inc(s_set, 1)
            pool.wait_ge(s_set, 1)


def kernel(**inputs):
    import numpy as _np
    import concourse.bacc as _bacc
    from concourse.bass_utils import run_bass_kernel_spmd as _run

    nc = _bacc.Bacc("TRN2", target_bir_lowering=False, num_devices=1)
    arrays = {k: _np.ascontiguousarray(v) for k, v in inputs.items() if k != "x"}
    x = _np.asarray(inputs["x"])
    arrays["ids"] = _np.ascontiguousarray(x.reshape(R)[::-1].reshape(NT, P).T)
    div = _np.exp(_np.arange(0, D, 2, dtype=_np.float32) * _np.float32(-_np.log(10000.0) / D))
    angle = _np.arange(S, dtype=_np.float32)[:, None] * div.astype(_np.float32)
    pos = _np.zeros((S, D), _np.float32)
    pos[:, 0::2], pos[:, 1::2] = _np.sin(angle), _np.cos(angle)
    arrays["pos"] = _np.ascontiguousarray(pos[::-1])
    arrays["tables"] = cope_tables()
    arrays["number"] = _np.arange(TMAX, dtype=_np.float32)
    arrays["minus"] = -_np.arange(32, dtype=_np.float32)
    feed, aps = {}, {}
    for name, v in arrays.items():
        feed[f"in_{name}"] = v
        aps[name] = nc.dram_tensor(f"in_{name}", v.shape, I32 if v.dtype.kind == "i" else F32, kind="ExternalInput").ap()
    out = nc.dram_tensor("out_rows", [R, D], F32, kind="ExternalOutput").ap()
    program(nc, aps, out)
    r = _run(nc, [feed], core_ids=[0])
    return _np.ascontiguousarray(r.results[0]["out_rows"][::-1].reshape(B, S, D))
```
